# Optimizing a Trainium2 kernel written in Bass

```python
import numpy as np
import jax
import jax.numpy as jnp

def _softmax(x, axis=-1):
    return jax.nn.softmax(x, axis=axis)

def _gelu(x):
    return jax.nn.gelu(x, approximate=True)

def _silu(x):
    return jax.nn.silu(x)

def _sigmoid(x):
    return jax.nn.sigmoid(x)

def _layernorm(x, axis=-1, eps=1e-05):
    m = jnp.mean(x, axis=axis, keepdims=True)
    v = jnp.var(x, axis=axis, keepdims=True)
    return (x - m) / jnp.sqrt(v + eps)

def _scatter_add(tgt, idx, src, axis=0):
    return tgt.at[idx].add(src)

def _segment_sum(src, seg, n):
    return jax.ops.segment_sum(src, seg, n)
kernel_name = 'mk_xattn_seq_d2_seqx_r8_250fe8'

def setup_inputs(seed: int=0):
    np.random.seed(seed)
    _w = jnp.asarray

    def _rec_inputs():
        import jax
        import jax.numpy as jnp
        _rk = jax.random.key(seed)
        x = -0.0005207 + 1.001 * jax.random.normal(jax.random.fold_in(_rk, 1), (4, 256, 256), jnp.float32)
        _lenS = 256 - jax.random.randint(jax.random.fold_in(_rk, 7), (4,), 0, max(1, 256 // 4) + 1, jnp.int32)
        _lenS2 = 256 - jax.random.randint(jax.random.fold_in(_rk, 8), (4,), 0, max(1, 256 // 4) + 1, jnp.int32)
        _ctx_2048P = jax.random.normal(jax.random.fold_in(_rk, 11), (4, 16, 256), jnp.float32)
        _ctx_2048c = jax.random.dirichlet(jax.random.fold_in(_rk, 511), 0.3 * jnp.ones((16,), jnp.float32), (4, 256))
        _ctx_2048t = jnp.einsum('bsk,bkd->bsd', _ctx_2048c, _ctx_2048P)
        _ctx_2048t = _ctx_2048t * jax.lax.rsqrt(jnp.mean(jnp.square(_ctx_2048t)) + 1e-12) * 0.953939
        ctx_2048 = 2.81802e-05 + 1.00001 * (_ctx_2048t + 0.3 * jax.random.normal(jax.random.fold_in(_rk, 611), (4, 256, 256), jnp.float32))
        _validS = jnp.arange(256)[None, :] < _lenS[:, None]
        _validS2 = jnp.arange(256)[None, :] < _lenS2[:, None]
        _causal = jnp.tril(jnp.ones((256, 256), dtype=bool))
        mask_Bx1xSxS2_ff0 = jnp.where(jnp.ones((4, 1, 256, 256), dtype=bool), 0.0, -1000000000.0).astype(jnp.float32)
        return (x, ctx_2048, mask_Bx1xSxS2_ff0)
    x, ctx_2048, mask_Bx1xSxS2_ff0 = _rec_inputs()

    def _L0_xattn_setup():
        import jax, jax.numpy as jnp
        import numpy as np
        B, Q, S1, S2 = (4, 32, 256, 256)
        D, H, K, F = (256, 16, 128, 1024)
        LN_EPS = 1e-05

        def _layer_norm(x, scale, offset):
            mu = jnp.mean(x, axis=-1, keepdims=True)
            var = jnp.var(x, axis=-1, keepdims=True)
            return (x - mu) * jax.lax.rsqrt(var + LN_EPS) * scale + offset

        def _cross_attention(q_in, kv_in, wq, bq, wk, bk, wv, bv, wo, bo, bias_k, bias_v):
            b, q_len, _ = q_in.shape
            t = kv_in.shape[1]
            qh = (q_in @ wq + bq).reshape(b, q_len, H, K)
            kh = (kv_in @ wk + bk).reshape(b, t, H, K)
            vh = (kv_in @ wv + bv).reshape(b, t, H, K)
            kh = jnp.concatenate([kh, jnp.broadcast_to(bias_k, (b, 1, H, K))], axis=1)
            vh = jnp.concatenate([vh, jnp.broadcast_to(bias_v, (b, 1, H, K))], axis=1)
            scale = jnp.sqrt(jnp.asarray(K, q_in.dtype))
            logits = jnp.einsum('bqhk,bthk->bhqt', qh, kh) / scale
            weights = jax.nn.softmax(logits, axis=-1)
            ctx = jnp.einsum('bhqt,bthk->bqhk', weights, vh).reshape(b, q_len, H * K)
            return ctx @ wo + bo

        def _forward(x, xf_1, xf_2, ln1_scale, ln1_offset, wq1, bq1, wk1, bk1, wv1, bv1, wo1, bo1, bias_k1, bias_v1, ln2_scale, ln2_offset, wq2, bq2, wk2, bk2, wv2, bv2, wo2, bo2, bias_k2, bias_v2, ln_mlp_scale, ln_mlp_offset, w_fc1, b_fc1, w_fc2, b_fc2):
            res = x
            h = _layer_norm(x, ln1_scale, ln1_offset)
            x = res + _cross_attention(h, xf_1, wq1, bq1, wk1, bk1, wv1, bv1, wo1, bo1, bias_k1, bias_v1)
            res = x
            h = _layer_norm(x, ln2_scale, ln2_offset)
            x = res + _cross_attention(h, xf_2, wq2, bq2, wk2, bk2, wv2, bv2, wo2, bo2, bias_k2, bias_v2)
            h = _layer_norm(x, ln_mlp_scale, ln_mlp_offset)
            h = jax.nn.gelu(h @ w_fc1 + b_fc1, approximate=False) @ w_fc2 + b_fc2
            return x + h
        key = jax.random.key(seed)
        ks = iter(jax.random.split(key, 64))

        def rn(shape, s=0.02):
            return jax.random.normal(next(ks), shape, jnp.float32) * s
        inp = {'x': rn((B, Q, D), 1.0), 'xf_1': rn((B, S1, D), 1.0), 'xf_2': rn((B, S2, D), 1.0)}
        for i in (1, 2):
            inp[f'ln{i}_scale'] = jnp.ones((D,), jnp.float32)
            inp[f'ln{i}_offset'] = jnp.zeros((D,), jnp.float32)
            inp[f'wq{i}'] = rn((D, H * K))
            inp[f'bq{i}'] = jnp.zeros((H * K,), jnp.float32)
            inp[f'wk{i}'] = rn((D, H * K))
            inp[f'bk{i}'] = jnp.zeros((H * K,), jnp.float32)
            inp[f'wv{i}'] = rn((D, H * K))
            inp[f'bv{i}'] = jnp.zeros((H * K,), jnp.float32)
            inp[f'wo{i}'] = rn((H * K, D))
            inp[f'bo{i}'] = jnp.zeros((D,), jnp.float32)
            inp[f'bias_k{i}'] = rn((1, 1, H, K))
            inp[f'bias_v{i}'] = rn((1, 1, H, K))
        inp['ln_mlp_scale'] = jnp.ones((D,), jnp.float32)
        inp['ln_mlp_offset'] = jnp.zeros((D,), jnp.float32)
        inp['w_fc1'] = rn((D, F))
        inp['b_fc1'] = jnp.zeros((F,), jnp.float32)
        inp['w_fc2'] = rn((F, D))
        inp['b_fc2'] = jnp.zeros((D,), jnp.float32)
        return inp
    _L0_xattn_all = _L0_xattn_setup()
    _L0_xattn_in = {k: v for k, v in _L0_xattn_all.items() if k in ('ln1_scale', 'ln1_offset', 'wq1', 'bq1', 'wk1', 'bk1', 'wv1', 'bv1', 'wo1', 'bo1', 'bias_k1', 'bias_v1', 'ln2_scale', 'ln2_offset', 'wq2', 'bq2', 'wk2', 'bk2', 'wv2', 'bv2', 'wo2', 'bo2', 'bias_k2', 'bias_v2', 'ln_mlp_scale', 'ln_mlp_offset', 'w_fc1', 'b_fc1', 'w_fc2', 'b_fc2')}
    del _L0_xattn_all

    def _L1_xattn_setup():
        import jax, jax.numpy as jnp
        import numpy as np
        H = 256
        NH = 32
        KVH = 8
        HD = H // NH
        GROUPS = NH // KVH
        EPS = 1e-06
        B, L, S = (4, 128, 128)

        def _gqa_forward(hidden_state, encoder_hidden_state, encoder_attention_mask, Wq, bq, Wk, bk, Wv, bv, Wo, bo, gamma, beta):
            b, l, _ = hidden_state.shape
            s = encoder_hidden_state.shape[1]
            q = hidden_state @ Wq + bq
            k = encoder_hidden_state @ Wk + bk
            v = encoder_hidden_state @ Wv + bv
            q = q.reshape(b, l, KVH, GROUPS, HD).transpose(0, 2, 3, 1, 4)
            k = k.reshape(b, s, KVH, HD).transpose(0, 2, 1, 3)
            v = v.reshape(b, s, KVH, HD).transpose(0, 2, 1, 3)
            scale = 1.0 / jnp.sqrt(jnp.asarray(HD, q.dtype))
            scores = jnp.einsum('bkgld,bksd->bkgls', q, k) * scale
            scores = scores + encoder_attention_mask[:, :, None, :, :]
            attn = jax.nn.softmax(scores, axis=-1)
            out = jnp.einsum('bkgls,bksd->bkgld', attn, v)
            out = out.transpose(0, 3, 1, 2, 4).reshape(b, l, H)
            out = out @ Wo + bo
            x = out + hidden_state
            mu = jnp.mean(x, axis=-1, keepdims=True)
            var = jnp.var(x, axis=-1, keepdims=True)
            return (x - mu) * jax.lax.rsqrt(var + EPS) * gamma + beta
        key = jax.random.key(seed)
        ks = jax.random.split(key, 12)
        sd = 0.02
        return {'hidden_state': jax.random.normal(ks[0], (B, L, H), jnp.float32), 'encoder_hidden_state': jax.random.normal(ks[1], (B, S, H), jnp.float32), 'encoder_attention_mask': jnp.zeros((B, 1, L, S), jnp.float32), 'Wq': jax.random.normal(ks[2], (H, H), jnp.float32) * sd, 'bq': jnp.zeros((H,), jnp.float32), 'Wk': jax.random.normal(ks[3], (H, KVH * HD), jnp.float32) * sd, 'bk': jnp.zeros((KVH * HD,), jnp.float32), 'Wv': jax.random.normal(ks[4], (H, KVH * HD), jnp.float32) * sd, 'bv': jnp.zeros((KVH * HD,), jnp.float32), 'Wo': jax.random.normal(ks[5], (H, H), jnp.float32) * sd, 'bo': jnp.zeros((H,), jnp.float32), 'gamma': jnp.ones((H,), jnp.float32), 'beta': jnp.zeros((H,), jnp.float32)}
    _L1_xattn_all = _L1_xattn_setup()
    _L1_xattn_in = {k: v for k, v in _L1_xattn_all.items() if k in ('Wq', 'bq', 'Wk', 'bk', 'Wv', 'bv', 'Wo', 'bo', 'gamma', 'beta')}
    del _L1_xattn_all
    return {'x': x, 'ctx_2048': ctx_2048, 'mask_Bx1xSxS2_ff0': mask_Bx1xSxS2_ff0, 'L0_xattn_ln1_scale': _L0_xattn_in['ln1_scale'], 'L0_xattn_ln1_offset': _L0_xattn_in['ln1_offset'], 'L0_xattn_wq1': _L0_xattn_in['wq1'], 'L0_xattn_bq1': _L0_xattn_in['bq1'], 'L0_xattn_wk1': _L0_xattn_in['wk1'], 'L0_xattn_bk1': _L0_xattn_in['bk1'], 'L0_xattn_wv1': _L0_xattn_in['wv1'], 'L0_xattn_bv1': _L0_xattn_in['bv1'], 'L0_xattn_wo1': _L0_xattn_in['wo1'], 'L0_xattn_bo1': _L0_xattn_in['bo1'], 'L0_xattn_bias_k1': _L0_xattn_in['bias_k1'], 'L0_xattn_bias_v1': _L0_xattn_in['bias_v1'], 'L0_xattn_ln2_scale': _L0_xattn_in['ln2_scale'], 'L0_xattn_ln2_offset': _L0_xattn_in['ln2_offset'], 'L0_xattn_wq2': _L0_xattn_in['wq2'], 'L0_xattn_bq2': _L0_xattn_in['bq2'], 'L0_xattn_wk2': _L0_xattn_in['wk2'], 'L0_xattn_bk2': _L0_xattn_in['bk2'], 'L0_xattn_wv2': _L0_xattn_in['wv2'], 'L0_xattn_bv2': _L0_xattn_in['bv2'], 'L0_xattn_wo2': _L0_xattn_in['wo2'], 'L0_xattn_bo2': _L0_xattn_in['bo2'], 'L0_xattn_bias_k2': _L0_xattn_in['bias_k2'], 'L0_xattn_bias_v2': _L0_xattn_in['bias_v2'], 'L0_xattn_ln_mlp_scale': _L0_xattn_in['ln_mlp_scale'], 'L0_xattn_ln_mlp_offset': _L0_xattn_in['ln_mlp_offset'], 'L0_xattn_w_fc1': _L0_xattn_in['w_fc1'], 'L0_xattn_b_fc1': _L0_xattn_in['b_fc1'], 'L0_xattn_w_fc2': _L0_xattn_in['w_fc2'], 'L0_xattn_b_fc2': _L0_xattn_in['b_fc2'], 'L1_xattn_Wq': _L1_xattn_in['Wq'], 'L1_xattn_bq': _L1_xattn_in['bq'], 'L1_xattn_Wk': _L1_xattn_in['Wk'], 'L1_xattn_bk': _L1_xattn_in['bk'], 'L1_xattn_Wv': _L1_xattn_in['Wv'], 'L1_xattn_bv': _L1_xattn_in['bv'], 'L1_xattn_Wo': _L1_xattn_in['Wo'], 'L1_xattn_bo': _L1_xattn_in['bo'], 'L1_xattn_gamma': _L1_xattn_in['gamma'], 'L1_xattn_beta': _L1_xattn_in['beta']}

def reference(x, ctx_2048, mask_Bx1xSxS2_ff0, L0_xattn_ln1_scale, L0_xattn_ln1_offset, L0_xattn_wq1, L0_xattn_bq1, L0_xattn_wk1, L0_xattn_bk1, L0_xattn_wv1, L0_xattn_bv1, L0_xattn_wo1, L0_xattn_bo1, L0_xattn_bias_k1, L0_xattn_bias_v1, L0_xattn_ln2_scale, L0_xattn_ln2_offset, L0_xattn_wq2, L0_xattn_bq2, L0_xattn_wk2, L0_xattn_bk2, L0_xattn_wv2, L0_xattn_bv2, L0_xattn_wo2, L0_xattn_bo2, L0_xattn_bias_k2, L0_xattn_bias_v2, L0_xattn_ln_mlp_scale, L0_xattn_ln_mlp_offset, L0_xattn_w_fc1, L0_xattn_b_fc1, L0_xattn_w_fc2, L0_xattn_b_fc2, L1_xattn_Wq, L1_xattn_bq, L1_xattn_Wk, L1_xattn_bk, L1_xattn_Wv, L1_xattn_bv, L1_xattn_Wo, L1_xattn_bo, L1_xattn_gamma, L1_xattn_beta):
    import jax
    import jax.numpy as jnp

    def _L0_xattn_ref(x, xf_1, xf_2, ln1_scale, ln1_offset, wq1, bq1, wk1, bk1, wv1, bv1, wo1, bo1, bias_k1, bias_v1, ln2_scale, ln2_offset, wq2, bq2, wk2, bk2, wv2, bv2, wo2, bo2, bias_k2, bias_v2, ln_mlp_scale, ln_mlp_offset, w_fc1, b_fc1, w_fc2, b_fc2):
        import jax, jax.numpy as jnp
        import numpy as np
        B, Q, S1, S2 = (4, 32, 256, 256)
        D, H, K, F = (256, 16, 128, 1024)
        LN_EPS = 1e-05

        def _layer_norm(x, scale, offset):
            mu = jnp.mean(x, axis=-1, keepdims=True)
            var = jnp.var(x, axis=-1, keepdims=True)
            return (x - mu) * jax.lax.rsqrt(var + LN_EPS) * scale + offset

        def _cross_attention(q_in, kv_in, wq, bq, wk, bk, wv, bv, wo, bo, bias_k, bias_v):
            b, q_len, _ = q_in.shape
            t = kv_in.shape[1]
            qh = (q_in @ wq + bq).reshape(b, q_len, H, K)
            kh = (kv_in @ wk + bk).reshape(b, t, H, K)
            vh = (kv_in @ wv + bv).reshape(b, t, H, K)
            kh = jnp.concatenate([kh, jnp.broadcast_to(bias_k, (b, 1, H, K))], axis=1)
            vh = jnp.concatenate([vh, jnp.broadcast_to(bias_v, (b, 1, H, K))], axis=1)
            scale = jnp.sqrt(jnp.asarray(K, q_in.dtype))
            logits = jnp.einsum('bqhk,bthk->bhqt', qh, kh) / scale
            weights = jax.nn.softmax(logits, axis=-1)
            ctx = jnp.einsum('bhqt,bthk->bqhk', weights, vh).reshape(b, q_len, H * K)
            return ctx @ wo + bo

        def _forward(x, xf_1, xf_2, ln1_scale, ln1_offset, wq1, bq1, wk1, bk1, wv1, bv1, wo1, bo1, bias_k1, bias_v1, ln2_scale, ln2_offset, wq2, bq2, wk2, bk2, wv2, bv2, wo2, bo2, bias_k2, bias_v2, ln_mlp_scale, ln_mlp_offset, w_fc1, b_fc1, w_fc2, b_fc2):
            res = x
            h = _layer_norm(x, ln1_scale, ln1_offset)
            x = res + _cross_attention(h, xf_1, wq1, bq1, wk1, bk1, wv1, bv1, wo1, bo1, bias_k1, bias_v1)
            res = x
            h = _layer_norm(x, ln2_scale, ln2_offset)
            x = res + _cross_attention(h, xf_2, wq2, bq2, wk2, bk2, wv2, bv2, wo2, bo2, bias_k2, bias_v2)
            h = _layer_norm(x, ln_mlp_scale, ln_mlp_offset)
            h = jax.nn.gelu(h @ w_fc1 + b_fc1, approximate=False) @ w_fc2 + b_fc2
            return x + h
        return _forward(x, xf_1, xf_2, ln1_scale, ln1_offset, wq1, bq1, wk1, bk1, wv1, bv1, wo1, bo1, bias_k1, bias_v1, ln2_scale, ln2_offset, wq2, bq2, wk2, bk2, wv2, bv2, wo2, bo2, bias_k2, bias_v2, ln_mlp_scale, ln_mlp_offset, w_fc1, b_fc1, w_fc2, b_fc2)

    def _L1_xattn_ref(hidden_state, encoder_hidden_state, encoder_attention_mask, Wq, bq, Wk, bk, Wv, bv, Wo, bo, gamma, beta):
        import jax, jax.numpy as jnp
        import numpy as np
        H = 256
        NH = 32
        KVH = 8
        HD = H // NH
        GROUPS = NH // KVH
        EPS = 1e-06
        B, L, S = (4, 128, 128)

        def _gqa_forward(hidden_state, encoder_hidden_state, encoder_attention_mask, Wq, bq, Wk, bk, Wv, bv, Wo, bo, gamma, beta):
            b, l, _ = hidden_state.shape
            s = encoder_hidden_state.shape[1]
            q = hidden_state @ Wq + bq
            k = encoder_hidden_state @ Wk + bk
            v = encoder_hidden_state @ Wv + bv
            q = q.reshape(b, l, KVH, GROUPS, HD).transpose(0, 2, 3, 1, 4)
            k = k.reshape(b, s, KVH, HD).transpose(0, 2, 1, 3)
            v = v.reshape(b, s, KVH, HD).transpose(0, 2, 1, 3)
            scale = 1.0 / jnp.sqrt(jnp.asarray(HD, q.dtype))
            scores = jnp.einsum('bkgld,bksd->bkgls', q, k) * scale
            scores = scores + encoder_attention_mask[:, :, None, :, :]
            attn = jax.nn.softmax(scores, axis=-1)
            out = jnp.einsum('bkgls,bksd->bkgld', attn, v)
            out = out.transpose(0, 3, 1, 2, 4).reshape(b, l, H)
            out = out @ Wo + bo
            x = out + hidden_state
            mu = jnp.mean(x, axis=-1, keepdims=True)
            var = jnp.var(x, axis=-1, keepdims=True)
            return (x - mu) * jax.lax.rsqrt(var + EPS) * gamma + beta
        return _gqa_forward(hidden_state, encoder_hidden_state, encoder_attention_mask, Wq, bq, Wk, bk, Wv, bv, Wo, bo, gamma, beta)
    x = _L0_xattn_ref(x, ctx_2048, ctx_2048, L0_xattn_ln1_scale, L0_xattn_ln1_offset, L0_xattn_wq1, L0_xattn_bq1, L0_xattn_wk1, L0_xattn_bk1, L0_xattn_wv1, L0_xattn_bv1, L0_xattn_wo1, L0_xattn_bo1, L0_xattn_bias_k1, L0_xattn_bias_v1, L0_xattn_ln2_scale, L0_xattn_ln2_offset, L0_xattn_wq2, L0_xattn_bq2, L0_xattn_wk2, L0_xattn_bk2, L0_xattn_wv2, L0_xattn_bv2, L0_xattn_wo2, L0_xattn_bo2, L0_xattn_bias_k2, L0_xattn_bias_v2, L0_xattn_ln_mlp_scale, L0_xattn_ln_mlp_offset, L0_xattn_w_fc1, L0_xattn_b_fc1, L0_xattn_w_fc2, L0_xattn_b_fc2)
    x = _L1_xattn_ref(x, ctx_2048, mask_Bx1xSxS2_ff0, L1_xattn_Wq, L1_xattn_bq, L1_xattn_Wk, L1_xattn_bk, L1_xattn_Wv, L1_xattn_bv, L1_xattn_Wo, L1_xattn_bo, L1_xattn_gamma, L1_xattn_beta)
    return x

_drawn_inputs = setup_inputs


def setup_inputs(seed=0):
    import zlib

    import numpy as np

    out = dict(_drawn_inputs(seed))
    spreads = {'L0_xattn_ln1_scale': (1.0, 0.6),
     'L0_xattn_ln1_offset': (0.0, 0.8),
     'L0_xattn_bq1': (0.0, 0.8),
     'L0_xattn_bk1': (0.0, 2.0),
     'L0_xattn_bv1': (0.0, 0.1),
     'L0_xattn_bo1': (0.0, 0.1),
     'L0_xattn_ln2_scale': (1.0, 0.6),
     'L0_xattn_ln2_offset': (0.0, 0.8),
     'L0_xattn_bq2': (0.0, 0.8),
     'L0_xattn_bk2': (0.0, 2.0),
     'L0_xattn_bv2': (0.0, 0.1),
     'L0_xattn_bo2': (0.0, 0.1),
     'L0_xattn_ln_mlp_scale': (1.0, 0.6),
     'L0_xattn_ln_mlp_offset': (0.0, 0.692),
     'L0_xattn_b_fc1': (0.0, 0.1),
     'L0_xattn_b_fc2': (0.0, 0.1),
     'L1_xattn_bq': (0.0, 0.8),
     'L1_xattn_bk': (0.0, 2.0),
     'L1_xattn_bv': (0.0, 0.284),
     'L1_xattn_bo': (0.0, 0.1),
     'L1_xattn_gamma': (1.0, 0.2),
     'L1_xattn_beta': (0.0, 0.1)}
    factors = {'L0_xattn_wq1': 8.0,
     'L0_xattn_wk1': 8.0,
     'L0_xattn_bias_k1': 64.0,
     'L0_xattn_bias_v1': 64.0,
     'L0_xattn_wq2': 8.0,
     'L0_xattn_wk2': 8.0,
     'L0_xattn_bias_k2': 64.0,
     'L0_xattn_bias_v2': 64.0,
     'L1_xattn_Wq': 8.0,
     'L1_xattn_Wk': 8.0}
    for name, (base, spread) in spreads.items():
        noise = np.random.default_rng([zlib.crc32(name.encode()), seed]).standard_normal(out[name].shape)
        drawn = base * np.exp(spread * noise) if base else spread * noise
        out[name] = jnp.asarray(drawn.astype(out[name].dtype))
    for name, factor in factors.items():
        out[name] = (out[name] * factor).astype(out[name].dtype)
    return out
```

```python
from contextlib import ExitStack

import concourse.bass as bass
from concourse import mybir

F32 = mybir.dt.float32
F32R = mybir.dt.float32r
ALU = mybir.AluOpType
ACT = mybir.ActivationFunctionType
AX = mybir.AxisListType

P = 128
B, S, D = 4, 256, 256
TOK = B * S
CH = TOK // P
KC = D // P
LN_EPS = 1e-5

H, K = 16, 128
ATT = 2
HG = 2
NG = H // HG
UN = HG * B
GC = HG * K
TP = S + 2
NQKV = 3 * KC * GC
NWO = HG * D
C_BQ = NQKV
C_KB = NQKV + 2 * HG
C_BV = NQKV + 3 * HG
C_VB = C_BV + GC
NPA = C_VB + GC
NPB = NWO + HG
NT = 12
NPAR = 2 * KC + D

F = 1024
FC = F // P

KVH, GR, HD = 8, 4, 8
KB = 2
GB = KVH // KB
REP = P // (GR * HD)
L1_EPS = 1e-6
BIG = 3.0e38

EXP0 = 4
TR0 = 2
DRAIN0 = 3
WO0 = 2
ADD0 = 4
VLO0 = 2
TURN0 = 2
FULL0 = 3
HLO0 = 2
SCORE0 = 1
PTLO0 = 1
OLO0 = 1


def slots(u):
    first = 3 * (u // 2)
    if u % 2 == 0:
        return ("proj", first), ("proj", first + 1)
    return ("wo", (u // 2 - 1) % B), ("proj", first + 2)


def cross_attentions(nc, x, ident, x_d, ident_d, ctx_t, packs_a, packs_b, params):
    with ExitStack() as ctx:
        def sb(name, shape, dt=F32):
            return ctx.enter_context(nc.sbuf_tensor(name, shape, dt))

        def sb2(name, shape, dt=F32):
            return [sb(f"{name}{i}", shape, dt) for i in range(2)]

        def bank(name, shape):
            return ctx.enter_context(nc.psum_tensor(name, shape, F32))

        def sem(name):
            return ctx.enter_context(nc.semaphore(name))

        cTh, cTl = sb("cTh", [P, KC, TOK], F32R), sb("cTl", [P, KC, TOK], F32R)
        hTh, hTl = sb("hTh", [P, KC, TOK], F32R), sb("hTl", [P, KC, TOK], F32R)
        pack_a, pack_b = sb("pack_a", [P, NPA]), sb("pack_b", [P, NPB])
        wh, wl = sb2("wh", [P, NQKV], F32R), sb2("wl", [P, NQKV], F32R)
        woh, wol = sb2("woh", [P, NWO], F32R), sb2("wol", [P, NWO], F32R)
        bcol, vrow, ocol = sb2("bcol", [P, 3 * HG]), sb2("vrow", [P, GC]), sb2("ocol", [P, HG])
        Qh, Ql = sb2("Qh", [P, HG, TOK], F32R), sb2("Ql", [P, HG, TOK], F32R)
        Kh, Kl = sb2("Kh", [P, HG, B, TP], F32R), sb2("Kl", [P, HG, B, TP], F32R)
        Vh, Vl = sb2("Vh", [P, CH, GC], F32R), sb2("Vl", [P, CH, GC], F32R)
        Oh, Ol = sb2("Oh", [P, HG, S], F32R), sb2("Ol", [P, HG, S], F32R)
        prob = sb2("prob", [P, 2, TP])
        PTh, PTl = sb2("PTh", [P, 2, S], F32R), sb2("PTl", [P, 2, S], F32R)
        work = sb2("work", [P, 2, D])
        attp = sb("attp", [P, NPAR])
        minus_half = sb("minus_half", [P, CH])
        nmax, sums, rsum = sb("nmax", [P, 2, 2]), sb("sums", [P, 2, 2]), sb("rsum", [P, 2, 2])
        stats, mv, rstd = sb("stats", [P, CH, 6]), sb("mv", [P, CH, 2]), sb("rstd", [P, CH])

        Sb = [bank(f"Sb{i}", [P, 2, 512]) for i in range(2)]
        PTb = bank("PTb", [P, 2, S])
        Ob = bank("Ob", [P, 512])
        slot_bank = [bank("Ab", [P, 2, D]), bank("Bb", [P, 2, D])]

        x_in, ident_in = sem("x_in"), sem("ident_in")
        ctx_in = [sem(f"ctx_in{i}") for i in range(2)]
        ctx_hi, ctx_split = sem("ctx_hi"), sem("ctx_split")
        pack_a_in, pack_b_in = sem("pack_a_in"), sem("pack_b_in")
        qkv_ready, wo_ready, pool_step = sem("qkv_ready"), sem("wo_ready"), sem("pool_step")
        stood, rstd_step, rstd_ready = sem("stood"), sem("rstd_step"), sem("rstd_ready")
        attp_in, bo_added = sem("attp_in"), sem("bo_added")
        ln_step, xn_ready, xn_turned = sem("ln_step"), sem("xn_ready"), sem("xn_turned")
        h_full, h_hi, h_lo = sem("h_full"), sem("h_hi"), sem("h_lo")
        proj_done, proj_hi, proj_drained = sem("proj_done"), sem("proj_hi"), sem("proj_drained")
        v_hi, v_lo = sem("v_hi"), sem("v_lo")
        wo_step, kb_step, kb_ready = sem("wo_step"), sem("kb_step"), sem("kb_ready")
        scored, max_done, exp_done = sem("scored"), sem("max_done"), sem("exp_done")
        rsum_done, normed, transposed = sem("rsum_done"), sem("normed"), sem("transposed")
        pt_hi, pt_lo = sem("pt_hi"), sem("pt_lo")
        pv_done, o_hi, o_lo = sem("pv_done"), sem("o_hi"), sem("o_lo")
        wo_done, wo_added = sem("wo_done"), sem("wo_added")

        def stand(eng, semaphore, value):
            eng.wait_ge(semaphore, value)
            eng.sem_inc(stood, 1)

        def wcol(w, which, kc, hh=None):
            c = (which * KC + kc) * GC
            return w[:, c:c + GC] if hh is None else w[:, c + hh * K:c + (hh + 1) * K]

        def tok(b, c=0, n=S):
            return slice(b * S + c, b * S + c + n)

        def att_loop(eng, prologue, unit, epilogue):
            with eng.Fori(0, ATT) as a:
                G0 = a * NG
                prologue(a, G0)
                for u in range(3):
                    unit(a, G0, 0, u, first=True)
                with eng.Fori(0, NG // 2 - 1) as j:
                    for p in range(2):
                        G = G0 + j * 2 + p
                        for u in range(3, UN):
                            unit(a, G, p, u)
                        for u in range(3):
                            unit(a, G + 1, 1 - p, u)
                for u in range(3, UN):
                    unit(a, G0 + NG - 2, 0, u)
                for u in range(UN):
                    unit(a, G0 + NG - 1, 1, u, last=True)
                epilogue(a)

        def drained_in(G, p, u, first, last):
            if u == 0 and first:
                return []
            v = (u - 1) % UN
            Gv, pv = (G - 1, 1 - p) if u == 0 else (G, p)
            found = []
            for where, (kind, t) in enumerate(slots(v)):
                if kind == "proj" and not (last and u > 0):
                    found.append((where, kind, t, Gv + 1, 1 - pv))
                if kind == "wo" and not (first and v == 1):
                    found.append((where, kind, t, Gv - 1 if v == 1 else Gv, None))
            return found

        block = ctx.enter_context(nc.Block())

        @block.sync
        def _(sp):
            sp.dma_start(x[:, :, :], x_d.rearrange("(c p) d -> p c d", p=P)).then_inc(x_in, 16)
            sp.dma_start(pack_a[:, :], packs_a[0]).then_inc(pack_a_in, 16)
            for b in range(B):
                if b >= 2:
                    sp.wait_ge(ctx_split, b - 1)
                sp.dma_start(work[b % 2][:, :, :],
                             ctx_t[:, tok(b)].rearrange("(k p) t -> p k t", p=P)).then_inc(ctx_in[b % 2], 16)
                if b == 0:
                    sp.dma_start(ident[:, :], ident_d).then_inc(ident_in, 16)
                    sp.dma_start(attp[:, :], params[0]).then_inc(attp_in, 16)
                    sp.dma_start(pack_b[:, :], packs_b[0]).then_inc(pack_b_in, 16)
            sp.wait_ge(qkv_ready, 1)
            sp.dma_start(pack_a[:, :], packs_a[1]).then_inc(pack_a_in, 16)
            with sp.Fori(0, ATT) as a:
                with sp.Fori(0, NG) as g:
                    sp.wait_ge(wo_ready, a * NG + g + 1)
                    sp.dma_start(pack_b[:, :], packs_b[bass.ds(a * NG + g + 1, 1), :, :]
                                 .rearrange("g p c -> (g p) c")).then_inc(pack_b_in, 16)
                    sp.wait_ge(qkv_ready, a * NG + g + 2)
                    sp.dma_start(pack_a[:, :], packs_a[bass.ds(a * NG + g + 2, 1), :, :]
                                 .rearrange("g p c -> (g p) c")).then_inc(pack_a_in, 16)
                sp.wait_ge(bo_added, a + 1)
                sp.wait_ge(h_lo, HLO0 + a * B + B)
                sp.dma_start(attp[:, :], params[bass.ds(a + 1, 1), :, :]
                             .rearrange("a p c -> (a p) c")).then_inc(attp_in, 16)
            sp.wait_ge(pack_a_in, 16 * (ATT * NG + 2))
            sp.wait_ge(pack_b_in, 16 * (ATT * NG + 1))
            sp.wait_ge(attp_in, 16 * (ATT + 1))

        @block.gpsimd
        def _(pool):
            pool.sem_inc(v_lo, VLO0)
            pool.memset(minus_half[:, :], -0.5).then_inc(rstd_step, 1)

            def split_qkv(G, i):
                done = G * 5
                stand(pool, pack_a_in, G * 16 + 16)
                q, bq = pack_a[:, 0:KC * GC], pack_a[:, C_BQ:C_BQ + HG]
                pool.tensor_scalar(q, q, K ** -0.5, None, ALU.mult).then_inc(pool_step, 1)
                pool.tensor_scalar(bq, bq, K ** -0.5, None, ALU.mult).then_inc(pool_step, 1)
                stand(pool, pool_step, done + 2)
                pool.tensor_copy(wh[i][:, :], pack_a[:, 0:NQKV]).then_inc(pool_step, 1)
                pool.tensor_copy(bcol[i][:, :], pack_a[:, C_BQ:C_BQ + 3 * HG]).then_inc(pool_step, 1)
                pool.tensor_tensor(vrow[i][:, :], pack_a[:, C_BV:C_BV + GC], pack_a[:, C_VB:C_VB + GC],
                                   ALU.subtract).then_inc(pool_step, 1)
                pool.wait_ge(pool_step, done + 5)
                pool.tensor_tensor(wl[i][:, :], pack_a[:, 0:NQKV], wh[i][:, :].bitcast(F32),
                                   ALU.subtract).then_inc(qkv_ready, 1)

            def split_wo(G, i):
                stand(pool, pack_b_in, G * 16 + 16)
                pool.tensor_copy(woh[i][:, :], pack_b[:, 0:NWO]).then_inc(wo_step, 1)
                pool.tensor_copy(ocol[i][:, :], pack_b[:, NWO:NWO + HG]).then_inc(wo_step, 1)
                pool.wait_ge(wo_step, G * 2 + 2)
                pool.tensor_tensor(wol[i][:, :], pack_b[:, 0:NWO], woh[i][:, :].bitcast(F32),
                                   ALU.subtract).then_inc(wo_ready, 1)

            def learned_key(G, i):
                col = bcol[i][:, 2 * HG:3 * HG].rearrange("p (h o t) -> p h o t", o=1, t=1)
                col = col.to_broadcast([P, HG, B, 2])
                hi, lo = Kh[i][:, :, :, S:TP], Kl[i][:, :, :, S:TP]
                pool.tensor_copy(hi, col).then_inc(kb_step, 1)
                pool.wait_ge(kb_step, G + 1)
                pool.tensor_tensor(lo, col, hi.bitcast(F32), ALU.subtract).then_inc(kb_ready, 1)

            def value_lo(G, i, b):
                pool.wait_ge(v_hi, G * B + b + 1)
                pool.tensor_tensor(Vl[i][:, 2 * b:2 * b + 2, :], work[b % 2][:, :, :],
                                   Vh[i][:, 2 * b:2 * b + 2, :].bitcast(F32),
                                   ALU.subtract).then_inc(v_lo, 1)

            split_qkv(0, 0)
            split_wo(0, 0)
            split_qkv(1, 1)

            def prologue(a, G):
                stand(pool, ln_step, a * 2 * CH + 2 * CH)
                pool.tensor_scalar(rstd[:, :], mv[:, :, 1], LN_EPS, None,
                                   ALU.add).then_inc(rstd_step, 1)
                pool.wait_ge(rstd_step, a + 2)
                pool.tensor_tensor(rstd[:, :], rstd[:, :], minus_half[:, :],
                                   ALU.pow).then_inc(rstd_ready, 1)
                pool.wait_ge(xn_ready, a * B + B)
                pool.wait_ge(attp_in, a * 16 + 16)
                bo = attp[:, 2 * KC:NPAR].rearrange("p (o d) -> p o d", o=1).to_broadcast([P, CH, D])
                pool.tensor_tensor(x[:, :, :], x[:, :, :], bo, ALU.add).then_inc(bo_added, 1)
                learned_key(G, 0)
                for b in range(B):
                    value_lo(G, 0, b)

            def unit(a, G, p, u, first=False, last=False):
                if u == 0:
                    pool.wait_ge(proj_done, G * NT + NT)
                    split_qkv(G + 2, p)
                    if not last:
                        stand(pool, scored, G * UN + SCORE0)
                        learned_key(G + 1, 1 - p)
                if u == 2:
                    pool.wait_ge(wo_done, G * B + WO0)
                    split_wo(G + 1, 1 - p)
                for kind, t in slots(u):
                    if kind == "proj" and t >= 8 and not last:
                        value_lo(G + 1, 1 - p, t - 8)

            att_loop(pool, prologue, unit, lambda a: None)

        @block.scalar
        def _(act):
            act.sem_inc(exp_done, EXP0)
            act.sem_inc(h_full, FULL0)
            for b in range(B):
                act.wait_ge(ctx_in[b % 2], 16 * (b // 2) + 16)
                act.activation(cTh[:, :, tok(b)], work[b % 2][:, :, :], ACT.Copy).then_inc(ctx_hi, 1)

            def project_hi(G, i, t, where):
                tile = slot_bank[where]
                if t < 8:
                    hh, n = t % 4 // 2, t % 2
                    act.wait_ge(proj_done, G * NT + t + 1)
                    if t < 4:
                        out = Qh[i][:, hh, n * 512:(n + 1) * 512].rearrange("p (c t) -> p c t", c=2)
                    else:
                        out = Kh[i][:, hh, 2 * n:2 * n + 2, 0:S]
                    c = hh + (t // 4) * HG
                    act.activation(out, tile[:, :, :], ACT.Identity,
                                   bias=bcol[i][:, c:c + 1]).then_inc(proj_hi, 1)
                else:
                    b = t - 8
                    act.wait_ge(proj_drained, G * NT + t + 1 + DRAIN0)
                    act.activation(Vh[i][:, 2 * b:2 * b + 2, :], work[b % 2][:, :, :],
                                   ACT.Copy).then_inc(v_hi, 1)

            def exps(U, r):
                for c in range(2):
                    act.wait_ge(max_done, U + 1)
                    act.wait_ge(transposed, U - 1 + TR0)
                    act.activation(prob[r][:, c, 0:S + 1], Sb[r][:, c, 0:S + 1], ACT.Exp,
                                   bias=nmax[:, r, c:c + 1],
                                   accum_out=sums[:, r, c:c + 1]).then_inc(exp_done, 1)

            def prologue(a, G):
                act.wait_ge(attp_in, a * 16 + 16)
                for b in range(B):
                    act.wait_ge(xn_turned, a * B + b + 1 + TURN0)
                    act.wait_ge(h_lo, a * B + b - 1 + HLO0)
                    for kc in range(KC):
                        act.activation(prob[b % 2][:, kc, 0:S], slot_bank[b % 2][:, kc, :],
                                       ACT.Identity, scale=attp[:, kc:kc + 1],
                                       bias=attp[:, KC + kc:KC + kc + 1]).then_inc(h_full, 1)
                    act.wait_ge(h_full, (a * B + b + 1) * 2 + FULL0)
                    act.activation(hTh[:, :, tok(b)], prob[b % 2][:, :, 0:S], ACT.Copy).then_inc(h_hi, 1)
                for u in range(UN):
                    for where, (kind, t) in enumerate(slots(u)):
                        if kind == "proj":
                            project_hi(G, 0, t, where)
                exps(G * UN, 0)

            def unit(a, G, p, u, first=False, last=False):
                U, b, hh = G * UN + u, u // HG, u % HG
                drains = drained_in(G, p, u, first, last)
                act.wait_ge(transposed, U + 1 + TR0)
                act.activation(PTh[u % 2][:, :, :], PTb[:, :, :], ACT.Copy).then_inc(pt_hi, 1)
                for where, kind, t, Gt, i in drains:
                    if kind == "proj" and where == 1 and t < 8 or kind == "proj" and where == 0 and t >= 8:
                        project_hi(Gt, i, t, where)
                if not (last and u == UN - 1):
                    exps(U + 1, (u + 1) % 2)
                for where, kind, t, Gt, i in drains:
                    if kind == "proj" and where == 1 and t >= 8:
                        project_hi(Gt, i, t, where)
                act.wait_ge(wo_done, G * B + b - 1 + WO0)
                act.wait_ge(pv_done, U + 1)
                act.activation(Oh[b % 2][:, hh, :], Ob[:, 0:S], ACT.Identity,
                               bias=ocol[p][:, hh:hh + 1]).then_inc(o_hi, 1)
                kind, t = slots(u)[0]
                if kind == "proj" and t < 8 and not last:
                    project_hi(G + 1, 1 - p, t, 0)

            att_loop(act, prologue, unit, lambda a: None)

        @block.vector
        def _(dve):
            dve.sem_inc(proj_drained, DRAIN0)
            dve.sem_inc(wo_added, ADD0)
            dve.sem_inc(h_lo, HLO0)
            dve.sem_inc(pt_lo, PTLO0)
            dve.sem_inc(o_lo, OLO0)
            for b in range(B):
                dve.wait_ge(ctx_hi, b + 1)
                dve.tensor_tensor(cTl[:, :, tok(b)], work[b % 2][:, :, :],
                                  cTh[:, :, tok(b)].bitcast(F32), ALU.subtract).then_inc(ctx_split, 1)
            dve.wait_ge(x_in, 16)
            dve.wait_ge(ctx_split, B)

            def project_drain(G, i, t, where):
                tile = slot_bank[where]
                if t < 8:
                    hh, n = t % 4 // 2, t % 2
                    dve.wait_ge(proj_hi, G * 8 + t + 1)
                    if t < 4:
                        hi, lo = (w[i][:, hh, n * 512:(n + 1) * 512].rearrange("p (c t) -> p c t", c=2)
                                  for w in (Qh, Ql))
                    else:
                        hi, lo = (w[i][:, hh, 2 * n:2 * n + 2, 0:S] for w in (Kh, Kl))
                    c = hh + (t // 4) * HG
                    dve.scalar_tensor_tensor(out=lo, in0=tile[:, :, :], scalar=bcol[i][:, c:c + 1],
                                             in1=hi.bitcast(F32), op0=ALU.add,
                                             op1=ALU.subtract).then_inc(proj_drained, 1)
                else:
                    b = t - 8
                    dve.wait_ge(proj_done, G * NT + t + 1)
                    dve.wait_ge(v_lo, G * B + b - 1 + VLO0)
                    row = vrow[i][:, :].rearrange("p (o d) -> p o d", o=1).to_broadcast([P, 2, D])
                    dve.tensor_tensor(work[b % 2][:, :, :], tile[:, :, :], row,
                                      ALU.add).then_inc(proj_drained, 1)

            def row_max(U, r):
                dve.wait_ge(scored, U + 1 + SCORE0)
                dve.tensor_reduce(nmax[:, r, :], Sb[r][:, :, 0:S + 1], AX.X, ALU.max,
                                  negate=True).then_inc(max_done, 1)

            def normalize(U, r):
                dve.wait_ge(exp_done, U * 2 + 2 + EXP0)
                dve.reciprocal(rsum[:, r, :], sums[:, r, :]).then_inc(rsum_done, 1)
                dve.wait_ge(rsum_done, U + 1)
                for c in range(2):
                    dve.tensor_scalar(prob[r][:, c, 0:S], prob[r][:, c, 0:S], rsum[:, r, c:c + 1],
                                      None, ALU.mult).then_inc(normed, 1)

            def add_wo(a, W, b):
                dve.wait_ge(wo_done, W + 1 + WO0)
                dve.wait_ge(bo_added, a + 1)
                dve.wait_ge(wo_added, W - B + 1 + ADD0)
                dve.tensor_tensor(x[:, 2 * b:2 * b + 2, :], slot_bank[0][:, :, :],
                                  x[:, 2 * b:2 * b + 2, :], ALU.add).then_inc(wo_added, 1)

            def prologue(a, G):
                steps = 2 * CH
                dve.wait_ge(wo_added, a * NG * B + ADD0)
                for c in range(CH):
                    dve.bn_stats(stats[:, c, :], x[:, c, :]).then_inc(ln_step, 1)
                stand(dve, ln_step, a * steps + CH)
                for c in range(CH):
                    dve.bn_aggr(mv[:, c, :], stats[:, c, :]).then_inc(ln_step, 1)
                dve.wait_ge(rstd_ready, a + 1)

                def turned_lo(b):
                    dve.wait_ge(h_hi, a * B + b + 1)
                    dve.tensor_tensor(hTl[:, :, tok(b)], prob[b % 2][:, :, 0:S],
                                      hTh[:, :, tok(b)].bitcast(F32), ALU.subtract).then_inc(h_lo, 1)
                for b in range(B):
                    dve.wait_ge(xn_turned, a * B + b - 1 + TURN0)
                    for c in range(2):
                        ins = dve.tensor_scalar(work[b % 2][:, c, :], x[:, 2 * b + c, :],
                                                mv[:, 2 * b + c, 0:1], rstd[:, 2 * b + c:2 * b + c + 1],
                                                ALU.subtract, ALU.mult)
                    ins.then_inc(xn_ready, 1)
                    if b >= 1:
                        turned_lo(b - 1)
                turned_lo(B - 1)
                for u in range(UN):
                    for where, (kind, t) in enumerate(slots(u)):
                        if kind == "proj":
                            project_drain(G, 0, t, where)
                row_max(G * UN, 0)
                normalize(G * UN, 0)

            def unit(a, G, p, u, first=False, last=False):
                U, b, hh = G * UN + u, u // HG, u % HG
                drains = drained_in(G, p, u, first, last)

                def drain(bank_no):
                    for where, kind, t, Gt, i in drains:
                        if where == bank_no:
                            if kind == "proj":
                                project_drain(Gt, i, t, where)
                            else:
                                add_wo(a, Gt * B + t, t)
                drain(0)
                dve.wait_ge(pt_hi, U + 1)
                dve.tensor_tensor(PTl[u % 2][:, :, :], PTb[:, :, :],
                                  PTh[u % 2][:, :, :].bitcast(F32), ALU.subtract).then_inc(pt_lo, 1)
                if not (last and u == UN - 1):
                    row_max(U + 1, (u + 1) % 2)
                drain(1)
                if not (last and u == UN - 1):
                    normalize(U + 1, (u + 1) % 2)
                dve.wait_ge(o_hi, U + 1)
                dve.scalar_tensor_tensor(out=Ol[b % 2][:, hh, :], in0=Ob[:, 0:S],
                                         scalar=ocol[p][:, hh:hh + 1],
                                         in1=Oh[b % 2][:, hh, :].bitcast(F32), op0=ALU.add,
                                         op1=ALU.subtract).then_inc(o_lo, 1)

            def epilogue(a):
                W = a * NG * B + NG * B - 2
                add_wo(a, W, B - 2)
                add_wo(a, W + 1, B - 1)

            att_loop(dve, prologue, unit, epilogue)

        @block.tensor
        def _(pe):
            pe.sem_inc(scored, SCORE0)
            pe.sem_inc(transposed, TR0)
            pe.sem_inc(wo_done, WO0)
            pe.sem_inc(xn_turned, TURN0)
            pe.wait_ge(ident_in, 16)
            pe.wait_ge(ctx_split, B)

            def three(out, w, m, first, final):
                (w_hi, w_lo), (m_hi, m_lo) = w, m
                pe.matmul(out, w_lo, m_hi, start=first, stop=False)
                pe.matmul(out, w_hi, m_lo, start=False, stop=False)
                return pe.matmul(out, w_hi, m_hi, start=False, stop=final)

            def project(G, i, t, where):
                tile = slot_bank[where]
                if t == 0:
                    pe.wait_ge(qkv_ready, G + 1)
                back = 3 if where == 0 else (2 if t % 3 == 1 else 1)
                pe.wait_ge(proj_drained, G * NT + t - back + 1 + DRAIN0)
                if t < 8:
                    which, hh, n = t // 4, t % 4 // 2, t % 2
                    src = (hTh, hTl) if which == 0 else (cTh, cTl)
                    for kc in range(KC):
                        ins = three(tile[:, :, :].rearrange("p a b -> p (a b)"),
                                    [wcol(w[i], which, kc, hh) for w in (wh, wl)],
                                    [s[:, kc, n * 512:(n + 1) * 512] for s in src],
                                    kc == 0, kc == KC - 1)
                else:
                    for c in range(2):
                        for kc in range(KC):
                            ins = three(tile[:, c, :],
                                        [s[:, kc, tok(t - 8, c * P, P)] for s in (cTh, cTl)],
                                        [wcol(w[i], 2, kc) for w in (wh, wl)],
                                        kc == 0, kc == KC - 1)
                ins.then_inc(proj_done, 1)

            def scores(U, G, i, u, r):
                b, hh = u // HG, u % HG
                if u == 0:
                    pe.wait_ge(proj_drained, G * NT + 8 + DRAIN0)
                    pe.wait_ge(kb_ready, G + 1)
                pe.wait_ge(exp_done, U * 2 - 2 + EXP0)
                for c in range(2):
                    ins = three(Sb[r][:, c, 0:TP],
                                [w[i][:, hh, tok(b, c * P, P)] for w in (Qh, Ql)],
                                [m[i][:, hh, b, :] for m in (Kh, Kl)], True, True)
                ins.then_inc(scored, 1)

            def wo_tile(W, Gw, i, b):
                pe.wait_ge(wo_ready, Gw + 1)
                pe.wait_ge(o_lo, Gw * UN + HG * b + HG + OLO0)
                for c in range(2):
                    for hh in range(HG):
                        ins = three(slot_bank[0][:, c, :],
                                    [o[b % 2][:, hh, c * P:(c + 1) * P] for o in (Oh, Ol)],
                                    [w[i][:, hh * D:(hh + 1) * D] for w in (woh, wol)],
                                    hh == 0, hh == HG - 1)
                ins.then_inc(wo_done, 1)

            def prologue(a, G):
                for b in range(B):
                    pe.wait_ge(xn_ready, a * B + b + 1)
                    pe.wait_ge(h_full, (a * B + b - 1) * 2 + FULL0)
                    for c in range(2):
                        for kc in range(KC):
                            ins = pe.transpose(slot_bank[b % 2][:, kc, c * P:(c + 1) * P],
                                               work[b % 2][:, c, kc * P:(kc + 1) * P], ident[:, :])
                    ins.then_inc(xn_turned, 1)
                pe.wait_ge(h_lo, a * B + B + HLO0)
                for u in range(UN):
                    for where, (kind, t) in enumerate(slots(u)):
                        if kind == "proj":
                            project(G, 0, t, where)
                scores(G * UN, G, 0, 0, 0)

            def unit(a, G, p, u, first=False, last=False):
                U, b, hh = G * UN + u, u // HG, u % HG
                pe.wait_ge(normed, U * 2 + 2)
                pe.wait_ge(pt_lo, U + PTLO0)
                for c in range(2):
                    for tc in range(2):
                        ins = pe.transpose(PTb[:, tc, c * P:(c + 1) * P],
                                           prob[u % 2][:, c, tc * P:(tc + 1) * P], ident[:, :])
                ins.then_inc(transposed, 1)
                if u < UN - 1:
                    scores(U + 1, G, p, u + 1, (u + 1) % 2)
                elif not last:
                    scores(U + 1, G + 1, 1 - p, 0, 0)
                A, Bt = slots(u)
                if A[0] == "wo":
                    if not (first and u == 1):
                        W = G * B + A[1] - (B if u == 1 else 0)
                        if last:
                            pe.wait_ge(wo_added, W + ADD0)
                        else:
                            pe.wait_ge(proj_drained, G * NT + NT + 3 * (u // 2) + 1 + DRAIN0)
                        if u == 1:
                            wo_tile(W, G - 1, 1 - p, A[1])
                        else:
                            wo_tile(W, G, p, A[1])
                elif not last:
                    pe.wait_ge(wo_added, G * B + u // 2 - 1 + ADD0)
                    project(G + 1, 1 - p, A[1], 0)
                if hh == 0:
                    pe.wait_ge(v_lo, G * B + b + 1 + VLO0)
                pe.wait_ge(pt_lo, U + 1 + PTLO0)
                pe.wait_ge(o_lo, U + OLO0)
                for tc in range(2):
                    ins = three(Ob[:, 0:S],
                                [v[p][:, 2 * b + tc, hh * K:(hh + 1) * K] for v in (Vh, Vl)],
                                [m[u % 2][:, tc, :] for m in (PTh, PTl)], tc == 0, tc == 1)
                ins.then_inc(pv_done, 1)
                if not last:
                    project(G + 1, 1 - p, Bt[1], 1)

            def epilogue(a):
                W = a * NG * B + NG * B - 1
                pe.wait_ge(wo_added, W + ADD0)
                wo_tile(W, a * NG + NG - 1, 1, B - 1)

            att_loop(pe, prologue, unit, epilogue)


def feed_forward(nc, x, ident, w1_d, w2_d, mlpp_d):
    with ExitStack() as ctx:
        def sb(name, shape, dt=F32):
            return ctx.enter_context(nc.sbuf_tensor("m_" + name, shape, dt))

        def bank(name, shape):
            return ctx.enter_context(nc.psum_tensor("m_" + name, shape, F32))

        def sem(name):
            return ctx.enter_context(nc.semaphore("m_" + name))

        w1, w2 = sb("w1", [P, KC, F]), sb("w2", [P, FC, D])
        w1h, w1l = sb("w1h", [P, KC, F], F32R), sb("w1l", [P, KC, F], F32R)
        w2h, w2l = sb("w2h", [P, FC, D], F32R), sb("w2l", [P, FC, D], F32R)
        mlpp = sb("mlpp", [P, 2 * KC + FC + D])
        hTh, hTl = sb("hTh", [P, KC, TOK], F32R), sb("hTl", [P, KC, TOK], F32R)
        Gh, Gl = sb("Gh", [P, FC, TOK], F32R), sb("Gl", [P, FC, TOK], F32R)
        xn = [sb(f"xn{i}", [P, 2, D]) for i in range(2)]
        full = [sb(f"full{i}", [P, KC, S]) for i in range(2)]
        act_out = [sb(f"act_out{i}", [P, 512]) for i in range(2)]
        stats, mv, rstd = sb("stats", [P, CH, 6]), sb("mv", [P, CH, 2]), sb("rstd", [P, CH])
        minus_half = sb("minus_half", [P, CH])
        turn = [bank(f"turn{i}", [P, KC, S]) for i in range(2)]
        hid = [bank(f"hid{i}", [P, 512]) for i in range(2)]
        res = [bank(f"res{i}", [P, 512]) for i in range(2)]

        w1_in, w2_in, mlpp_in = sem("w1_in"), sem("w2_in"), sem("mlpp_in")
        w1_hi, w1_lo, w2_hi, w2_lo = sem("w1_hi"), sem("w1_lo"), sem("w2_hi"), sem("w2_lo")
        ln_step, rstd_step, rstd_ready = sem("ln_step"), sem("rstd_step"), sem("rstd_ready")
        xn_ready, xn_turned, h_full = sem("xn_ready"), sem("xn_turned"), sem("h_full")
        h_hi, h_lo, b2_added = sem("h_hi"), sem("h_lo"), sem("b2_added")
        hid_done, gelu_done, g_hi, g_lo = sem("hid_done"), sem("gelu_done"), sem("g_hi"), sem("g_lo")
        res_done, res_added = sem("res_done"), sem("res_added")
        block = ctx.enter_context(nc.Block())
        NTILE = FC * 2

        @block.sync
        def _(sp):
            sp.dma_start(w1[:, :, :], w1_d).then_inc(w1_in, 16)
            sp.dma_start(mlpp[:, :], mlpp_d).then_inc(mlpp_in, 16)
            sp.dma_start(w2[:, :, :], w2_d).then_inc(w2_in, 16)

        @block.gpsimd
        def _(pool):
            pool.memset(minus_half[:, :], -0.5).then_inc(rstd_step, 1)
            pool.wait_ge(ln_step, 2 * CH)
            pool.tensor_scalar(rstd[:, :], mv[:, :, 1], LN_EPS, None, ALU.add).then_inc(rstd_step, 1)
            pool.wait_ge(rstd_step, 2)
            pool.tensor_tensor(rstd[:, :], rstd[:, :], minus_half[:, :], ALU.pow).then_inc(rstd_ready, 1)
            pool.wait_ge(w2_in, 16)
            pool.tensor_copy(w2h[:, :, :], w2[:, :, :]).then_inc(w2_hi, 1)
            pool.wait_ge(w2_hi, 1)
            pool.tensor_tensor(w2l[:, :, :], w2[:, :, :], w2h[:, :, :].bitcast(F32),
                               ALU.subtract).then_inc(w2_lo, 1)
            pool.wait_ge(xn_ready, B)
            pool.wait_ge(mlpp_in, 16)
            b2 = mlpp[:, 2 * KC + FC:].rearrange("p (o d) -> p o d", o=1).to_broadcast([P, CH, D])
            pool.tensor_tensor(x[:, :, :], x[:, :, :], b2, ALU.add).then_inc(b2_added, 1)

        @block.scalar
        def _(act):
            act.wait_ge(w1_in, 16)
            act.activation(w1h[:, :, :], w1[:, :, :], ACT.Copy).then_inc(w1_hi, 1)
            act.wait_ge(mlpp_in, 16)
            for b in range(B):
                act.wait_ge(xn_turned, b + 1)
                if b >= 2:
                    act.wait_ge(h_lo, b - 1)
                for kc in range(KC):
                    act.activation(full[b % 2][:, kc, :], turn[b % 2][:, kc, :], ACT.Identity,
                                   scale=mlpp[:, kc:kc + 1],
                                   bias=mlpp[:, KC + kc:KC + kc + 1]).then_inc(h_full, 1)
                act.wait_ge(h_full, 2 * b + 2)
                act.activation(hTh[:, :, b * S:(b + 1) * S], full[b % 2][:, :, :],
                               ACT.Copy).then_inc(h_hi, 1)
            for n in range(2):
                for f in range(FC):
                    t = n * FC + f
                    act.wait_ge(hid_done, t + 1)
                    if t >= 2:
                        act.wait_ge(g_lo, t - 1)
                    act.activation(act_out[t % 2][:, :], hid[t % 2][:, :], ACT.Gelu,
                                   bias=mlpp[:, 2 * KC + f:2 * KC + f + 1]).then_inc(gelu_done, 1)
                    act.wait_ge(gelu_done, t + 1)
                    act.activation(Gh[:, f, n * 512:(n + 1) * 512], act_out[t % 2][:, :],
                                   ACT.Copy).then_inc(g_hi, 1)

        @block.vector
        def _(dve):
            for c in range(CH):
                dve.bn_stats(stats[:, c, :], x[:, c, :]).then_inc(ln_step, 1)
            dve.wait_ge(ln_step, CH)
            for c in range(CH):
                dve.bn_aggr(mv[:, c, :], stats[:, c, :]).then_inc(ln_step, 1)
            dve.wait_ge(w1_hi, 1)
            dve.tensor_tensor(w1l[:, :, :], w1[:, :, :], w1h[:, :, :].bitcast(F32),
                              ALU.subtract).then_inc(w1_lo, 1)
            dve.wait_ge(rstd_ready, 1)

            def turned_lo(b):
                dve.wait_ge(h_hi, b + 1)
                dve.tensor_tensor(hTl[:, :, b * S:(b + 1) * S], full[b % 2][:, :, :],
                                  hTh[:, :, b * S:(b + 1) * S].bitcast(F32),
                                  ALU.subtract).then_inc(h_lo, 1)
            for b in range(B):
                if b >= 2:
                    dve.wait_ge(xn_turned, b - 1)
                for c in range(2 * b, 2 * b + 2):
                    ins = dve.tensor_scalar(xn[b % 2][:, c % 2, :], x[:, c, :], mv[:, c, 0:1],
                                            rstd[:, c:c + 1], ALU.subtract, ALU.mult)
                ins.then_inc(xn_ready, 1)
                if b >= 1:
                    turned_lo(b - 1)
            turned_lo(B - 1)
            for n in range(2):
                for f in range(FC):
                    t = n * FC + f
                    dve.wait_ge(g_hi, t + 1)
                    dve.tensor_tensor(Gl[:, f, n * 512:(n + 1) * 512], act_out[t % 2][:, :],
                                      Gh[:, f, n * 512:(n + 1) * 512].bitcast(F32),
                                      ALU.subtract).then_inc(g_lo, 1)
                if n == 1:
                    dve.wait_ge(b2_added, 1)
            for c in range(CH):
                dve.wait_ge(res_done, c + 1)
                dve.tensor_tensor(x[:, c, :], res[c % 2][:, 0:D], x[:, c, :], ALU.add).then_inc(res_added, 1)

        @block.tensor
        def _(pe):
            def three(out, w, m, first, final):
                (w_hi, w_lo), (m_hi, m_lo) = w, m
                pe.matmul(out, w_lo, m_hi, start=first, stop=False)
                pe.matmul(out, w_hi, m_lo, start=False, stop=False)
                return pe.matmul(out, w_hi, m_hi, start=False, stop=final)

            for b in range(B):
                pe.wait_ge(xn_ready, b + 1)
                if b >= 2:
                    pe.wait_ge(h_full, 2 * (b - 1))
                for c in range(2):
                    for kc in range(KC):
                        ins = pe.transpose(turn[b % 2][:, kc, c * P:(c + 1) * P],
                                           xn[b % 2][:, c, kc * P:(kc + 1) * P], ident[:, :])
                ins.then_inc(xn_turned, 1)
            pe.wait_ge(w1_lo, 1)
            for n in range(2):
                pe.wait_ge(h_lo, 2 * n + 2)
                for f in range(FC):
                    t = n * FC + f
                    if t >= 2:
                        pe.wait_ge(gelu_done, t - 1)
                    for kc in range(KC):
                        ins = three(hid[t % 2][:, :], [w[:, kc, f * P:(f + 1) * P] for w in (w1h, w1l)],
                                    [m[:, kc, n * 512:(n + 1) * 512] for m in (hTh, hTl)],
                                    kc == 0, kc == KC - 1)
                    ins.then_inc(hid_done, 1)
            pe.wait_ge(w2_lo, 1)
            for c in range(CH):
                pe.wait_ge(g_lo, FC if c < CH // 2 else NTILE)
                if c >= 2:
                    pe.wait_ge(res_added, c - 1)
                for f in range(FC):
                    ins = three(res[c % 2][:, 0:D], [g[:, f, c * P:(c + 1) * P] for g in (Gh, Gl)],
                                [w[:, f, :] for w in (w2h, w2l)], f == 0, f == FC - 1)
                ins.then_inc(res_done, 1)


def grouped_projections(nc, x, ident, Qr, Kr, V, ctx_t, wq_d, wk_d, wv_d, l1p_d):
    with ExitStack() as ctx:
        def sb(name, shape, dt=F32):
            return ctx.enter_context(nc.sbuf_tensor("p_" + name, shape, dt))

        def bank(name, shape):
            return ctx.enter_context(nc.psum_tensor("p_" + name, shape, F32))

        def sem(name):
            return ctx.enter_context(nc.semaphore("p_" + name))

        VW = KVH * HD
        wq, wk, wv = sb("wq", [P, KC, F]), sb("wk", [P, KC, F]), sb("wv", [P, KC, VW])
        wqh, wql = sb("wqh", [P, KC, F], F32R), sb("wql", [P, KC, F], F32R)
        wkh, wkl = sb("wkh", [P, KC, F], F32R), sb("wkl", [P, KC, F], F32R)
        wvh, wvl = sb("wvh", [P, KC, VW], F32R), sb("wvl", [P, KC, VW], F32R)
        l1p = sb("l1p", [P, 2 * KVH + VW])
        xTh, xTl = sb("xTh", [P, KC, TOK], F32R), sb("xTl", [P, KC, TOK], F32R)
        cTh, cTl = sb("cTh", [P, KC, TOK], F32R), sb("cTl", [P, KC, TOK], F32R)
        c_in = sb("c_in", [P, KC, TOK])
        turn = [bank(f"turn{i}", [P, KC, S]) for i in range(2)]
        tile = [bank(f"tile{i}", [P, 512]) for i in range(2)]
        vbank = bank("vbank", [P, CH, VW])

        wq_in, wk_in, wv_in, l1p_in, ctx_in = (sem(n) for n in ("wq_in", "wk_in", "wv_in", "l1p_in", "ctx_in"))
        wq_scaled, bq_scaled, wq_hi, wq_lo = (sem(n) for n in ("wq_scaled", "bq_scaled", "wq_hi", "wq_lo"))
        wk_hi, wk_lo, wv_hi, wv_lo = (sem(n) for n in ("wk_hi", "wk_lo", "wv_hi", "wv_lo"))
        ctx_hi, ctx_lo = sem("ctx_hi"), sem("ctx_lo")
        turned, x_hi, x_lo = sem("turned"), sem("x_hi"), sem("x_lo")
        tile_done, tile_hi, tile_lo = sem("tile_done"), sem("tile_hi"), sem("tile_lo")
        v_done, v_out = sem("v_done"), sem("v_out")
        block = ctx.enter_context(nc.Block())
        TILES = [("k", g, n) for g in range(KVH) for n in range(2)]
        TILES += [("q", g, n) for g in range(KVH) for n in range(2)]

        @block.sync
        def _(sp):
            sp.dma_start(c_in[:, :, :], ctx_t.rearrange("(k p) t -> p k t", p=P)).then_inc(ctx_in, 16)
            sp.dma_start(wk[:, :, :], wk_d).then_inc(wk_in, 16)
            sp.dma_start(l1p[:, :], l1p_d).then_inc(l1p_in, 16)
            sp.dma_start(wv[:, :, :], wv_d).then_inc(wv_in, 16)
            sp.dma_start(wq[:, :, :], wq_d).then_inc(wq_in, 16)

        @block.gpsimd
        def _(pool):
            pool.wait_ge(l1p_in, 16)
            pool.tensor_scalar(l1p[:, 0:KVH], l1p[:, 0:KVH], HD ** -0.5, None, ALU.mult).then_inc(bq_scaled, 1)
            pool.wait_ge(wv_in, 16)
            pool.tensor_copy(wvh[:, :, :], wv[:, :, :]).then_inc(wv_hi, 1)
            pool.wait_ge(wv_hi, 1)
            pool.tensor_tensor(wvl[:, :, :], wv[:, :, :], wvh[:, :, :].bitcast(F32),
                               ALU.subtract).then_inc(wv_lo, 1)
            pool.wait_ge(wq_in, 16)
            pool.tensor_scalar(wq[:, :, :], wq[:, :, :], HD ** -0.5, None, ALU.mult).then_inc(wq_scaled, 1)
            pool.wait_ge(wq_scaled, 1)
            pool.tensor_copy(wqh[:, :, :], wq[:, :, :]).then_inc(wq_hi, 1)
            pool.wait_ge(wq_hi, 1)
            pool.tensor_tensor(wql[:, :, :], wq[:, :, :], wqh[:, :, :].bitcast(F32),
                               ALU.subtract).then_inc(wq_lo, 1)

        @block.scalar
        def _(act):
            act.wait_ge(ctx_in, 16)
            act.activation(cTh[:, :, :], c_in[:, :, :], ACT.Copy).then_inc(ctx_hi, 1)
            act.wait_ge(wk_in, 16)
            act.activation(wkh[:, :, :], wk[:, :, :], ACT.Copy).then_inc(wk_hi, 1)
            for b in range(B):
                act.wait_ge(turned, b + 1)
                act.activation(xTh[:, :, b * S:(b + 1) * S], turn[b % 2][:, :, :],
                               ACT.Copy).then_inc(x_hi, 1)
            act.wait_ge(bq_scaled, 1)
            for t, (kind, g, n) in enumerate(TILES):
                out, c = (Qr, g) if kind == "q" else (Kr, KVH + g)
                act.wait_ge(tile_done, t + 1)
                act.activation(out[:, g, n * 512:(n + 1) * 512], tile[t % 2][:, :], ACT.Identity,
                               bias=l1p[:, c:c + 1]).then_inc(tile_hi, 1)

        @block.vector
        def _(dve):
            dve.wait_ge(ctx_hi, 1)
            dve.tensor_tensor(cTl[:, :, :], c_in[:, :, :], cTh[:, :, :].bitcast(F32),
                              ALU.subtract).then_inc(ctx_lo, 1)
            dve.wait_ge(wk_hi, 1)
            dve.tensor_tensor(wkl[:, :, :], wk[:, :, :], wkh[:, :, :].bitcast(F32),
                              ALU.subtract).then_inc(wk_lo, 1)
            for b in range(B):
                dve.wait_ge(x_hi, b + 1)
                dve.tensor_tensor(xTl[:, :, b * S:(b + 1) * S], turn[b % 2][:, :, :],
                                  xTh[:, :, b * S:(b + 1) * S].bitcast(F32),
                                  ALU.subtract).then_inc(x_lo, 1)
            for t, (kind, g, n) in enumerate(TILES):
                out, c = (Qr, g) if kind == "q" else (Kr, KVH + g)
                dve.wait_ge(tile_hi, t + 1)
                for p0, p1 in ([(64, 128)] if kind == "q" else [(32, 64), (96, 128)]):
                    part = out[p0:p1, g, n * 512:(n + 1) * 512]
                    ins = dve.scalar_tensor_tensor(out=part, in0=tile[t % 2][p0:p1, :],
                                                   scalar=l1p[p0:p1, c:c + 1], in1=part.bitcast(F32),
                                                   op0=ALU.add, op1=ALU.subtract)
                ins.then_inc(tile_lo, 1)
            dve.wait_ge(v_done, 1)
            bv = l1p[:, 2 * KVH:].rearrange("p (o d) -> p o d", o=1).to_broadcast([P, CH, VW])
            dve.tensor_tensor(V[:, :, :], vbank[:, :, :], bv, ALU.add).then_inc(v_out, 1)

        @block.tensor
        def _(pe):
            def three(out, w, m, first, final):
                (w_hi, w_lo), (m_hi, m_lo) = w, m
                pe.matmul(out, w_lo, m_hi, start=first, stop=False)
                pe.matmul(out, w_hi, m_lo, start=False, stop=False)
                return pe.matmul(out, w_hi, m_hi, start=False, stop=final)

            for b in range(B):
                if b >= 2:
                    pe.wait_ge(x_lo, b - 1)
                for c in range(2):
                    for kc in range(KC):
                        ins = pe.transpose(turn[b % 2][:, kc, c * P:(c + 1) * P],
                                           x[:, 2 * b + c, kc * P:(kc + 1) * P], ident[:, :])
                ins.then_inc(turned, 1)
            pe.wait_ge(ctx_lo, 1)
            pe.wait_ge(wk_lo, 1)
            for t, (kind, g, n) in enumerate(TILES):
                if t == 2 * KVH:
                    pe.wait_ge(wq_lo, 1)
                    pe.wait_ge(x_lo, B)
                if t >= 2:
                    pe.wait_ge(tile_lo, t - 1)
                w, m = ((wqh, wql), (xTh, xTl)) if kind == "q" else ((wkh, wkl), (cTh, cTl))
                for kc in range(KC):
                    ins = three(tile[t % 2][:, :], [a[:, kc, g * P:(g + 1) * P] for a in w],
                                [a[:, kc, n * 512:(n + 1) * 512] for a in m], kc == 0, kc == KC - 1)
                ins.then_inc(tile_done, 1)
            pe.wait_ge(wv_lo, 1)
            for c in range(CH):
                for kc in range(KC):
                    ins = three(vbank[:, c, :], [a[:, kc, c * P:(c + 1) * P] for a in (cTh, cTl)],
                                [a[:, kc, :] for a in (wvh, wvl)], kc == 0, kc == KC - 1)
            ins.then_inc(v_done, 1)


SC0, MK0, PV0, PT0, OT0 = 3, 2, 2, 1, 1
NPR = 4
NV = KB * GB * 2


def grouped_attention(nc, ident, Qr, Kr, V, OT, sums, mask_d, gmask_d):
    with ExitStack() as ctx:
        def sb(name, shape, dt=F32):
            return ctx.enter_context(nc.sbuf_tensor("g_" + name, shape, dt))

        def bank(name, shape):
            return ctx.enter_context(nc.psum_tensor("g_" + name, shape, F32))

        def sem(name):
            return ctx.enter_context(nc.semaphore("g_" + name))

        Qb = [sb(f"Qb{i}", [P, GB, S], F32R) for i in range(KB)]
        KP = [sb(f"KP{i}", [P, GR, S], F32R) for i in range(2)]
        VP = [sb(f"VP{i}", [P, 2, GB, GR, GR * HD]) for i in range(KB)]
        PT = [sb(f"PT{i}", [P, GB, 2, GR, S]) for i in range(KB)]
        maskb = [sb(f"maskb{i}", [P, 2, S]) for i in range(KB)]
        prob = [sb(f"prob{i}", [P, GR, S]) for i in range(NPR)]
        nmax = sb("nmax", [P, NPR, GR])
        gmask = sb("gmask", [P, GR])
        Sb = [bank(f"Sb{i}", [P, 2, 512]) for i in range(2)]
        PTb = [bank(f"PTb{i}", [P, GR, P]) for i in range(2)]
        Ob = bank("Ob", [P, 512])

        q_in = [sem(f"q_in{i}") for i in range(KB)]
        mask_in = [sem(f"mask_in{i}") for i in range(KB)]
        gmask_in, kp_ready, vp_zero, vp_ready = sem("gmask_in"), sem("kp_ready"), sem("vp_zero"), sem("vp_ready")
        scored, masked, exp_done = sem("scored"), sem("masked"), sem("exp_done")
        turned = [sem(f"turned{i}") for i in range(2)]
        pt0_out, pt1_out, pv_done, ot_out = sem("pt0_out"), sem("pt1_out"), sem("pv_done"), sem("ot_out")
        stood = sem("stood")

        def stand(eng, semaphore, value):
            eng.wait_ge(semaphore, value)
            eng.sem_inc(stood, 1)

        def batches(eng, unit, last):
            for v in range(NV // 2):
                unit(0, v, first=True)
            with eng.Fori(0, B - 1) as b:
                for v in range(NV // 2, NV):
                    unit(b, v)
                for v in range(NV // 2):
                    unit(b + 1, v)
            for v in range(NV // 2, NV):
                unit(B - 1, v)
            last()

        def ahead(part, b, v, by):
            if v + by < NV:
                part(b, v + by, b * NV + v + by)
            elif not (isinstance(b, int) and b == B - 1):
                part(b + 1, v + by - NV, b * NV + v + by)

        block = ctx.enter_context(nc.Block())

        @block.sync
        def _(sp):
            sp.dma_start(gmask[:, :], gmask_d).then_inc(gmask_in, 16)

            def load(b, kb):
                sp.dma_start(Qb[kb][:, :, :].bitcast(F32),
                             Qr[:, kb * GB:(kb + 1) * GB, bass.ds(b * S, S)].bitcast(F32)
                             ).then_inc(q_in[kb], 16)
                sp.dma_start(maskb[kb][:, :, :], mask_d[bass.ds(b * S, S), :]
                             .rearrange("(c p) t -> p c t", p=P)).then_inc(mask_in[kb], 16)
            for kb in range(KB):
                load(0, kb)
            with sp.Fori(0, B - 1) as b:
                for kb in range(KB):
                    stand(sp, masked, b * NV + (kb + 1) * 8 + MK0)
                    load(b + 1, kb)

        @block.gpsimd
        def _(pool):
            for kb in range(KB):
                pool.memset(VP[kb][:, :, :, :, :], 0.0).then_inc(vp_zero, 1)
            pool.wait_ge(vp_zero, KB)
            pool.wait_ge(gmask_in, 16)

            def keys(b, kb, k):
                J = b * KVH + kb * GB + k
                pool.wait_ge(scored, J * 2 - 2 + SC0)
                out = KP[k % 2][:, :, :]
                rows = Kr[:, kb * GB + k, bass.ds(b * S, S)].bitcast(F32)
                rows = rows.rearrange("p (o t) -> p o t", o=1).to_broadcast([P, GR, S])
                head = gmask[:, :].rearrange("p (g o) -> p g o", o=1).to_broadcast([P, GR, S])
                pool.tensor_tensor(out, rows, head, ALU.mult).then_inc(kp_ready, 1)

            def values(b, kb):
                su = b * KB + kb
                stand(pool, pv_done, su - 1 + PV0)
                for g in range(GR):
                    src = V[:, bass.ds(b * 2, 2), kb * GB * HD:(kb + 1) * GB * HD]
                    pool.tensor_copy(VP[kb][:, :, :, g, g * HD:(g + 1) * HD],
                                     src.rearrange("p c (k d) -> p c k d", d=HD)).then_inc(vp_ready, 1)

            def batch(b):
                for kb in range(KB):
                    for k in range(GB):
                        keys(b, kb, k)
                    values(b, kb)
            with pool.Fori(0, B) as b:
                batch(b)

        @block.scalar
        def _(act):
            act.sem_inc(pt0_out, PT0)

            def exps(b, v, N):
                kb, k, c = v // 8, v % 8 // 2, v % 2
                act.wait_ge(masked, N + 1 + MK0)
                for g in range(GR):
                    h = (kb * GB + k) * GR + g
                    ins = act.activation(prob[v % NPR][:, g, :], prob[v % NPR][:, g, :], ACT.Exp,
                                         scale=-1.0, bias=nmax[:, v % NPR, g:g + 1],
                                         accum_out=sums[:, bass.ds(b * 2 + c, 1), h])
                ins.then_inc(exp_done, 1)

            def unit(b, v, first=False):
                N, kb, k, c = b * NV + v, v // 8, v % 8 // 2, v % 2
                if first and v == 0:
                    exps(b, v, N)
                ahead(exps, b, v, 1)
                act.wait_ge(turned[0], N + 1)
                act.wait_ge(pv_done, b * KB + kb - 1 + PV0)
                act.activation(PT[kb][:, k, 0, :, c * P:(c + 1) * P], PTb[0][:, :, :],
                               ACT.Copy).then_inc(pt0_out, 1)
            batches(act, unit, lambda: None)

        @block.vector
        def _(dve):
            dve.sem_inc(masked, MK0)
            dve.sem_inc(pt1_out, PT0)
            dve.sem_inc(ot_out, OT0)

            def mask_and_max(b, v, N):
                kb, c = v // 8, v % 2
                if v % 8 == 0:
                    dve.wait_ge(mask_in[kb], b * 16 + 16)
                stand(dve, scored, N + 1 + SC0)
                for g in range(GR):
                    ins = dve.tensor_tensor_reduce(
                        out=prob[v % NPR][:, g, :], in0=Sb[v % 2][:, g // 2, (g % 2) * S:(g % 2 + 1) * S],
                        in1=maskb[kb][:, c, :], scale=-1.0, scalar=BIG, op0=ALU.add, op1=ALU.min,
                        accum_out=nmax[:, v % NPR, g:g + 1])
                ins.then_inc(masked, 1)

            def out_block(su, kb, b):
                dve.wait_ge(pv_done, su + 1 + PV0)
                dve.tensor_copy(OT[:, kb, bass.ds(b * S, S)], Ob[:, 0:S]).then_inc(ot_out, 1)

            def unit(b, v, first=False):
                N, kb, k, c = b * NV + v, v // 8, v % 8 // 2, v % 2
                if first and v == 0:
                    mask_and_max(b, 0, N)
                    mask_and_max(b, 1, N + 1)
                ahead(mask_and_max, b, v, 2)
                dve.wait_ge(turned[1], N + 1)
                dve.wait_ge(pv_done, b * KB + kb - 1 + PV0)
                dve.tensor_copy(PT[kb][:, k, 1, :, c * P:(c + 1) * P], PTb[1][:, :, :]).then_inc(pt1_out, 1)
                if v % 8 == 7 and not first:
                    out_block(b * KB + kb - 1, 1 - kb, b - 1 if kb == 0 else b)
            batches(dve, unit, lambda: out_block(B * KB - 1, 1, B - 1))

        @block.tensor
        def _(pe):
            pe.sem_inc(scored, SC0)
            pe.sem_inc(pv_done, PV0)

            def scores(b, v, N):
                kb, k, c = v // 8, v % 8 // 2, v % 2
                if v % 8 == 0:
                    pe.wait_ge(q_in[kb], b * 16 + 16)
                if c == 0:
                    pe.wait_ge(kp_ready, b * KVH + kb * GB + k + 1)
                pe.wait_ge(masked, N - 1 + MK0)
                for half in range(2):
                    ins = pe.matmul(Sb[v % 2][:, half, :], Qb[kb][:, k, c * P:(c + 1) * P],
                                    KP[k % 2][:, 2 * half:2 * half + 2, :].rearrange("p g t -> p (g t)"),
                                    start=True, stop=True)
                ins.then_inc(scored, 1)

            def turn(v, N, tc):
                pe.wait_ge((pt0_out, pt1_out)[tc], N + PT0)
                for g in range(GR):
                    ins = pe.transpose(PTb[tc][:, g, :], prob[v % NPR][:, g, tc * P:(tc + 1) * P],
                                       ident[:, :])
                ins.then_inc(turned[tc], 1)

            def sum_values(su, kb, steps):
                if steps[0] == 0:
                    pe.wait_ge(pt0_out, su * 8 + 8 + PT0)
                    pe.wait_ge(pt1_out, su * 8 + 8 + PT0)
                    pe.wait_ge(vp_ready, su * GR + GR)
                    pe.wait_ge(ot_out, su + OT0)
                for i in steps:
                    tc, g = i // GR, i % GR
                    for k in range(GB):
                        ins = pe.matmul(Ob[32 * k:32 * k + 32, 0:S], VP[kb][:, tc, k, g, :],
                                        PT[kb][:, k, tc, g, :], start=(i == 0), stop=(i == 2 * GR - 1))
                if steps[-1] == 2 * GR - 1:
                    ins.then_inc(pv_done, 1)

            def unit(b, v, first=False):
                N, kb = b * NV + v, v // 8
                if first and v == 0:
                    scores(b, 0, N)
                    scores(b, 1, N + 1)
                ahead(scores, b, v, 2)
                pe.wait_ge(exp_done, N + 1)
                turn(v, N, 0)
                turn(v, N, 1)
                if v % 8 >= 1 and not first:
                    sum_values(b * KB + kb - 1, 1 - kb, [v % 8 - 1] if v % 8 < 7 else [6, 7])
            batches(pe, unit, lambda: sum_values(B * KB - 1, 1, list(range(2 * GR))))


def closing(nc, x, ident, OT, sums, wo_d, lastp_d, out):
    with ExitStack() as ctx:
        def sb(name, shape, dt=F32):
            return ctx.enter_context(nc.sbuf_tensor("c_" + name, shape, dt))

        def bank(name, shape):
            return ctx.enter_context(nc.psum_tensor("c_" + name, shape, F32))

        def sem(name):
            return ctx.enter_context(nc.semaphore("c_" + name))

        wo, lastp = sb("wo", [P, KB, D]), sb("lastp", [P, 3, D])
        woh, wol = sb("woh", [P, KB, D], F32R), sb("wol", [P, KB, D], F32R)
        rsum = sb("rsum", [P, CH, KVH * GR])
        On = [sb(f"On{i}", [P, D]) for i in range(2)]
        Oh, Ol = sb("Oh", [P, KB, TOK], F32R), sb("Ol", [P, KB, TOK], F32R)
        stats, mv, rstd = sb("stats", [P, CH, 6]), sb("mv", [P, CH, 2]), sb("rstd", [P, CH])
        minus_half = sb("minus_half", [P, CH])
        y = sb("y", [P, CH, D])
        nat = [bank(f"nat{i}", [P, D]) for i in range(2)]
        back = [bank(f"back{i}", [P, KB, P]) for i in range(2)]
        res = [bank(f"res{i}", [P, 512]) for i in range(2)]

        wo_in, lastp_in, wo_hi, wo_lo = sem("wo_in"), sem("lastp_in"), sem("wo_hi"), sem("wo_lo")
        rsum_done, natural, normed, turned = sem("rsum_done"), sem("natural"), sem("normed"), sem("turned")
        o_hi, o_lo, res_done, res_added = sem("o_hi"), sem("o_lo"), sem("res_done"), sem("res_added")
        bo_added, stat_done, aggr_done = sem("bo_added"), sem("stat_done"), sem("aggr_done")
        rstd_step, rstd_ready = sem("rstd_step"), sem("rstd_ready")
        centered, scaled, stored = sem("centered"), sem("scaled"), sem("stored")
        shifted = sem("shifted")
        block = ctx.enter_context(nc.Block())

        @block.sync
        def _(sp):
            sp.dma_start(wo[:, :, :], wo_d).then_inc(wo_in, 16)
            sp.dma_start(lastp[:, :, :], lastp_d).then_inc(lastp_in, 16)
            for half in range(2):
                sp.wait_ge(shifted, (half + 1) * CH // 2)
                sp.dma_start(out.rearrange("(c p) d -> p c d", p=P)[:, half * 4:half * 4 + 4, :],
                             y[:, half * 4:half * 4 + 4, :]).then_inc(stored, 16)
            sp.wait_ge(stored, 32)

        @block.gpsimd
        def _(pool):
            pool.memset(minus_half[:, :], -0.5).then_inc(rstd_step, 1)
            pool.wait_ge(wo_in, 16)
            pool.tensor_copy(woh[:, :, :], wo[:, :, :]).then_inc(wo_hi, 1)
            pool.wait_ge(wo_hi, 1)
            pool.tensor_tensor(wol[:, :, :], wo[:, :, :], woh[:, :, :].bitcast(F32),
                               ALU.subtract).then_inc(wo_lo, 1)
            pool.wait_ge(lastp_in, 16)
            bo = lastp[:, 0:1, :].to_broadcast([P, CH, D])
            pool.tensor_tensor(x[:, :, :], x[:, :, :], bo, ALU.add).then_inc(bo_added, 1)
            for half in range(2):
                cs = slice(half * 4, half * 4 + 4)
                pool.wait_ge(aggr_done, half * 4 + 4)
                pool.tensor_scalar(rstd[:, cs], mv[:, cs, 1], L1_EPS, None, ALU.add).then_inc(rstd_step, 1)
                pool.wait_ge(rstd_step, half + 2)
                pool.tensor_tensor(rstd[:, cs], rstd[:, cs], minus_half[:, cs],
                                   ALU.pow).then_inc(rstd_ready, 1)
            for c in range(CH):
                pool.wait_ge(scaled, c + 1)
                pool.tensor_tensor(y[:, c, :], y[:, c, :], lastp[:, 2, :], ALU.add).then_inc(shifted, 1)

        @block.scalar
        def _(act):
            for c in range(CH):
                act.wait_ge(turned, c + 1)
                act.activation(Oh[:, :, c * P:(c + 1) * P], back[c % 2][:, :, :],
                               ACT.Copy).then_inc(o_hi, 1)

        @block.vector
        def _(dve):
            dve.reciprocal(rsum[:, :, :], sums[:, :, :]).then_inc(rsum_done, 1)
            dve.wait_ge(rsum_done, 1)

            def normalize(c):
                dve.wait_ge(natural, c + 1)
                if c >= 2:
                    dve.wait_ge(turned, c - 1)
                r = rsum[:, c, :].rearrange("p (h o) -> p h o", o=1).to_broadcast([P, KVH * GR, HD])
                dve.tensor_tensor(On[c % 2][:, :].rearrange("p (h d) -> p h d", d=HD),
                                  nat[c % 2][:, :].rearrange("p (h d) -> p h d", d=HD), r,
                                  ALU.mult).then_inc(normed, 1)

            def add(c):
                if c == 0:
                    dve.wait_ge(bo_added, 1)
                dve.wait_ge(res_done, c + 1)
                dve.tensor_tensor(x[:, c, :], res[c % 2][:, 0:D], x[:, c, :], ALU.add).then_inc(res_added, 1)
                dve.wait_ge(res_added, c + 1)
                dve.bn_stats(stats[:, c, :], x[:, c, :]).then_inc(stat_done, 1)
                dve.wait_ge(stat_done, c + 1)
                dve.bn_aggr(mv[:, c, :], stats[:, c, :]).then_inc(aggr_done, 1)

            normalize(0)
            for c in range(CH):
                if c + 1 < CH:
                    normalize(c + 1)
                dve.wait_ge(o_hi, c + 1)
                dve.tensor_tensor(Ol[:, :, c * P:(c + 1) * P], back[c % 2][:, :, :],
                                  Oh[:, :, c * P:(c + 1) * P].bitcast(F32), ALU.subtract).then_inc(o_lo, 1)
                if c >= 1:
                    add(c - 1)
            add(CH - 1)
            dve.wait_ge(lastp_in, 16)
            for c in range(CH):
                dve.wait_ge(rstd_ready, c // 4 + 1)
                dve.tensor_scalar(y[:, c, :], x[:, c, :], mv[:, c, 0:1], rstd[:, c:c + 1],
                                  ALU.subtract, ALU.mult).then_inc(centered, 1)
                dve.wait_ge(centered, c + 1)
                dve.tensor_tensor(y[:, c, :], y[:, c, :], lastp[:, 1, :], ALU.mult).then_inc(scaled, 1)

        @block.tensor
        def _(pe):
            def natural_chunk(c):
                if c >= 2:
                    pe.wait_ge(normed, c - 1)
                for kb in range(KB):
                    ins = pe.transpose(nat[c % 2][:, kb * P:(kb + 1) * P], OT[:, kb, c * P:(c + 1) * P],
                                       ident[:, :])
                ins.then_inc(natural, 1)

            def out_chunk(c):
                pe.wait_ge(o_lo, c + 1)
                if c >= 2:
                    pe.wait_ge(res_added, c - 1)
                n = 0
                for kb in range(KB):
                    for a, w in ((Ol, woh), (Oh, wol), (Oh, woh)):
                        n += 1
                        ins = pe.matmul(res[c % 2][:, 0:D], a[:, kb, c * P:(c + 1) * P], w[:, kb, :],
                                        start=(n == 1), stop=(n == 6))
                ins.then_inc(res_done, 1)

            natural_chunk(0)
            for c in range(CH):
                if c + 1 < CH:
                    natural_chunk(c + 1)
                pe.wait_ge(normed, c + 1)
                if c >= 2:
                    pe.wait_ge(o_lo, c - 1)
                for kb in range(KB):
                    ins = pe.transpose(back[c % 2][:, kb, :], On[c % 2][:, kb * P:(kb + 1) * P], ident[:, :])
                ins.then_inc(turned, 1)
                if c == 1:
                    pe.wait_ge(wo_lo, 1)
                if c >= 1:
                    out_chunk(c - 1)
            out_chunk(CH - 1)


def build(nc, x_d, ident_d, ctx_t, packs_a, packs_b, params, w1_d, w2_d, mlpp_d, wq_d, wk_d, wv_d,
          l1p_d, mask_d, gmask_d, wo_d, lastp_d, out):
    with ExitStack() as ctx:
        def sb(name, shape, dt=F32):
            return ctx.enter_context(nc.sbuf_tensor(name, shape, dt))

        x = sb("x", [P, CH, D])
        ident = sb("ident", [P, P])
        cross_attentions(nc, x, ident, x_d, ident_d, ctx_t, packs_a, packs_b, params)
        feed_forward(nc, x, ident, w1_d, w2_d, mlpp_d)
        OT, sums = sb("OT", [P, KB, TOK]), sb("row_sums", [P, CH, KVH * GR])
        with ExitStack() as inner:
            Qr = inner.enter_context(nc.sbuf_tensor("Qr", [P, KVH, TOK], F32R))
            Kr = inner.enter_context(nc.sbuf_tensor("Kr", [P, KVH, TOK], F32R))
            V = inner.enter_context(nc.sbuf_tensor("V", [P, CH, KVH * HD], F32))
            grouped_projections(nc, x, ident, Qr, Kr, V, ctx_t, wq_d, wk_d, wv_d, l1p_d)
            grouped_attention(nc, ident, Qr, Kr, V, OT, sums, mask_d, gmask_d)
        closing(nc, x, ident, OT, sums, wo_d, lastp_d, out)


def kernel(**inputs):
    import numpy as np
    import concourse.bacc as bacc
    from concourse.bass_utils import run_bass_kernel_spmd as run

    def f(name):
        return np.ascontiguousarray(inputs[name])

    def feature_major(w):
        return w.reshape(KC, P, -1).transpose(1, 0, 2)

    def rows(v):
        return np.broadcast_to(v.reshape(1, -1), (P, v.size))

    def queries(w):
        w = w.reshape(-1, KVH, 1, GR * HD)
        return np.broadcast_to(w, (w.shape[0], KVH, REP, GR * HD)).reshape(w.shape[0], -1)

    def keys(w):
        w = w.reshape(-1, KVH, 1, HD)
        return np.broadcast_to(w, (w.shape[0], KVH, REP * GR, HD)).reshape(w.shape[0], -1)

    packs_a, packs_b, params = [], [], []
    for i in (1, 2):
        L = "L0_xattn_"
        for g in range(NG):
            cols, heads = slice(g * GC, (g + 1) * GC), slice(g * HG, (g + 1) * HG)
            parts = [feature_major(f(f"{L}w{n}{i}")[:, cols]).reshape(P, -1) for n in "qkv"]
            parts += [f(f"{L}b{n}{i}").reshape(H, K)[heads].T for n in "qk"]
            parts += [f(f"{L}bias_k{i}").reshape(H, K)[heads].T]
            parts += [rows(f(f"{L}bv{i}")[cols]), rows(f(f"{L}bias_v{i}").reshape(-1)[cols])]
            packs_a.append(np.concatenate(parts, 1))
            wo = f(f"{L}wo{i}").reshape(H, K, D)[heads].transpose(1, 0, 2).reshape(P, -1)
            packs_b.append(np.concatenate([wo, f(f"{L}bias_v{i}").reshape(H, K)[heads].T], 1))
        params.append(np.concatenate([f(f"{L}ln{i}_scale").reshape(KC, P).T,
                                      f(f"{L}ln{i}_offset").reshape(KC, P).T,
                                      rows(f(f"{L}bo{i}"))], 1))
    arrays = {
        "x": f("x").reshape(TOK, D),
        "ident": np.eye(P, dtype=np.float32),
        "ctx_t": np.ascontiguousarray(f("ctx_2048").reshape(TOK, D).T),
        "packs_a": np.stack(packs_a + packs_a[:2]),
        "packs_b": np.stack(packs_b + packs_b[:1]),
        "params": np.stack(params + params[:1]),
        "w1": feature_major(f("L0_xattn_w_fc1")),
        "w2": f("L0_xattn_w_fc2").reshape(FC, P, D).transpose(1, 0, 2),
        "mlpp": np.concatenate([f("L0_xattn_ln_mlp_scale").reshape(KC, P).T,
                                f("L0_xattn_ln_mlp_offset").reshape(KC, P).T,
                                f("L0_xattn_b_fc1").reshape(FC, P).T, rows(f("L0_xattn_b_fc2"))], 1),
        "wq": feature_major(queries(f("L1_xattn_Wq"))),
        "wk": feature_major(keys(f("L1_xattn_Wk"))),
        "wv": feature_major(f("L1_xattn_Wv")),
        "l1p": np.concatenate([queries(f("L1_xattn_bq")).reshape(KVH, P).T,
                               keys(f("L1_xattn_bk")).reshape(KVH, P).T, rows(f("L1_xattn_bv"))], 1),
        "mask": f("mask_Bx1xSxS2_ff0").reshape(TOK, S),
        "gmask": (np.arange(P)[:, None] // HD % GR == np.arange(GR)).astype(np.float32),
        "wo": f("L1_xattn_Wo").reshape(KB, P, D).transpose(1, 0, 2),
        "lastp": np.stack([rows(f(f"L1_xattn_{n}")) for n in ("bo", "gamma", "beta")], 1),
    }
    arrays = {n: np.ascontiguousarray(a) for n, a in arrays.items()}
    nc = bacc.Bacc("TRN2", target_bir_lowering=False, num_devices=1)
    args = [nc.dram_tensor(n + "_dram", a.shape, F32, kind="ExternalInput").ap() for n, a in arrays.items()]
    out = nc.dram_tensor("out_dram", (TOK, D), F32, kind="ExternalOutput").ap()
    build(nc, *args, out)
    r = run(nc, [{n + "_dram": a for n, a in arrays.items()}], core_ids=[0])
    return r.results[0]["out_dram"].reshape(B, S, D)
```

```python
from contextlib import ExitStack

import concourse.bass as bass
from concourse import mybir

F32 = mybir.dt.float32
F32R = mybir.dt.float32r
ALU = mybir.AluOpType
ACT = mybir.ActivationFunctionType
AX = mybir.AxisListType

P = 128
B, S, D = 4, 256, 256
TOK = B * S
CH = TOK // P
KC = D // P
LN_EPS = 1e-5

H, K = 16, 128
ATT = 2
HG = 2
NG = H // HG
UN = HG * B
GC = HG * K
TP = S + 2
NQKV = 3 * KC * GC
NWO = HG * D
C_BQ = NQKV
C_KB = NQKV + 2 * HG
C_BV = NQKV + 3 * HG
C_VB = C_BV + GC
NPA = C_VB + GC
NPB = NWO + HG
NPAR = 2 * KC + D

F = 1024
FC = F // P

KVH, GR, HD = 8, 4, 8
KB = 2
GB = KVH // KB
REP = P // (GR * HD)
L1_EPS = 1e-6
BIG = 3.0e38

EXP0 = 4
TR0 = 2
VLO0 = 2
TURN0 = 2
FULL0 = 3
HLO0 = 2
SCORE0 = 1
PTLO0 = 1
OLO0 = 1


KT, QT, VT = range(0, 4), range(4, 8), range(8, 12)


def slots(u, first=False, last=False):
    t = 3 * (u // 2)
    if u % 2:
        a = None if first and u == 1 else ("wo", (u // 2 - 1) % B)
        b = ("proj", t + 2)
    else:
        a, b = ("proj", t), ("proj", t + 1)
    if last:
        a, b = (x if x is None or x[0] == "wo" else ("proj", VT[x[1]]) if x[1] < 4 else None
                for x in (a, b))
    return a, b


PRO = len(KT) + len(QT)
USE0 = len(VT) + PRO - 1


def use(G, u, where, first=False, last=False):
    if last:
        n = sum(x is not None for v in range(u) for x in slots(v, last=True))
        n += where * (slots(u, last=True)[0] is not None)
    else:
        n = 2 * u + where + (1 if first and u == 0 else 0)
    return G * 2 * UN + USE0 + n


def prologue_use(G, j):
    return G * 2 * UN + len(VT) + j


def last_use(G):
    return use(G, UN, 0, last=True)


def output_use(G, b, last):
    return use(G, 2 * b - 1, 0, last=last) if b else G * 2 * UN + USE0 - 2


def cross_attentions(nc, x, ident, x_d, ident_d, ctx_t, packs_a, packs_b, params):
    with ExitStack() as ctx:
        def sb(name, shape, dt=F32):
            return ctx.enter_context(nc.sbuf_tensor(name, shape, dt))

        def sb2(name, shape, dt=F32):
            return [sb(f"{name}{i}", shape, dt) for i in range(2)]

        def bank(name, shape):
            return ctx.enter_context(nc.psum_tensor(name, shape, F32))

        def sem(name):
            return ctx.enter_context(nc.semaphore(name))

        cTh, cTl = sb("cTh", [P, KC, TOK], F32R), sb("cTl", [P, KC, TOK], F32R)
        hTh, hTl = sb("hTh", [P, KC, TOK], F32R), sb("hTl", [P, KC, TOK], F32R)
        pack_a, pack_b = sb("pack_a", [P, NPA]), sb("pack_b", [P, NPB])
        wh, wl = sb2("wh", [P, NQKV], F32R), sb2("wl", [P, NQKV], F32R)
        woh, wol = sb2("woh", [P, NWO], F32R), sb2("wol", [P, NWO], F32R)
        bcol, vrow, ocol = sb2("bcol", [P, 3 * HG]), sb2("vrow", [P, GC]), sb2("ocol", [P, HG])
        Qh, Ql = sb2("Qh", [P, HG, TOK], F32R), sb2("Ql", [P, HG, TOK], F32R)
        Kh, Kl = sb2("Kh", [P, HG, B, TP], F32R), sb2("Kl", [P, HG, B, TP], F32R)
        Vh, Vl = sb2("Vh", [P, CH, GC], F32R), sb2("Vl", [P, CH, GC], F32R)
        Oh, Ol = sb2("Oh", [P, HG, S], F32R), sb2("Ol", [P, HG, S], F32R)
        prob = sb2("prob", [P, 2, TP])
        PTh, PTl = sb2("PTh", [P, 2, S], F32R), sb2("PTl", [P, 2, S], F32R)
        work = sb2("work", [P, 2, D])
        attp = sb("attp", [P, NPAR])
        minus_half = sb("minus_half", [P, CH])
        nmax, sums, rsum = sb("nmax", [P, 2, 2]), sb("sums", [P, 2, 2]), sb("rsum", [P, 2, 2])
        stats, mv, rstd = sb("stats", [P, CH, 6]), sb("mv", [P, CH, 2]), sb("rstd", [P, CH])

        Sb = [bank(f"Sb{i}", [P, 2, 512]) for i in range(2)]
        PTb = bank("PTb", [P, 2, S])
        Ob = bank("Ob", [P, 512])
        slot_bank = [bank("Ab", [P, 2, D]), bank("Bb", [P, 2, D])]

        x_in, ident_in = sem("x_in"), sem("ident_in")
        ctx_in = [sem(f"ctx_in{i}") for i in range(B)]
        ctx_hi, ctx_split = sem("ctx_hi"), sem("ctx_split")
        pack_a_in, pack_b_in = sem("pack_a_in"), sem("pack_b_in")
        v0_in, kq0_in, w0_hi, w0_lo, bias0_step = (
            sem(n) for n in ("v0_in", "kq0_in", "w0_hi", "w0_lo", "bias0_step"))
        qkv_ready, wo_ready, pool_step = sem("qkv_ready"), sem("wo_ready"), sem("pool_step")
        stood, rstd_step, rstd_ready = sem("stood"), sem("rstd_step"), sem("rstd_ready")
        attp_in, bo_added = sem("attp_in"), sem("bo_added")
        ln_step, xn_ready, xn_turned = sem("ln_step"), sem("xn_ready"), sem("xn_turned")
        h_full, h_hi, h_lo = sem("h_full"), sem("h_hi"), sem("h_lo")
        slot_done, proj_hi, drained = sem("slot_done"), sem("proj_hi"), sem("drained")
        v_hi, v_lo = sem("v_hi"), sem("v_lo")
        wo_step, kb_step, kb_ready = sem("wo_step"), sem("kb_step"), sem("kb_ready")
        scored, max_done, exp_done = sem("scored"), sem("max_done"), sem("exp_done")
        rsum_done, normed, transposed = sem("rsum_done"), sem("normed"), sem("transposed")
        pt_hi, pt_lo = sem("pt_hi"), sem("pt_lo")
        pv_done, o_hi, o_lo = sem("pv_done"), sem("o_hi"), sem("o_lo")

        def stand(eng, semaphore, value):
            eng.wait_ge(semaphore, value)
            eng.sem_inc(stood, 1)

        def wcol(w, which, kc, hh=None):
            c = (which * KC + kc) * GC
            return w[:, c:c + GC] if hh is None else w[:, c + hh * K:c + (hh + 1) * K]

        def kq_tile(t, i, keys, queries):
            hh, half = t % 2, t % 4 // 2
            if t in QT:
                out = queries[i][:, hh, half * 512:(half + 1) * 512]
                return hh, half, 0, out.rearrange("p (c t) -> p c t", c=2)
            return hh, half, 1, keys[i][:, hh, 2 * half:2 * half + 2, 0:S]

        def tok(b, c=0, n=S):
            return slice(b * S + c, b * S + c + n)

        ctx_at = [work[0], work[1], prob[0], prob[1]]

        def att_loop(eng, prologue, unit, epilogue):
            with eng.Fori(0, ATT) as a:
                G0 = a * NG
                prologue(a, G0)
                for u in range(2):
                    unit(a, G0, 0, u, first=True)
                with eng.Fori(0, NG // 2 - 1) as j:
                    for p in range(2):
                        G = G0 + j * 2 + p
                        for u in range(2, UN):
                            unit(a, G, p, u)
                        for u in range(2):
                            unit(a, G + 1, 1 - p, u)
                for u in range(2, UN):
                    unit(a, G0 + NG - 2, 0, u)
                for u in range(UN):
                    unit(a, G0 + NG - 1, 1, u, last=True)
                epilogue(a, G0 + NG - 1)

        def b_before(G, p, u, first, last):
            if u == 0 and first:
                return None
            v, Gv, pv = (UN - 1, G - 1, 1 - p) if u == 0 else (u - 1, G, p)
            at_last = last and u > 0
            b = slots(v, first, at_last)[1]
            return b and (b[1], Gv + 1, 1 - pv, use(Gv, v, 1, first, at_last))

        block = ctx.enter_context(nc.Block())

        @block.sync
        def _(sp):
            v0 = 2 * KC * GC
            sp.dma_start(pack_a[:, v0:], packs_a[0][:, v0:]).then_inc(v0_in, 16)

            def load_ctx(b):
                sp.dma_start(ctx_at[b][:, :, 0:S],
                             ctx_t[:, tok(b)].rearrange("(k p) t -> p k t", p=P)).then_inc(ctx_in[b], 16)
            load_ctx(0)
            load_ctx(1)
            sp.dma_start(x[:, :, :], x_d.rearrange("(c p) d -> p c d", p=P)).then_inc(x_in, 16)
            load_ctx(2)
            load_ctx(3)
            sp.dma_start(pack_a[:, 0:v0], packs_a[0][:, 0:v0]).then_inc(kq0_in, 16)
            sp.dma_start(ident[:, :], ident_d).then_inc(ident_in, 16)
            sp.dma_start(attp[:, :], params[0]).then_inc(attp_in, 16)
            sp.dma_start(pack_b[:, :], packs_b[0]).then_inc(pack_b_in, 16)
            sp.wait_ge(w0_lo, 3)
            sp.wait_ge(bias0_step, 3)
            sp.dma_start(pack_a[:, :], packs_a[1]).then_inc(pack_a_in, 16)
            with sp.Fori(0, ATT) as a:
                with sp.Fori(0, NG) as g:
                    sp.wait_ge(wo_ready, a * NG + g + 1)
                    sp.dma_start(pack_b[:, :], packs_b[bass.ds(a * NG + g + 1, 1), :, :]
                                 .rearrange("g p c -> (g p) c")).then_inc(pack_b_in, 16)
                    sp.wait_ge(qkv_ready, a * NG + g + 1)
                    sp.dma_start(pack_a[:, :], packs_a[bass.ds(a * NG + g + 2, 1), :, :]
                                 .rearrange("g p c -> (g p) c")).then_inc(pack_a_in, 16)
                sp.wait_ge(bo_added, a + 1)
                sp.wait_ge(h_lo, HLO0 + a * B + B)
                sp.dma_start(attp[:, :], params[bass.ds(a + 1, 1), :, :]
                             .rearrange("a p c -> (a p) c")).then_inc(attp_in, 16)
            sp.wait_ge(pack_a_in, 16 * (ATT * NG + 1))
            sp.wait_ge(pack_b_in, 16 * (ATT * NG + 1))
            sp.wait_ge(attp_in, 16 * (ATT + 1))

        @block.gpsimd
        def _(pool):
            pool.sem_inc(v_lo, VLO0)
            pool.memset(minus_half[:, :], -0.5).then_inc(rstd_step, 1)

            def split_qkv(G, i):
                done = (G - 1) * 5
                stand(pool, pack_a_in, G * 16)
                q, bq = pack_a[:, 0:KC * GC], pack_a[:, C_BQ:C_BQ + HG]
                pool.tensor_scalar(q, q, K ** -0.5, None, ALU.mult).then_inc(pool_step, 1)
                pool.tensor_scalar(bq, bq, K ** -0.5, None, ALU.mult).then_inc(pool_step, 1)
                stand(pool, pool_step, done + 2)
                pool.tensor_copy(wh[i][:, :], pack_a[:, 0:NQKV]).then_inc(pool_step, 1)
                pool.tensor_copy(bcol[i][:, :], pack_a[:, C_BQ:C_BQ + 3 * HG]).then_inc(pool_step, 1)
                pool.tensor_tensor(vrow[i][:, :], pack_a[:, C_BV:C_BV + GC], pack_a[:, C_VB:C_VB + GC],
                                   ALU.subtract).then_inc(pool_step, 1)
                pool.wait_ge(pool_step, done + 5)
                pool.tensor_tensor(wl[i][:, :], pack_a[:, 0:NQKV], wh[i][:, :].bitcast(F32),
                                   ALU.subtract).then_inc(qkv_ready, 1)

            def split_wo(G, i):
                stand(pool, pack_b_in, G * 16 + 16)
                pool.tensor_copy(woh[i][:, :], pack_b[:, 0:NWO]).then_inc(wo_step, 1)
                pool.tensor_copy(ocol[i][:, :], pack_b[:, NWO:NWO + HG]).then_inc(wo_step, 1)
                pool.wait_ge(wo_step, G * 2 + 2)
                pool.tensor_tensor(wol[i][:, :], pack_b[:, 0:NWO], woh[i][:, :].bitcast(F32),
                                   ALU.subtract).then_inc(wo_ready, 1)

            def learned_key(G, i):
                col = bcol[i][:, 2 * HG:3 * HG].rearrange("p (h o t) -> p h o t", o=1, t=1)
                col = col.to_broadcast([P, HG, B, 2])
                hi, lo = Kh[i][:, :, :, S:TP], Kl[i][:, :, :, S:TP]
                pool.tensor_copy(hi, col).then_inc(kb_step, 1)
                pool.wait_ge(kb_step, G + 1)
                pool.tensor_tensor(lo, col, hi.bitcast(F32), ALU.subtract).then_inc(kb_ready, 1)

            def value_lo(G, i, b):
                pool.wait_ge(v_hi, G * B + b + 1)
                pool.tensor_tensor(Vl[i][:, 2 * b:2 * b + 2, :], work[b % 2][:, :, :],
                                   Vh[i][:, 2 * b:2 * b + 2, :].bitcast(F32),
                                   ALU.subtract).then_inc(v_lo, 1)

            pool.wait_ge(v0_in, 16)
            pool.tensor_tensor(vrow[0][:, :], pack_a[:, C_BV:C_BV + GC], pack_a[:, C_VB:C_VB + GC],
                               ALU.subtract).then_inc(bias0_step, 1)
            bq = pack_a[:, C_BQ:C_BQ + HG]
            pool.tensor_scalar(bq, bq, K ** -0.5, None, ALU.mult).then_inc(bias0_step, 1)
            pool.wait_ge(bias0_step, 2)
            pool.tensor_copy(bcol[0][:, :], pack_a[:, C_BQ:C_BQ + 3 * HG]).then_inc(bias0_step, 1)
            pool.wait_ge(bias0_step, 3)
            learned_key(0, 0)
            for b in range(B):
                value_lo(0, 0, b)

            def deviations(k):
                stand(pool, ln_step, k * 2 * CH + 2 * CH)
                pool.tensor_scalar(rstd[:, :], mv[:, :, 1], LN_EPS, None,
                                   ALU.add).then_inc(rstd_step, 1)
                pool.wait_ge(rstd_step, k + 2)
                pool.tensor_tensor(rstd[:, :], rstd[:, :], minus_half[:, :],
                                   ALU.pow).then_inc(rstd_ready, 1)
            deviations(0)
            split_qkv(1, 1)
            split_wo(0, 0)

            def prologue(a, G):
                pool.wait_ge(xn_ready, a * B + B)
                pool.wait_ge(attp_in, a * 16 + 16)
                bo = attp[:, 2 * KC:NPAR].rearrange("p (o d) -> p o d", o=1).to_broadcast([P, CH, D])
                pool.tensor_tensor(x[:, :, :], x[:, :, :], bo, ALU.add).then_inc(bo_added, 1)

            def unit(a, G, p, u, first=False, last=False):
                if u == 0:
                    stand(pool, scored, G * UN + SCORE0)
                    learned_key(G + 1, 1 - p)
                    pool.wait_ge(drained, use(G, 0, 0, first=first))
                    split_qkv(G + 2, p)
                if u == 2:
                    pool.wait_ge(slot_done, use(G, 1, 0) + 1)
                    split_wo(G + 1, 1 - p)
                for item in slots(u, first, last):
                    if item and item[0] == "proj" and item[1] in VT:
                        value_lo(G + 1, 1 - p, item[1] - VT[0])

            att_loop(pool, prologue, unit, lambda a, G: deviations(a + 1))

        @block.scalar
        def _(act):
            act.sem_inc(exp_done, EXP0)
            act.sem_inc(h_full, FULL0)

            def ctx_part(b):
                act.wait_ge(ctx_in[b], 16)
                act.activation(cTh[:, :, tok(b)], ctx_at[b][:, :, 0:S], ACT.Copy).then_inc(ctx_hi, 1)

            def project_hi(G, i, t, where, n):
                hh, half, which, out = kq_tile(t, i, Kh, Qh)
                act.wait_ge(slot_done, n + 1)
                c = hh + which * HG
                act.activation(out, slot_bank[where][:, :, :], ACT.Identity,
                               bias=bcol[i][:, c:c + 1]).then_inc(proj_hi, 1)

            def value_hi(G, i, b, n):
                act.wait_ge(drained, n + 1)
                act.activation(Vh[i][:, 2 * b:2 * b + 2, :], work[b % 2][:, :, :],
                               ACT.Copy).then_inc(v_hi, 1)

            def exps(U, r):
                for c in range(2):
                    act.wait_ge(max_done, U + 1)
                    act.wait_ge(transposed, U - 1 + TR0)
                    act.activation(prob[r][:, c, 0:S + 1], Sb[r][:, c, 0:S + 1], ACT.Exp,
                                   bias=nmax[:, r, c:c + 1],
                                   accum_out=sums[:, r, c:c + 1]).then_inc(exp_done, 1)

            def output_hi(G, p, u, last):
                b, hh = u // HG, u % HG
                if hh == 0:
                    act.wait_ge(slot_done, output_use(G, b, last) + 1)
                if u == 0:
                    act.wait_ge(wo_ready, G + 1)
                act.wait_ge(pv_done, G * UN + u + 1)
                act.activation(Oh[b % 2][:, hh, :], Ob[:, 0:S], ACT.Identity,
                               bias=ocol[p][:, hh:hh + 1]).then_inc(o_hi, 1)

            v0, k0 = 2 * KC * GC, KC * GC
            act.wait_ge(v0_in, 16)
            act.activation(wh[0][:, v0:NQKV], pack_a[:, v0:NQKV], ACT.Copy).then_inc(w0_hi, 1)
            ctx_part(0)
            ctx_part(1)
            value_hi(0, 0, 0, 0)
            ctx_part(2)
            value_hi(0, 0, 1, 1)
            ctx_part(3)
            act.wait_ge(kq0_in, 16)
            act.activation(wh[0][:, k0:v0], pack_a[:, k0:v0], ACT.Copy).then_inc(w0_hi, 1)
            act.activation(wh[0][:, 0:k0], pack_a[:, 0:k0], ACT.Copy, scale=K ** -0.5).then_inc(w0_hi, 1)
            value_hi(0, 0, 2, 2)
            value_hi(0, 0, 3, 3)
            act.wait_ge(bias0_step, 3)

            def prologue(a, G):
                for t in KT:
                    project_hi(G, 0, t, (t + 1) % 2, prologue_use(G, t))
                act.wait_ge(attp_in, a * 16 + 16)
                for b in range(B):
                    act.wait_ge(xn_turned, a * B + b + 1 + TURN0)
                    act.wait_ge(h_lo, a * B + b - 1 + HLO0)
                    for kc in range(KC):
                        act.activation(prob[b % 2][:, kc, 0:S], slot_bank[(b + 1) % 2][:, kc, :],
                                       ACT.Identity, scale=attp[:, kc:kc + 1],
                                       bias=attp[:, KC + kc:KC + kc + 1]).then_inc(h_full, 1)
                    act.wait_ge(h_full, (a * B + b + 1) * 2 + FULL0)
                    act.activation(hTh[:, :, tok(b)], prob[b % 2][:, :, 0:S], ACT.Copy).then_inc(h_hi, 1)
                for t in QT:
                    project_hi(G, 0, t, (t + 1) % 2, prologue_use(G, t))
                exps(G * UN, 0)

            def unit(a, G, p, u, first=False, last=False):
                U = G * UN + u
                before = b_before(G, p, u, first, last)
                if before and before[0] not in VT:
                    project_hi(before[1], before[2], before[0], 1, before[3])
                if u == 0 and not first:
                    output_hi(G - 1, 1 - p, UN - 1, False)
                elif u > 0:
                    output_hi(G, p, u - 1, last)
                if u > 0:
                    item = slots(u - 1, first, last)[0]
                    if item and item[0] == "proj" and item[1] in VT:
                        value_hi(G + 1, 1 - p, item[1] - VT[0], use(G, u - 1, 0, first, last))
                if before and before[0] in VT:
                    value_hi(before[1], before[2], before[0] - VT[0], before[3])
                act.wait_ge(transposed, U + 1 + TR0)
                act.activation(PTh[u % 2][:, :, :], PTb[:, :, :], ACT.Copy).then_inc(pt_hi, 1)
                if not (last and u == UN - 1):
                    exps(U + 1, (u + 1) % 2)
                item = slots(u, first, last)[0]
                if item and item[0] == "proj" and item[1] not in VT:
                    project_hi(G + 1, 1 - p, item[1], 0, use(G, u, 0, first, last))

            att_loop(act, prologue, unit, lambda a, G: output_hi(G, 1, UN - 1, True))

        @block.vector
        def _(dve):
            dve.sem_inc(h_lo, HLO0)
            dve.sem_inc(pt_lo, PTLO0)
            dve.sem_inc(o_lo, OLO0)

            def ctx_part(b):
                dve.wait_ge(ctx_hi, b + 1)
                dve.tensor_tensor(cTl[:, :, tok(b)], ctx_at[b][:, :, 0:S],
                                  cTh[:, :, tok(b)].bitcast(F32), ALU.subtract).then_inc(ctx_split, 1)

            def project_lo(G, i, t, where):
                hh, half, which, lo = kq_tile(t, i, Kl, Ql)
                hi = kq_tile(t, i, Kh, Qh)[3]
                dve.wait_ge(proj_hi, G * 8 + t + 1)
                c = hh + which * HG
                dve.scalar_tensor_tensor(out=lo, in0=slot_bank[where][:, :, :], scalar=bcol[i][:, c:c + 1],
                                         in1=hi.bitcast(F32), op0=ALU.add,
                                         op1=ALU.subtract).then_inc(drained, 1)

            def value_sum(G, i, b, where, n):
                dve.wait_ge(slot_done, n + 1)
                dve.wait_ge(v_lo, G * B + b - 1 + VLO0)
                row = vrow[i][:, :].rearrange("p (o d) -> p o d", o=1).to_broadcast([P, 2, D])
                dve.tensor_tensor(work[b % 2][:, :, :], slot_bank[where][:, :, :], row,
                                  ALU.add).then_inc(drained, 1)

            def row_max(U, r):
                dve.wait_ge(scored, U + 1 + SCORE0)
                dve.tensor_reduce(nmax[:, r, :], Sb[r][:, :, 0:S + 1], AX.X, ALU.max,
                                  negate=True).then_inc(max_done, 1)

            def normalize(U, r):
                dve.wait_ge(exp_done, U * 2 + 2 + EXP0)
                dve.reciprocal(rsum[:, r, :], sums[:, r, :]).then_inc(rsum_done, 1)
                dve.wait_ge(rsum_done, U + 1)
                for c in range(2):
                    dve.tensor_scalar(prob[r][:, c, 0:S], prob[r][:, c, 0:S], rsum[:, r, c:c + 1],
                                      None, ALU.mult).then_inc(normed, 1)

            def moments(k, b):
                for c in range(2 * b, 2 * b + 2):
                    dve.bn_stats(stats[:, c, :], x[:, c, :]).then_inc(ln_step, 1)
                stand(dve, ln_step, k * 2 * CH + 4 * b + 2)
                for c in range(2 * b, 2 * b + 2):
                    dve.bn_aggr(mv[:, c, :], stats[:, c, :]).then_inc(ln_step, 1)

            def add_wo(a, b, n):
                dve.wait_ge(slot_done, n + 1)
                dve.wait_ge(bo_added, a + 1)
                dve.wait_ge(drained, n)
                dve.tensor_tensor(x[:, 2 * b:2 * b + 2, :], slot_bank[0][:, :, :],
                                  x[:, 2 * b:2 * b + 2, :], ALU.add).then_inc(drained, 1)

            def last_add(a, b, n):
                add_wo(a, b, n)
                dve.wait_ge(drained, n + 1)
                moments(a + 1, b)

            def output_lo(G, p, u):
                b, hh = u // HG, u % HG
                dve.wait_ge(o_hi, G * UN + u + 1)
                dve.scalar_tensor_tensor(out=Ol[b % 2][:, hh, :], in0=Ob[:, 0:S],
                                         scalar=ocol[p][:, hh:hh + 1],
                                         in1=Oh[b % 2][:, hh, :].bitcast(F32), op0=ALU.add,
                                         op1=ALU.subtract).then_inc(o_lo, 1)

            v0, k0 = 2 * KC * GC, KC * GC
            dve.wait_ge(w0_hi, 1)
            dve.tensor_tensor(wl[0][:, v0:NQKV], pack_a[:, v0:NQKV], wh[0][:, v0:NQKV].bitcast(F32),
                              ALU.subtract).then_inc(w0_lo, 1)
            ctx_part(0)
            ctx_part(1)
            dve.wait_ge(bias0_step, 1)
            value_sum(0, 0, 0, 1, 0)
            ctx_part(2)
            value_sum(0, 0, 1, 0, 1)
            ctx_part(3)
            dve.wait_ge(x_in, 16)
            moments(0, 0)
            moments(0, 1)
            dve.wait_ge(w0_hi, 2)
            dve.tensor_tensor(wl[0][:, k0:v0], pack_a[:, k0:v0], wh[0][:, k0:v0].bitcast(F32),
                              ALU.subtract).then_inc(w0_lo, 1)
            value_sum(0, 0, 2, 1, 2)
            dve.wait_ge(w0_hi, 3)
            dve.scalar_tensor_tensor(out=wl[0][:, 0:k0], in0=pack_a[:, 0:k0], scalar=K ** -0.5,
                                     in1=wh[0][:, 0:k0].bitcast(F32), op0=ALU.mult,
                                     op1=ALU.subtract).then_inc(w0_lo, 1)
            moments(0, 2)
            moments(0, 3)
            value_sum(0, 0, 3, 0, 3)

            def prologue(a, G):
                for t in KT:
                    project_lo(G, 0, t, (t + 1) % 2)
                dve.wait_ge(rstd_ready, a + 1)

                def turned_lo(b):
                    dve.wait_ge(h_hi, a * B + b + 1)
                    dve.tensor_tensor(hTl[:, :, tok(b)], prob[b % 2][:, :, 0:S],
                                      hTh[:, :, tok(b)].bitcast(F32), ALU.subtract).then_inc(h_lo, 1)
                for b in range(B):
                    if b < 2:
                        dve.wait_ge(v_lo, G * B + 3 + b + VLO0)
                    dve.wait_ge(xn_turned, a * B + b - 1 + TURN0)
                    for c in range(2):
                        ins = dve.tensor_scalar(work[b % 2][:, c, :], x[:, 2 * b + c, :],
                                                mv[:, 2 * b + c, 0:1], rstd[:, 2 * b + c:2 * b + c + 1],
                                                ALU.subtract, ALU.mult)
                    ins.then_inc(xn_ready, 1)
                    if b >= 1:
                        turned_lo(b - 1)
                turned_lo(B - 1)
                for t in QT:
                    project_lo(G, 0, t, (t + 1) % 2)
                row_max(G * UN, 0)
                normalize(G * UN, 0)

            def unit(a, G, p, u, first=False, last=False):
                U = G * UN + u
                before = b_before(G, p, u, first, last)
                if before:
                    t, Gt, i, n = before
                    if t in VT:
                        value_sum(Gt, i, t - VT[0], 1, n)
                    else:
                        project_lo(Gt, i, t, 1)
                if not (last and u == UN - 1):
                    row_max(U + 1, (u + 1) % 2)
                if u == 0 and not first:
                    output_lo(G - 1, 1 - p, UN - 1)
                elif u > 0:
                    output_lo(G, p, u - 1)
                dve.wait_ge(pt_hi, U + 1)
                dve.tensor_tensor(PTl[u % 2][:, :, :], PTb[:, :, :],
                                  PTh[u % 2][:, :, :].bitcast(F32), ALU.subtract).then_inc(pt_lo, 1)
                if not (last and u == UN - 1):
                    normalize(U + 1, (u + 1) % 2)
                item = slots(u, first, last)[0]
                if item:
                    kind, t = item
                    n = use(G, u, 0, first, last)
                    if kind == "wo":
                        (last_add if last and u > 1 else add_wo)(a, t, n)
                    elif t in VT:
                        value_sum(G + 1, 1 - p, t - VT[0], 0, n)
                    else:
                        project_lo(G + 1, 1 - p, t, 0)

            def epilogue(a, G):
                output_lo(G, 1, UN - 1)
                last_add(a, B - 1, last_use(G))

            att_loop(dve, prologue, unit, epilogue)

        @block.tensor
        def _(pe):
            pe.sem_inc(scored, SCORE0)
            pe.sem_inc(transposed, TR0)
            pe.sem_inc(xn_turned, TURN0)

            def three(out, w, m, first, final):
                (w_hi, w_lo), (m_hi, m_lo) = w, m
                pe.matmul(out, w_lo, m_hi, start=first, stop=False)
                pe.matmul(out, w_hi, m_lo, start=False, stop=False)
                return pe.matmul(out, w_hi, m_hi, start=False, stop=final)

            def project(i, t, where):
                tile = slot_bank[where]
                if t in VT:
                    for c in range(2):
                        for kc in range(KC):
                            ins = three(tile[:, c, :],
                                        [s[:, kc, tok(t - VT[0], c * P, P)] for s in (cTh, cTl)],
                                        [wcol(w[i], 2, kc) for w in (wh, wl)],
                                        kc == 0, kc == KC - 1)
                else:
                    hh, half, which, _ = kq_tile(t, i, Kh, Qh)
                    src = (hTh, hTl) if which == 0 else (cTh, cTl)
                    for kc in range(KC):
                        ins = three(tile[:, :, :].rearrange("p a b -> p (a b)"),
                                    [wcol(w[i], which, kc, hh) for w in (wh, wl)],
                                    [s[:, kc, half * 512:(half + 1) * 512] for s in src],
                                    kc == 0, kc == KC - 1)
                ins.then_inc(slot_done, 1)

            def scores(U, G, i, u, last_q=None):
                b, hh, r = u // HG, u % HG, u % 2
                if u == 0:
                    pe.wait_ge(drained, last_q + 1)
                    pe.wait_ge(kb_ready, G + 1)
                pe.wait_ge(exp_done, U * 2 - 2 + EXP0)
                for c in range(2):
                    ins = three(Sb[r][:, c, 0:TP],
                                [w[i][:, hh, tok(b, c * P, P)] for w in (Qh, Ql)],
                                [m[i][:, hh, b, :] for m in (Kh, Kl)], True, True)
                ins.then_inc(scored, 1)

            def wo_tile(Gw, i, b):
                pe.wait_ge(wo_ready, Gw + 1)
                pe.wait_ge(o_lo, Gw * UN + HG * b + HG + OLO0)
                for c in range(2):
                    for hh in range(HG):
                        ins = three(slot_bank[0][:, c, :],
                                    [o[b % 2][:, hh, c * P:(c + 1) * P] for o in (Oh, Ol)],
                                    [w[i][:, hh * D:(hh + 1) * D] for w in (woh, wol)],
                                    hh == 0, hh == HG - 1)
                ins.then_inc(slot_done, 1)

            pe.wait_ge(w0_lo, 1)
            for b in range(B):
                pe.wait_ge(ctx_split, b + 1)
                if b >= 2:
                    pe.wait_ge(drained, b - 1)
                project(0, VT[b], (b + 1) % 2)
            pe.wait_ge(w0_lo, 3)
            pe.wait_ge(ident_in, 16)

            def prologue(a, G):
                for t in KT:
                    pe.wait_ge(drained, prologue_use(G, t) - 1)
                    project(0, t, (t + 1) % 2)
                for b in range(B):
                    pe.wait_ge(xn_ready, a * B + b + 1)
                    if b < 2:
                        pe.wait_ge(drained, prologue_use(G, KT[2 + b]) + 1)
                    else:
                        pe.wait_ge(h_full, (a * B + b - 1) * 2 + FULL0)
                    for c in range(2):
                        for kc in range(KC):
                            ins = pe.transpose(slot_bank[(b + 1) % 2][:, kc, c * P:(c + 1) * P],
                                               work[b % 2][:, c, kc * P:(kc + 1) * P], ident[:, :])
                    ins.then_inc(xn_turned, 1)
                for t in QT:
                    half = kq_tile(t, 0, Kh, Qh)[1]
                    pe.wait_ge(h_lo, a * B + 2 * half + 2 + HLO0)
                    if half == 0:
                        pe.wait_ge(h_full, (a * B + 3 + t % 2) * 2 + FULL0)
                    else:
                        pe.wait_ge(drained, prologue_use(G, t) - 1)
                    project(0, t, (t + 1) % 2)
                scores(G * UN, G, 0, 0, prologue_use(G, QT[-1]))

            def unit(a, G, p, u, first=False, last=False):
                U, b, hh = G * UN + u, u // HG, u % HG
                if u < UN - 1:
                    scores(U + 1, G, p, u + 1)
                elif not last:
                    scores(U + 1, G + 1, 1 - p, 0, use(G, 4, 1))
                pe.wait_ge(normed, U * 2 + 2)
                pe.wait_ge(pt_lo, U + PTLO0)
                for c in range(2):
                    for tc in range(2):
                        ins = pe.transpose(PTb[:, tc, c * P:(c + 1) * P],
                                           prob[u % 2][:, c, tc * P:(tc + 1) * P], ident[:, :])
                ins.then_inc(transposed, 1)
                for where, item in enumerate(slots(u, first, last)):
                    if item is None:
                        continue
                    kind, t = item
                    n = use(G, u, where, first, last)
                    alone = first and u == where or last and u >= 3
                    pe.wait_ge(drained, n if alone else n - 1)
                    if kind == "proj":
                        if t == (VT if last else KT)[0]:
                            pe.wait_ge(qkv_ready, G + 1)
                        project(1 - p, t, where)
                    elif u == 1:
                        wo_tile(G - 1, 1 - p, t)
                    else:
                        wo_tile(G, p, t)
                if hh == 0:
                    pe.wait_ge(v_lo, G * B + b + 1 + VLO0)
                pe.wait_ge(pt_lo, U + 1 + PTLO0)
                pe.wait_ge(o_lo, U + OLO0)
                for tc in range(2):
                    ins = three(Ob[:, 0:S],
                                [v[p][:, 2 * b + tc, hh * K:(hh + 1) * K] for v in (Vh, Vl)],
                                [m[u % 2][:, tc, :] for m in (PTh, PTl)], tc == 0, tc == 1)
                ins.then_inc(pv_done, 1)

            def epilogue(a, G):
                pe.wait_ge(drained, last_use(G))
                wo_tile(G, 1, B - 1)

            att_loop(pe, prologue, unit, epilogue)


def feed_forward(nc, x, ident, w1_d, w2_d, mlpp_d):
    with ExitStack() as ctx:
        def sb(name, shape, dt=F32):
            return ctx.enter_context(nc.sbuf_tensor("m_" + name, shape, dt))

        def bank(name, shape):
            return ctx.enter_context(nc.psum_tensor("m_" + name, shape, F32))

        def sem(name):
            return ctx.enter_context(nc.semaphore("m_" + name))

        w1, w2 = sb("w1", [P, KC, F]), sb("w2", [P, FC, D])
        w1h, w1l = sb("w1h", [P, KC, F], F32R), sb("w1l", [P, KC, F], F32R)
        w2h, w2l = sb("w2h", [P, FC, D], F32R), sb("w2l", [P, FC, D], F32R)
        mlpp = sb("mlpp", [P, 2 * KC + FC + D])
        hTh, hTl = sb("hTh", [P, KC, TOK], F32R), sb("hTl", [P, KC, TOK], F32R)
        Gh, Gl = sb("Gh", [P, FC, TOK], F32R), sb("Gl", [P, FC, TOK], F32R)
        xn = [sb(f"xn{i}", [P, 2, D]) for i in range(2)]
        full = [sb(f"full{i}", [P, KC, S]) for i in range(2)]
        act_out = [sb(f"act_out{i}", [P, 512]) for i in range(2)]
        stats, mv, rstd = sb("stats", [P, CH, 6]), sb("mv", [P, CH, 2]), sb("rstd", [P, CH])
        minus_half = sb("minus_half", [P, CH])
        turn = [bank(f"turn{i}", [P, KC, S]) for i in range(2)]
        hid = [bank(f"hid{i}", [P, 512]) for i in range(2)]
        res = [bank(f"res{i}", [P, 512]) for i in range(2)]

        w1_in, w2_in, mlpp_in = sem("w1_in"), sem("w2_in"), sem("mlpp_in")
        w1_hi, w1_lo, w2_hi, w2_lo = sem("w1_hi"), sem("w1_lo"), sem("w2_hi"), sem("w2_lo")
        ln_step, rstd_step, rstd_ready = sem("ln_step"), sem("rstd_step"), sem("rstd_ready")
        xn_ready, xn_turned, h_full = sem("xn_ready"), sem("xn_turned"), sem("h_full")
        h_hi, h_lo, b2_added = sem("h_hi"), sem("h_lo"), sem("b2_added")
        hid_done, gelu_done, g_hi, g_lo = sem("hid_done"), sem("gelu_done"), sem("g_hi"), sem("g_lo")
        res_done, res_added = sem("res_done"), sem("res_added")
        block = ctx.enter_context(nc.Block())
        NTILE = FC * 2

        @block.sync
        def _(sp):
            sp.dma_start(w1[:, :, :], w1_d).then_inc(w1_in, 16)
            sp.dma_start(mlpp[:, :], mlpp_d).then_inc(mlpp_in, 16)
            sp.dma_start(w2[:, :, :], w2_d).then_inc(w2_in, 16)

        @block.gpsimd
        def _(pool):
            pool.memset(minus_half[:, :], -0.5).then_inc(rstd_step, 1)
            pool.wait_ge(ln_step, 2 * CH)
            pool.tensor_scalar(rstd[:, :], mv[:, :, 1], LN_EPS, None, ALU.add).then_inc(rstd_step, 1)
            pool.wait_ge(rstd_step, 2)
            pool.tensor_tensor(rstd[:, :], rstd[:, :], minus_half[:, :], ALU.pow).then_inc(rstd_ready, 1)
            pool.wait_ge(w2_in, 16)
            pool.tensor_copy(w2h[:, :, :], w2[:, :, :]).then_inc(w2_hi, 1)
            pool.wait_ge(w2_hi, 1)
            pool.tensor_tensor(w2l[:, :, :], w2[:, :, :], w2h[:, :, :].bitcast(F32),
                               ALU.subtract).then_inc(w2_lo, 1)
            pool.wait_ge(xn_ready, B)
            pool.wait_ge(mlpp_in, 16)
            b2 = mlpp[:, 2 * KC + FC:].rearrange("p (o d) -> p o d", o=1).to_broadcast([P, CH, D])
            pool.tensor_tensor(x[:, :, :], x[:, :, :], b2, ALU.add).then_inc(b2_added, 1)

        @block.scalar
        def _(act):
            act.wait_ge(w1_in, 16)
            act.activation(w1h[:, :, :], w1[:, :, :], ACT.Copy).then_inc(w1_hi, 1)
            act.wait_ge(mlpp_in, 16)
            for b in range(B):
                act.wait_ge(xn_turned, b + 1)
                if b >= 2:
                    act.wait_ge(h_lo, b - 1)
                for kc in range(KC):
                    act.activation(full[b % 2][:, kc, :], turn[b % 2][:, kc, :], ACT.Identity,
                                   scale=mlpp[:, kc:kc + 1],
                                   bias=mlpp[:, KC + kc:KC + kc + 1]).then_inc(h_full, 1)
                act.wait_ge(h_full, 2 * b + 2)
                act.activation(hTh[:, :, b * S:(b + 1) * S], full[b % 2][:, :, :],
                               ACT.Copy).then_inc(h_hi, 1)
            for n in range(2):
                for f in range(FC):
                    t = n * FC + f
                    act.wait_ge(hid_done, t + 1)
                    if t >= 2:
                        act.wait_ge(g_lo, t - 1)
                    act.activation(act_out[t % 2][:, :], hid[t % 2][:, :], ACT.Gelu,
                                   bias=mlpp[:, 2 * KC + f:2 * KC + f + 1]).then_inc(gelu_done, 1)
                    act.wait_ge(gelu_done, t + 1)
                    act.activation(Gh[:, f, n * 512:(n + 1) * 512], act_out[t % 2][:, :],
                                   ACT.Copy).then_inc(g_hi, 1)

        @block.vector
        def _(dve):
            for c in range(CH):
                dve.bn_stats(stats[:, c, :], x[:, c, :]).then_inc(ln_step, 1)
            dve.wait_ge(ln_step, CH)
            for c in range(CH):
                dve.bn_aggr(mv[:, c, :], stats[:, c, :]).then_inc(ln_step, 1)
            dve.wait_ge(w1_hi, 1)
            dve.tensor_tensor(w1l[:, :, :], w1[:, :, :], w1h[:, :, :].bitcast(F32),
                              ALU.subtract).then_inc(w1_lo, 1)
            dve.wait_ge(rstd_ready, 1)

            def turned_lo(b):
                dve.wait_ge(h_hi, b + 1)
                dve.tensor_tensor(hTl[:, :, b * S:(b + 1) * S], full[b % 2][:, :, :],
                                  hTh[:, :, b * S:(b + 1) * S].bitcast(F32),
                                  ALU.subtract).then_inc(h_lo, 1)
            for b in range(B):
                if b >= 2:
                    dve.wait_ge(xn_turned, b - 1)
                for c in range(2 * b, 2 * b + 2):
                    ins = dve.tensor_scalar(xn[b % 2][:, c % 2, :], x[:, c, :], mv[:, c, 0:1],
                                            rstd[:, c:c + 1], ALU.subtract, ALU.mult)
                ins.then_inc(xn_ready, 1)
                if b >= 1:
                    turned_lo(b - 1)
            turned_lo(B - 1)
            for n in range(2):
                for f in range(FC):
                    t = n * FC + f
                    dve.wait_ge(g_hi, t + 1)
                    dve.tensor_tensor(Gl[:, f, n * 512:(n + 1) * 512], act_out[t % 2][:, :],
                                      Gh[:, f, n * 512:(n + 1) * 512].bitcast(F32),
                                      ALU.subtract).then_inc(g_lo, 1)
                if n == 1:
                    dve.wait_ge(b2_added, 1)
            for c in range(CH):
                dve.wait_ge(res_done, c + 1)
                dve.tensor_tensor(x[:, c, :], res[c % 2][:, 0:D], x[:, c, :], ALU.add).then_inc(res_added, 1)

        @block.tensor
        def _(pe):
            def three(out, w, m, first, final):
                (w_hi, w_lo), (m_hi, m_lo) = w, m
                pe.matmul(out, w_lo, m_hi, start=first, stop=False)
                pe.matmul(out, w_hi, m_lo, start=False, stop=False)
                return pe.matmul(out, w_hi, m_hi, start=False, stop=final)

            for b in range(B):
                pe.wait_ge(xn_ready, b + 1)
                if b >= 2:
                    pe.wait_ge(h_full, 2 * (b - 1))
                for c in range(2):
                    for kc in range(KC):
                        ins = pe.transpose(turn[b % 2][:, kc, c * P:(c + 1) * P],
                                           xn[b % 2][:, c, kc * P:(kc + 1) * P], ident[:, :])
                ins.then_inc(xn_turned, 1)
            pe.wait_ge(w1_lo, 1)
            for n in range(2):
                pe.wait_ge(h_lo, 2 * n + 2)
                for f in range(FC):
                    t = n * FC + f
                    if t >= 2:
                        pe.wait_ge(gelu_done, t - 1)
                    for kc in range(KC):
                        ins = three(hid[t % 2][:, :], [w[:, kc, f * P:(f + 1) * P] for w in (w1h, w1l)],
                                    [m[:, kc, n * 512:(n + 1) * 512] for m in (hTh, hTl)],
                                    kc == 0, kc == KC - 1)
                    ins.then_inc(hid_done, 1)
            pe.wait_ge(w2_lo, 1)
            for c in range(CH):
                pe.wait_ge(g_lo, FC if c < CH // 2 else NTILE)
                if c >= 2:
                    pe.wait_ge(res_added, c - 1)
                for f in range(FC):
                    ins = three(res[c % 2][:, 0:D], [g[:, f, c * P:(c + 1) * P] for g in (Gh, Gl)],
                                [w[:, f, :] for w in (w2h, w2l)], f == 0, f == FC - 1)
                ins.then_inc(res_done, 1)


def grouped_projections(nc, x, ident, Qr, Kr, V, ctx_t, wq_d, wk_d, wv_d, l1p_d):
    with ExitStack() as ctx:
        def sb(name, shape, dt=F32):
            return ctx.enter_context(nc.sbuf_tensor("p_" + name, shape, dt))

        def bank(name, shape):
            return ctx.enter_context(nc.psum_tensor("p_" + name, shape, F32))

        def sem(name):
            return ctx.enter_context(nc.semaphore("p_" + name))

        VW = KVH * HD
        wq, wk, wv = sb("wq", [P, KC, F]), sb("wk", [P, KC, F]), sb("wv", [P, KC, VW])
        wqh, wql = sb("wqh", [P, KC, F], F32R), sb("wql", [P, KC, F], F32R)
        wkh, wkl = sb("wkh", [P, KC, F], F32R), sb("wkl", [P, KC, F], F32R)
        wvh, wvl = sb("wvh", [P, KC, VW], F32R), sb("wvl", [P, KC, VW], F32R)
        l1p = sb("l1p", [P, 2 * KVH + VW])
        xTh, xTl = sb("xTh", [P, KC, TOK], F32R), sb("xTl", [P, KC, TOK], F32R)
        cTh, cTl = sb("cTh", [P, KC, TOK], F32R), sb("cTl", [P, KC, TOK], F32R)
        c_in = sb("c_in", [P, KC, TOK])
        turn = [bank(f"turn{i}", [P, KC, S]) for i in range(2)]
        tile = [bank(f"tile{i}", [P, 512]) for i in range(2)]
        vbank = bank("vbank", [P, CH, VW])

        wq_in, wk_in, wv_in, l1p_in, ctx_in = (sem(n) for n in ("wq_in", "wk_in", "wv_in", "l1p_in", "ctx_in"))
        wq_scaled, bq_scaled, wq_hi, wq_lo = (sem(n) for n in ("wq_scaled", "bq_scaled", "wq_hi", "wq_lo"))
        wk_hi, wk_lo, wv_hi, wv_lo = (sem(n) for n in ("wk_hi", "wk_lo", "wv_hi", "wv_lo"))
        ctx_hi, ctx_lo = sem("ctx_hi"), sem("ctx_lo")
        turned, x_hi, x_lo = sem("turned"), sem("x_hi"), sem("x_lo")
        tile_done, tile_hi, tile_lo = sem("tile_done"), sem("tile_hi"), sem("tile_lo")
        v_done, v_out = sem("v_done"), sem("v_out")
        block = ctx.enter_context(nc.Block())
        TILES = [("k", g, n) for g in range(KVH) for n in range(2)]
        TILES += [("q", g, n) for g in range(KVH) for n in range(2)]

        @block.sync
        def _(sp):
            sp.dma_start(c_in[:, :, :], ctx_t.rearrange("(k p) t -> p k t", p=P)).then_inc(ctx_in, 16)
            sp.dma_start(wk[:, :, :], wk_d).then_inc(wk_in, 16)
            sp.dma_start(l1p[:, :], l1p_d).then_inc(l1p_in, 16)
            sp.dma_start(wv[:, :, :], wv_d).then_inc(wv_in, 16)
            sp.dma_start(wq[:, :, :], wq_d).then_inc(wq_in, 16)

        @block.gpsimd
        def _(pool):
            pool.wait_ge(l1p_in, 16)
            pool.tensor_scalar(l1p[:, 0:KVH], l1p[:, 0:KVH], HD ** -0.5, None, ALU.mult).then_inc(bq_scaled, 1)
            pool.wait_ge(wv_in, 16)
            pool.tensor_copy(wvh[:, :, :], wv[:, :, :]).then_inc(wv_hi, 1)
            pool.wait_ge(wv_hi, 1)
            pool.tensor_tensor(wvl[:, :, :], wv[:, :, :], wvh[:, :, :].bitcast(F32),
                               ALU.subtract).then_inc(wv_lo, 1)
            pool.wait_ge(wq_in, 16)
            pool.tensor_scalar(wq[:, :, :], wq[:, :, :], HD ** -0.5, None, ALU.mult).then_inc(wq_scaled, 1)
            pool.wait_ge(wq_scaled, 1)
            pool.tensor_copy(wqh[:, :, :], wq[:, :, :]).then_inc(wq_hi, 1)
            pool.wait_ge(wq_hi, 1)
            pool.tensor_tensor(wql[:, :, :], wq[:, :, :], wqh[:, :, :].bitcast(F32),
                               ALU.subtract).then_inc(wq_lo, 1)

        @block.scalar
        def _(act):
            act.wait_ge(ctx_in, 16)
            act.activation(cTh[:, :, :], c_in[:, :, :], ACT.Copy).then_inc(ctx_hi, 1)
            act.wait_ge(wk_in, 16)
            act.activation(wkh[:, :, :], wk[:, :, :], ACT.Copy).then_inc(wk_hi, 1)
            for b in range(B):
                act.wait_ge(turned, b + 1)
                act.activation(xTh[:, :, b * S:(b + 1) * S], turn[b % 2][:, :, :],
                               ACT.Copy).then_inc(x_hi, 1)
            act.wait_ge(bq_scaled, 1)
            for t, (kind, g, n) in enumerate(TILES):
                out, c = (Qr, g) if kind == "q" else (Kr, KVH + g)
                act.wait_ge(tile_done, t + 1)
                act.activation(out[:, g, n * 512:(n + 1) * 512], tile[t % 2][:, :], ACT.Identity,
                               bias=l1p[:, c:c + 1]).then_inc(tile_hi, 1)

        @block.vector
        def _(dve):
            dve.wait_ge(ctx_hi, 1)
            dve.tensor_tensor(cTl[:, :, :], c_in[:, :, :], cTh[:, :, :].bitcast(F32),
                              ALU.subtract).then_inc(ctx_lo, 1)
            dve.wait_ge(wk_hi, 1)
            dve.tensor_tensor(wkl[:, :, :], wk[:, :, :], wkh[:, :, :].bitcast(F32),
                              ALU.subtract).then_inc(wk_lo, 1)
            for b in range(B):
                dve.wait_ge(x_hi, b + 1)
                dve.tensor_tensor(xTl[:, :, b * S:(b + 1) * S], turn[b % 2][:, :, :],
                                  xTh[:, :, b * S:(b + 1) * S].bitcast(F32),
                                  ALU.subtract).then_inc(x_lo, 1)
            for t, (kind, g, n) in enumerate(TILES):
                out, c = (Qr, g) if kind == "q" else (Kr, KVH + g)
                dve.wait_ge(tile_hi, t + 1)
                for p0, p1 in ([(64, 128)] if kind == "q" else [(32, 64), (96, 128)]):
                    part = out[p0:p1, g, n * 512:(n + 1) * 512]
                    ins = dve.scalar_tensor_tensor(out=part, in0=tile[t % 2][p0:p1, :],
                                                   scalar=l1p[p0:p1, c:c + 1], in1=part.bitcast(F32),
                                                   op0=ALU.add, op1=ALU.subtract)
                ins.then_inc(tile_lo, 1)
            dve.wait_ge(v_done, 1)
            bv = l1p[:, 2 * KVH:].rearrange("p (o d) -> p o d", o=1).to_broadcast([P, CH, VW])
            dve.tensor_tensor(V[:, :, :], vbank[:, :, :], bv, ALU.add).then_inc(v_out, 1)

        @block.tensor
        def _(pe):
            def three(out, w, m, first, final):
                (w_hi, w_lo), (m_hi, m_lo) = w, m
                pe.matmul(out, w_lo, m_hi, start=first, stop=False)
                pe.matmul(out, w_hi, m_lo, start=False, stop=False)
                return pe.matmul(out, w_hi, m_hi, start=False, stop=final)

            for b in range(B):
                if b >= 2:
                    pe.wait_ge(x_lo, b - 1)
                for c in range(2):
                    for kc in range(KC):
                        ins = pe.transpose(turn[b % 2][:, kc, c * P:(c + 1) * P],
                                           x[:, 2 * b + c, kc * P:(kc + 1) * P], ident[:, :])
                ins.then_inc(turned, 1)
            pe.wait_ge(ctx_lo, 1)
            pe.wait_ge(wk_lo, 1)
            for t, (kind, g, n) in enumerate(TILES):
                if t == 2 * KVH:
                    pe.wait_ge(wq_lo, 1)
                    pe.wait_ge(x_lo, B)
                if t >= 2:
                    pe.wait_ge(tile_lo, t - 1)
                w, m = ((wqh, wql), (xTh, xTl)) if kind == "q" else ((wkh, wkl), (cTh, cTl))
                for kc in range(KC):
                    ins = three(tile[t % 2][:, :], [a[:, kc, g * P:(g + 1) * P] for a in w],
                                [a[:, kc, n * 512:(n + 1) * 512] for a in m], kc == 0, kc == KC - 1)
                ins.then_inc(tile_done, 1)
            pe.wait_ge(wv_lo, 1)
            for c in range(CH):
                for kc in range(KC):
                    ins = three(vbank[:, c, :], [a[:, kc, c * P:(c + 1) * P] for a in (cTh, cTl)],
                                [a[:, kc, :] for a in (wvh, wvl)], kc == 0, kc == KC - 1)
            ins.then_inc(v_done, 1)


SC0, MK0, PV0, PT0, OT0 = 3, 2, 2, 1, 1
NPR = 4
NV = KB * GB * 2


def grouped_attention(nc, ident, Qr, Kr, V, OT, sums, mask_d, gmask_d):
    with ExitStack() as ctx:
        def sb(name, shape, dt=F32):
            return ctx.enter_context(nc.sbuf_tensor("g_" + name, shape, dt))

        def bank(name, shape):
            return ctx.enter_context(nc.psum_tensor("g_" + name, shape, F32))

        def sem(name):
            return ctx.enter_context(nc.semaphore("g_" + name))

        Qb = [sb(f"Qb{i}", [P, GB, S], F32R) for i in range(KB)]
        KP = [sb(f"KP{i}", [P, GR, S], F32R) for i in range(2)]
        VP = [sb(f"VP{i}", [P, 2, GB, GR, GR * HD]) for i in range(KB)]
        PT = [sb(f"PT{i}", [P, GB, 2, GR, S]) for i in range(KB)]
        maskb = [sb(f"maskb{i}", [P, 2, S]) for i in range(KB)]
        prob = [sb(f"prob{i}", [P, GR, S]) for i in range(NPR)]
        nmax = sb("nmax", [P, NPR, GR])
        gmask = sb("gmask", [P, GR])
        Sb = [bank(f"Sb{i}", [P, 2, 512]) for i in range(2)]
        PTb = [bank(f"PTb{i}", [P, GR, P]) for i in range(2)]
        Ob = bank("Ob", [P, 512])

        q_in = [sem(f"q_in{i}") for i in range(KB)]
        mask_in = [sem(f"mask_in{i}") for i in range(KB)]
        gmask_in, kp_ready, vp_zero, vp_ready = sem("gmask_in"), sem("kp_ready"), sem("vp_zero"), sem("vp_ready")
        scored, masked, exp_done = sem("scored"), sem("masked"), sem("exp_done")
        turned = [sem(f"turned{i}") for i in range(2)]
        pt0_out, pt1_out, pv_done, ot_out = sem("pt0_out"), sem("pt1_out"), sem("pv_done"), sem("ot_out")
        stood = sem("stood")

        def stand(eng, semaphore, value):
            eng.wait_ge(semaphore, value)
            eng.sem_inc(stood, 1)

        def batches(eng, unit, last):
            for v in range(NV // 2):
                unit(0, v, first=True)
            with eng.Fori(0, B - 1) as b:
                for v in range(NV // 2, NV):
                    unit(b, v)
                for v in range(NV // 2):
                    unit(b + 1, v)
            for v in range(NV // 2, NV):
                unit(B - 1, v)
            last()

        def ahead(part, b, v, by):
            if v + by < NV:
                part(b, v + by, b * NV + v + by)
            elif not (isinstance(b, int) and b == B - 1):
                part(b + 1, v + by - NV, b * NV + v + by)

        block = ctx.enter_context(nc.Block())

        @block.sync
        def _(sp):
            sp.dma_start(gmask[:, :], gmask_d).then_inc(gmask_in, 16)

            def load(b, kb):
                sp.dma_start(Qb[kb][:, :, :].bitcast(F32),
                             Qr[:, kb * GB:(kb + 1) * GB, bass.ds(b * S, S)].bitcast(F32)
                             ).then_inc(q_in[kb], 16)
                sp.dma_start(maskb[kb][:, :, :], mask_d[bass.ds(b * S, S), :]
                             .rearrange("(c p) t -> p c t", p=P)).then_inc(mask_in[kb], 16)
            for kb in range(KB):
                load(0, kb)
            with sp.Fori(0, B - 1) as b:
                for kb in range(KB):
                    stand(sp, masked, b * NV + (kb + 1) * 8 + MK0)
                    load(b + 1, kb)

        @block.gpsimd
        def _(pool):
            for kb in range(KB):
                pool.memset(VP[kb][:, :, :, :, :], 0.0).then_inc(vp_zero, 1)
            pool.wait_ge(vp_zero, KB)
            pool.wait_ge(gmask_in, 16)

            def keys(b, kb, k):
                J = b * KVH + kb * GB + k
                pool.wait_ge(scored, J * 2 - 2 + SC0)
                out = KP[k % 2][:, :, :]
                rows = Kr[:, kb * GB + k, bass.ds(b * S, S)].bitcast(F32)
                rows = rows.rearrange("p (o t) -> p o t", o=1).to_broadcast([P, GR, S])
                head = gmask[:, :].rearrange("p (g o) -> p g o", o=1).to_broadcast([P, GR, S])
                pool.tensor_tensor(out, rows, head, ALU.mult).then_inc(kp_ready, 1)

            def values(b, kb):
                su = b * KB + kb
                stand(pool, pv_done, su - 1 + PV0)
                for g in range(GR):
                    src = V[:, bass.ds(b * 2, 2), kb * GB * HD:(kb + 1) * GB * HD]
                    pool.tensor_copy(VP[kb][:, :, :, g, g * HD:(g + 1) * HD],
                                     src.rearrange("p c (k d) -> p c k d", d=HD)).then_inc(vp_ready, 1)

            def batch(b):
                for kb in range(KB):
                    for k in range(GB):
                        keys(b, kb, k)
                    values(b, kb)
            with pool.Fori(0, B) as b:
                batch(b)

        @block.scalar
        def _(act):
            act.sem_inc(pt0_out, PT0)

            def exps(b, v, N):
                kb, k, c = v // 8, v % 8 // 2, v % 2
                act.wait_ge(masked, N + 1 + MK0)
                for g in range(GR):
                    h = (kb * GB + k) * GR + g
                    ins = act.activation(prob[v % NPR][:, g, :], prob[v % NPR][:, g, :], ACT.Exp,
                                         scale=-1.0, bias=nmax[:, v % NPR, g:g + 1],
                                         accum_out=sums[:, bass.ds(b * 2 + c, 1), h])
                ins.then_inc(exp_done, 1)

            def unit(b, v, first=False):
                N, kb, k, c = b * NV + v, v // 8, v % 8 // 2, v % 2
                if first and v == 0:
                    exps(b, v, N)
                ahead(exps, b, v, 1)
                act.wait_ge(turned[0], N + 1)
                act.wait_ge(pv_done, b * KB + kb - 1 + PV0)
                act.activation(PT[kb][:, k, 0, :, c * P:(c + 1) * P], PTb[0][:, :, :],
                               ACT.Copy).then_inc(pt0_out, 1)
            batches(act, unit, lambda: None)

        @block.vector
        def _(dve):
            dve.sem_inc(masked, MK0)
            dve.sem_inc(pt1_out, PT0)
            dve.sem_inc(ot_out, OT0)

            def mask_and_max(b, v, N):
                kb, c = v // 8, v % 2
                if v % 8 == 0:
                    dve.wait_ge(mask_in[kb], b * 16 + 16)
                stand(dve, scored, N + 1 + SC0)
                for g in range(GR):
                    ins = dve.tensor_tensor_reduce(
                        out=prob[v % NPR][:, g, :], in0=Sb[v % 2][:, g // 2, (g % 2) * S:(g % 2 + 1) * S],
                        in1=maskb[kb][:, c, :], scale=-1.0, scalar=BIG, op0=ALU.add, op1=ALU.min,
                        accum_out=nmax[:, v % NPR, g:g + 1])
                ins.then_inc(masked, 1)

            def out_block(su, kb, b):
                dve.wait_ge(pv_done, su + 1 + PV0)
                dve.tensor_copy(OT[:, kb, bass.ds(b * S, S)], Ob[:, 0:S]).then_inc(ot_out, 1)

            def unit(b, v, first=False):
                N, kb, k, c = b * NV + v, v // 8, v % 8 // 2, v % 2
                if first and v == 0:
                    mask_and_max(b, 0, N)
                    mask_and_max(b, 1, N + 1)
                ahead(mask_and_max, b, v, 2)
                dve.wait_ge(turned[1], N + 1)
                dve.wait_ge(pv_done, b * KB + kb - 1 + PV0)
                dve.tensor_copy(PT[kb][:, k, 1, :, c * P:(c + 1) * P], PTb[1][:, :, :]).then_inc(pt1_out, 1)
                if v % 8 == 7 and not first:
                    out_block(b * KB + kb - 1, 1 - kb, b - 1 if kb == 0 else b)
            batches(dve, unit, lambda: out_block(B * KB - 1, 1, B - 1))

        @block.tensor
        def _(pe):
            pe.sem_inc(scored, SC0)
            pe.sem_inc(pv_done, PV0)

            def scores(b, v, N):
                kb, k, c = v // 8, v % 8 // 2, v % 2
                if v % 8 == 0:
                    pe.wait_ge(q_in[kb], b * 16 + 16)
                if c == 0:
                    pe.wait_ge(kp_ready, b * KVH + kb * GB + k + 1)
                pe.wait_ge(masked, N - 1 + MK0)
                for half in range(2):
                    ins = pe.matmul(Sb[v % 2][:, half, :], Qb[kb][:, k, c * P:(c + 1) * P],
                                    KP[k % 2][:, 2 * half:2 * half + 2, :].rearrange("p g t -> p (g t)"),
                                    start=True, stop=True)
                ins.then_inc(scored, 1)

            def turn(v, N, tc):
                pe.wait_ge((pt0_out, pt1_out)[tc], N + PT0)
                for g in range(GR):
                    ins = pe.transpose(PTb[tc][:, g, :], prob[v % NPR][:, g, tc * P:(tc + 1) * P],
                                       ident[:, :])
                ins.then_inc(turned[tc], 1)

            def sum_values(su, kb, steps):
                if steps[0] == 0:
                    pe.wait_ge(pt0_out, su * 8 + 8 + PT0)
                    pe.wait_ge(pt1_out, su * 8 + 8 + PT0)
                    pe.wait_ge(vp_ready, su * GR + GR)
                    pe.wait_ge(ot_out, su + OT0)
                for i in steps:
                    tc, g = i // GR, i % GR
                    for k in range(GB):
                        ins = pe.matmul(Ob[32 * k:32 * k + 32, 0:S], VP[kb][:, tc, k, g, :],
                                        PT[kb][:, k, tc, g, :], start=(i == 0), stop=(i == 2 * GR - 1))
                if steps[-1] == 2 * GR - 1:
                    ins.then_inc(pv_done, 1)

            def unit(b, v, first=False):
                N, kb = b * NV + v, v // 8
                if first and v == 0:
                    scores(b, 0, N)
                    scores(b, 1, N + 1)
                ahead(scores, b, v, 2)
                pe.wait_ge(exp_done, N + 1)
                turn(v, N, 0)
                turn(v, N, 1)
                if v % 8 >= 1 and not first:
                    sum_values(b * KB + kb - 1, 1 - kb, [v % 8 - 1] if v % 8 < 7 else [6, 7])
            batches(pe, unit, lambda: sum_values(B * KB - 1, 1, list(range(2 * GR))))


def closing(nc, x, ident, OT, sums, wo_d, lastp_d, out):
    with ExitStack() as ctx:
        def sb(name, shape, dt=F32):
            return ctx.enter_context(nc.sbuf_tensor("c_" + name, shape, dt))

        def bank(name, shape):
            return ctx.enter_context(nc.psum_tensor("c_" + name, shape, F32))

        def sem(name):
            return ctx.enter_context(nc.semaphore("c_" + name))

        wo, lastp = sb("wo", [P, KB, D]), sb("lastp", [P, 3, D])
        woh, wol = sb("woh", [P, KB, D], F32R), sb("wol", [P, KB, D], F32R)
        rsum = sb("rsum", [P, CH, KVH * GR])
        On = [sb(f"On{i}", [P, D]) for i in range(2)]
        Oh, Ol = sb("Oh", [P, KB, TOK], F32R), sb("Ol", [P, KB, TOK], F32R)
        stats, mv, rstd = sb("stats", [P, CH, 6]), sb("mv", [P, CH, 2]), sb("rstd", [P, CH])
        minus_half = sb("minus_half", [P, CH])
        y = sb("y", [P, CH, D])
        nat = [bank(f"nat{i}", [P, D]) for i in range(2)]
        back = [bank(f"back{i}", [P, KB, P]) for i in range(2)]
        res = [bank(f"res{i}", [P, 512]) for i in range(2)]

        wo_in, lastp_in, wo_hi, wo_lo = sem("wo_in"), sem("lastp_in"), sem("wo_hi"), sem("wo_lo")
        rsum_done, natural, normed, turned = sem("rsum_done"), sem("natural"), sem("normed"), sem("turned")
        o_hi, o_lo, res_done, res_added = sem("o_hi"), sem("o_lo"), sem("res_done"), sem("res_added")
        bo_added, stat_done, aggr_done = sem("bo_added"), sem("stat_done"), sem("aggr_done")
        rstd_step, rstd_ready = sem("rstd_step"), sem("rstd_ready")
        centered, scaled, stored = sem("centered"), sem("scaled"), sem("stored")
        shifted = sem("shifted")
        block = ctx.enter_context(nc.Block())

        @block.sync
        def _(sp):
            sp.dma_start(wo[:, :, :], wo_d).then_inc(wo_in, 16)
            sp.dma_start(lastp[:, :, :], lastp_d).then_inc(lastp_in, 16)
            for half in range(2):
                sp.wait_ge(shifted, (half + 1) * CH // 2)
                sp.dma_start(out.rearrange("(c p) d -> p c d", p=P)[:, half * 4:half * 4 + 4, :],
                             y[:, half * 4:half * 4 + 4, :]).then_inc(stored, 16)
            sp.wait_ge(stored, 32)

        @block.gpsimd
        def _(pool):
            pool.memset(minus_half[:, :], -0.5).then_inc(rstd_step, 1)
            pool.wait_ge(wo_in, 16)
            pool.tensor_copy(woh[:, :, :], wo[:, :, :]).then_inc(wo_hi, 1)
            pool.wait_ge(wo_hi, 1)
            pool.tensor_tensor(wol[:, :, :], wo[:, :, :], woh[:, :, :].bitcast(F32),
                               ALU.subtract).then_inc(wo_lo, 1)
            pool.wait_ge(lastp_in, 16)
            bo = lastp[:, 0:1, :].to_broadcast([P, CH, D])
            pool.tensor_tensor(x[:, :, :], x[:, :, :], bo, ALU.add).then_inc(bo_added, 1)
            for half in range(2):
                cs = slice(half * 4, half * 4 + 4)
                pool.wait_ge(aggr_done, half * 4 + 4)
                pool.tensor_scalar(rstd[:, cs], mv[:, cs, 1], L1_EPS, None, ALU.add).then_inc(rstd_step, 1)
                pool.wait_ge(rstd_step, half + 2)
                pool.tensor_tensor(rstd[:, cs], rstd[:, cs], minus_half[:, cs],
                                   ALU.pow).then_inc(rstd_ready, 1)
            for c in range(CH):
                pool.wait_ge(scaled, c + 1)
                pool.tensor_tensor(y[:, c, :], y[:, c, :], lastp[:, 2, :], ALU.add).then_inc(shifted, 1)

        @block.scalar
        def _(act):
            for c in range(CH):
                act.wait_ge(turned, c + 1)
                act.activation(Oh[:, :, c * P:(c + 1) * P], back[c % 2][:, :, :],
                               ACT.Copy).then_inc(o_hi, 1)

        @block.vector
        def _(dve):
            dve.reciprocal(rsum[:, :, :], sums[:, :, :]).then_inc(rsum_done, 1)
            dve.wait_ge(rsum_done, 1)

            def normalize(c):
                dve.wait_ge(natural, c + 1)
                if c >= 2:
                    dve.wait_ge(turned, c - 1)
                r = rsum[:, c, :].rearrange("p (h o) -> p h o", o=1).to_broadcast([P, KVH * GR, HD])
                dve.tensor_tensor(On[c % 2][:, :].rearrange("p (h d) -> p h d", d=HD),
                                  nat[c % 2][:, :].rearrange("p (h d) -> p h d", d=HD), r,
                                  ALU.mult).then_inc(normed, 1)

            def add(c):
                if c == 0:
                    dve.wait_ge(bo_added, 1)
                dve.wait_ge(res_done, c + 1)
                dve.tensor_tensor(x[:, c, :], res[c % 2][:, 0:D], x[:, c, :], ALU.add).then_inc(res_added, 1)
                dve.wait_ge(res_added, c + 1)
                dve.bn_stats(stats[:, c, :], x[:, c, :]).then_inc(stat_done, 1)
                dve.wait_ge(stat_done, c + 1)
                dve.bn_aggr(mv[:, c, :], stats[:, c, :]).then_inc(aggr_done, 1)

            normalize(0)
            for c in range(CH):
                if c + 1 < CH:
                    normalize(c + 1)
                dve.wait_ge(o_hi, c + 1)
                dve.tensor_tensor(Ol[:, :, c * P:(c + 1) * P], back[c % 2][:, :, :],
                                  Oh[:, :, c * P:(c + 1) * P].bitcast(F32), ALU.subtract).then_inc(o_lo, 1)
                if c >= 1:
                    add(c - 1)
            add(CH - 1)
            dve.wait_ge(lastp_in, 16)
            for c in range(CH):
                dve.wait_ge(rstd_ready, c // 4 + 1)
                dve.tensor_scalar(y[:, c, :], x[:, c, :], mv[:, c, 0:1], rstd[:, c:c + 1],
                                  ALU.subtract, ALU.mult).then_inc(centered, 1)
                dve.wait_ge(centered, c + 1)
                dve.tensor_tensor(y[:, c, :], y[:, c, :], lastp[:, 1, :], ALU.mult).then_inc(scaled, 1)

        @block.tensor
        def _(pe):
            def natural_chunk(c):
                if c >= 2:
                    pe.wait_ge(normed, c - 1)
                for kb in range(KB):
                    ins = pe.transpose(nat[c % 2][:, kb * P:(kb + 1) * P], OT[:, kb, c * P:(c + 1) * P],
                                       ident[:, :])
                ins.then_inc(natural, 1)

            def out_chunk(c):
                pe.wait_ge(o_lo, c + 1)
                if c >= 2:
                    pe.wait_ge(res_added, c - 1)
                n = 0
                for kb in range(KB):
                    for a, w in ((Ol, woh), (Oh, wol), (Oh, woh)):
                        n += 1
                        ins = pe.matmul(res[c % 2][:, 0:D], a[:, kb, c * P:(c + 1) * P], w[:, kb, :],
                                        start=(n == 1), stop=(n == 6))
                ins.then_inc(res_done, 1)

            natural_chunk(0)
            for c in range(CH):
                if c + 1 < CH:
                    natural_chunk(c + 1)
                pe.wait_ge(normed, c + 1)
                if c >= 2:
                    pe.wait_ge(o_lo, c - 1)
                for kb in range(KB):
                    ins = pe.transpose(back[c % 2][:, kb, :], On[c % 2][:, kb * P:(kb + 1) * P], ident[:, :])
                ins.then_inc(turned, 1)
                if c == 1:
                    pe.wait_ge(wo_lo, 1)
                if c >= 1:
                    out_chunk(c - 1)
            out_chunk(CH - 1)


def build(nc, x_d, ident_d, ctx_t, packs_a, packs_b, params, w1_d, w2_d, mlpp_d, wq_d, wk_d, wv_d,
          l1p_d, mask_d, gmask_d, wo_d, lastp_d, out):
    with ExitStack() as ctx:
        def sb(name, shape, dt=F32):
            return ctx.enter_context(nc.sbuf_tensor(name, shape, dt))

        x = sb("x", [P, CH, D])
        ident = sb("ident", [P, P])
        cross_attentions(nc, x, ident, x_d, ident_d, ctx_t, packs_a, packs_b, params)
        feed_forward(nc, x, ident, w1_d, w2_d, mlpp_d)
        OT, sums = sb("OT", [P, KB, TOK]), sb("row_sums", [P, CH, KVH * GR])
        with ExitStack() as inner:
            Qr = inner.enter_context(nc.sbuf_tensor("Qr", [P, KVH, TOK], F32R))
            Kr = inner.enter_context(nc.sbuf_tensor("Kr", [P, KVH, TOK], F32R))
            V = inner.enter_context(nc.sbuf_tensor("V", [P, CH, KVH * HD], F32))
            grouped_projections(nc, x, ident, Qr, Kr, V, ctx_t, wq_d, wk_d, wv_d, l1p_d)
            grouped_attention(nc, ident, Qr, Kr, V, OT, sums, mask_d, gmask_d)
        closing(nc, x, ident, OT, sums, wo_d, lastp_d, out)


def kernel(**inputs):
    import numpy as np
    import concourse.bacc as bacc
    from concourse.bass_utils import run_bass_kernel_spmd as run

    def f(name):
        return np.ascontiguousarray(inputs[name])

    def feature_major(w):
        return w.reshape(KC, P, -1).transpose(1, 0, 2)

    def rows(v):
        return np.broadcast_to(v.reshape(1, -1), (P, v.size))

    def queries(w):
        w = w.reshape(-1, KVH, 1, GR * HD)
        return np.broadcast_to(w, (w.shape[0], KVH, REP, GR * HD)).reshape(w.shape[0], -1)

    def keys(w):
        w = w.reshape(-1, KVH, 1, HD)
        return np.broadcast_to(w, (w.shape[0], KVH, REP * GR, HD)).reshape(w.shape[0], -1)

    packs_a, packs_b, params = [], [], []
    for i in (1, 2):
        L = "L0_xattn_"
        for g in range(NG):
            cols, heads = slice(g * GC, (g + 1) * GC), slice(g * HG, (g + 1) * HG)
            parts = [feature_major(f(f"{L}w{n}{i}")[:, cols]).reshape(P, -1) for n in "qkv"]
            parts += [f(f"{L}b{n}{i}").reshape(H, K)[heads].T for n in "qk"]
            parts += [f(f"{L}bias_k{i}").reshape(H, K)[heads].T]
            parts += [rows(f(f"{L}bv{i}")[cols]), rows(f(f"{L}bias_v{i}").reshape(-1)[cols])]
            packs_a.append(np.concatenate(parts, 1))
            wo = f(f"{L}wo{i}").reshape(H, K, D)[heads].transpose(1, 0, 2).reshape(P, -1)
            packs_b.append(np.concatenate([wo, f(f"{L}bias_v{i}").reshape(H, K)[heads].T], 1))
        params.append(np.concatenate([f(f"{L}ln{i}_scale").reshape(KC, P).T,
                                      f(f"{L}ln{i}_offset").reshape(KC, P).T,
                                      rows(f(f"{L}bo{i}"))], 1))
    arrays = {
        "x": f("x").reshape(TOK, D),
        "ident": np.eye(P, dtype=np.float32),
        "ctx_t": np.ascontiguousarray(f("ctx_2048").reshape(TOK, D).T),
        "packs_a": np.stack(packs_a + packs_a[:2]),
        "packs_b": np.stack(packs_b + packs_b[:1]),
        "params": np.stack(params + params[:1]),
        "w1": feature_major(f("L0_xattn_w_fc1")),
        "w2": f("L0_xattn_w_fc2").reshape(FC, P, D).transpose(1, 0, 2),
        "mlpp": np.concatenate([f("L0_xattn_ln_mlp_scale").reshape(KC, P).T,
                                f("L0_xattn_ln_mlp_offset").reshape(KC, P).T,
                                f("L0_xattn_b_fc1").reshape(FC, P).T, rows(f("L0_xattn_b_fc2"))], 1),
        "wq": feature_major(queries(f("L1_xattn_Wq"))),
        "wk": feature_major(keys(f("L1_xattn_Wk"))),
        "wv": feature_major(f("L1_xattn_Wv")),
        "l1p": np.concatenate([queries(f("L1_xattn_bq")).reshape(KVH, P).T,
                               keys(f("L1_xattn_bk")).reshape(KVH, P).T, rows(f("L1_xattn_bv"))], 1),
        "mask": f("mask_Bx1xSxS2_ff0").reshape(TOK, S),
        "gmask": (np.arange(P)[:, None] // HD % GR == np.arange(GR)).astype(np.float32),
        "wo": f("L1_xattn_Wo").reshape(KB, P, D).transpose(1, 0, 2),
        "lastp": np.stack([rows(f(f"L1_xattn_{n}")) for n in ("bo", "gamma", "beta")], 1),
    }
    arrays = {n: np.ascontiguousarray(a) for n, a in arrays.items()}
    nc = bacc.Bacc("TRN2", target_bir_lowering=False, num_devices=1)
    args = [nc.dram_tensor(n + "_dram", a.shape, F32, kind="ExternalInput").ap() for n, a in arrays.items()]
    out = nc.dram_tensor("out_dram", (TOK, D), F32, kind="ExternalOutput").ap()
    build(nc, *args, out)
    r = run(nc, [{n + "_dram": a for n, a in arrays.items()}], core_ids=[0])
    return r.results[0]["out_dram"].reshape(B, S, D)
```

```python
from contextlib import ExitStack

import concourse.bass as bass
from concourse import mybir

F32 = mybir.dt.float32
F32R = mybir.dt.float32r
ALU = mybir.AluOpType
ACT = mybir.ActivationFunctionType
AX = mybir.AxisListType

P = 128
B, S, D = 4, 256, 256
TOK = B * S
CH = TOK // P
KC = D // P
LN_EPS = 1e-5

H, K = 16, 128
ATT = 2
HG = 2
NG = H // HG
UN = HG * B
GC = HG * K
TP = S + 2
NQKV = 3 * KC * GC
NWO = HG * D
C_BQ = NQKV
C_KB = NQKV + 2 * HG
C_BV = NQKV + 3 * HG
C_VB = C_BV + GC
NPA = C_VB + GC
NPB = NWO + HG
NPAR = 2 * KC + D

F = 1024
FC = F // P

KVH, GR, HD = 8, 4, 8
KB = 2
GB = KVH // KB
REP = P // (GR * HD)
L1_EPS = 1e-6
BIG = 3.0e38

EXP0 = 4
TR0 = 2
VLO0 = 2
TURN0 = 2
FULL0 = 3
HLO0 = 2
SCORE0 = 1
PTLO0 = 1
OLO0 = 1


KT, QT, VT = range(0, 4), range(4, 8), range(8, 12)


def slots(u, first=False, last=False):
    t = 3 * (u // 2)
    if u % 2:
        a = None if first and u == 1 else ("wo", (u // 2 - 1) % B)
        b = ("proj", t + 2)
    else:
        a, b = ("proj", t), ("proj", t + 1)
    if last:
        a, b = (x if x is None or x[0] == "wo" else ("proj", VT[x[1]]) if x[1] < 4 else None
                for x in (a, b))
    return a, b


PRO = len(KT) + len(QT)
USE0 = len(VT) + PRO - 1


def use(G, u, where, first=False, last=False):
    if last:
        n = sum(x is not None for v in range(u) for x in slots(v, last=True))
        n += where * (slots(u, last=True)[0] is not None)
    else:
        n = 2 * u + where + (1 if first and u == 0 else 0)
    return G * 2 * UN + USE0 + n


def prologue_use(G, j):
    return G * 2 * UN + len(VT) + j


def last_use(G):
    return use(G, UN, 0, last=True)


def output_use(G, b, last):
    return use(G, 2 * b - 1, 0, last=last) if b else G * 2 * UN + USE0 - 2


def cross_attentions(nc, x, ident, cTh, cTl, mv, rstd, mlpp, x_d, ident_d, ctx_t, packs_a, packs_b,
                     params, mlpp_d):
    with ExitStack() as ctx:
        def sb(name, shape, dt=F32):
            return ctx.enter_context(nc.sbuf_tensor(name, shape, dt))

        def sb2(name, shape, dt=F32):
            return [sb(f"{name}{i}", shape, dt) for i in range(2)]

        def bank(name, shape):
            return ctx.enter_context(nc.psum_tensor(name, shape, F32))

        def sem(name):
            return ctx.enter_context(nc.semaphore(name))

        hTh, hTl = sb("hTh", [P, KC, TOK], F32R), sb("hTl", [P, KC, TOK], F32R)
        pack_a, pack_b = sb("pack_a", [P, NPA]), sb("pack_b", [P, NPB])
        wh, wl = sb2("wh", [P, NQKV], F32R), sb2("wl", [P, NQKV], F32R)
        woh, wol = sb2("woh", [P, NWO], F32R), sb2("wol", [P, NWO], F32R)
        bcol, vrow, ocol = sb2("bcol", [P, 3 * HG]), sb2("vrow", [P, GC]), sb2("ocol", [P, HG])
        Qh, Ql = sb2("Qh", [P, HG, TOK], F32R), sb2("Ql", [P, HG, TOK], F32R)
        Kh, Kl = sb2("Kh", [P, HG, B, TP], F32R), sb2("Kl", [P, HG, B, TP], F32R)
        Vh, Vl = sb2("Vh", [P, CH, GC], F32R), sb2("Vl", [P, CH, GC], F32R)
        Oh, Ol = sb2("Oh", [P, HG, S], F32R), sb2("Ol", [P, HG, S], F32R)
        prob = sb2("prob", [P, 2, TP])
        PTh, PTl = sb2("PTh", [P, 2, S], F32R), sb2("PTl", [P, 2, S], F32R)
        work = sb2("work", [P, 2, D])
        attp = sb("attp", [P, NPAR])
        minus_half = sb("minus_half", [P, CH])
        nmax, sums, rsum = sb("nmax", [P, 2, 2]), sb("sums", [P, 2, 2]), sb("rsum", [P, 2, 2])
        stats = sb("stats", [P, CH, 6])

        Sb = [bank(f"Sb{i}", [P, 2, 512]) for i in range(2)]
        PTb = bank("PTb", [P, 2, S])
        Ob = bank("Ob", [P, 512])
        slot_bank = [bank("Ab", [P, 2, D]), bank("Bb", [P, 2, D])]

        x_in, ident_in = sem("x_in"), sem("ident_in")
        ctx_in = [sem(f"ctx_in{i}") for i in range(B)]
        ctx_hi, ctx_split = sem("ctx_hi"), sem("ctx_split")
        pack_a_in, pack_b_in = sem("pack_a_in"), sem("pack_b_in")
        v0_in, kq0_in, w0_hi, w0_lo, bias0_step = (
            sem(n) for n in ("v0_in", "kq0_in", "w0_hi", "w0_lo", "bias0_step"))
        qkv_ready, wo_ready, pool_step = sem("qkv_ready"), sem("wo_ready"), sem("pool_step")
        stood, rstd_step, rstd_ready = sem("stood"), sem("rstd_step"), sem("rstd_ready")
        attp_in, bo_added, mlpp_in = sem("attp_in"), sem("bo_added"), sem("mlpp_in")
        ln_step, xn_ready, xn_turned = sem("ln_step"), sem("xn_ready"), sem("xn_turned")
        h_full, h_hi, h_lo = sem("h_full"), sem("h_hi"), sem("h_lo")
        slot_done, proj_hi, drained = sem("slot_done"), sem("proj_hi"), sem("drained")
        v_hi, v_lo = sem("v_hi"), sem("v_lo")
        wo_step, kb_step, kb_ready = sem("wo_step"), sem("kb_step"), sem("kb_ready")
        scored, max_done, exp_done = sem("scored"), sem("max_done"), sem("exp_done")
        rsum_done, normed, transposed = sem("rsum_done"), sem("normed"), sem("transposed")
        pt_hi, pt_lo = sem("pt_hi"), sem("pt_lo")
        pv_done, o_hi, o_lo = sem("pv_done"), sem("o_hi"), sem("o_lo")

        def stand(eng, semaphore, value):
            eng.wait_ge(semaphore, value)
            eng.sem_inc(stood, 1)

        def wcol(w, which, kc, hh=None):
            c = (which * KC + kc) * GC
            return w[:, c:c + GC] if hh is None else w[:, c + hh * K:c + (hh + 1) * K]

        def kq_tile(t, i, keys, queries):
            hh, half = t % 2, t % 4 // 2
            if t in QT:
                out = queries[i][:, hh, half * 512:(half + 1) * 512]
                return hh, half, 0, out.rearrange("p (c t) -> p c t", c=2)
            return hh, half, 1, keys[i][:, hh, 2 * half:2 * half + 2, 0:S]

        def tok(b, c=0, n=S):
            return slice(b * S + c, b * S + c + n)

        ctx_at = [work[0], work[1], prob[0], prob[1]]

        def att_loop(eng, prologue, unit, epilogue):
            with eng.Fori(0, ATT) as a:
                G0 = a * NG
                prologue(a, G0)
                for u in range(2):
                    unit(a, G0, 0, u, first=True)
                with eng.Fori(0, NG // 2 - 1) as j:
                    for p in range(2):
                        G = G0 + j * 2 + p
                        for u in range(2, UN):
                            unit(a, G, p, u)
                        for u in range(2):
                            unit(a, G + 1, 1 - p, u)
                for u in range(2, UN):
                    unit(a, G0 + NG - 2, 0, u)
                for u in range(UN):
                    unit(a, G0 + NG - 1, 1, u, last=True)
                epilogue(a, G0 + NG - 1)

        def b_before(G, p, u, first, last):
            if u == 0 and first:
                return None
            v, Gv, pv = (UN - 1, G - 1, 1 - p) if u == 0 else (u - 1, G, p)
            at_last = last and u > 0
            b = slots(v, first, at_last)[1]
            return b and (b[1], Gv + 1, 1 - pv, use(Gv, v, 1, first, at_last))

        block = ctx.enter_context(nc.Block())

        @block.sync
        def _(sp):
            v0 = 2 * KC * GC
            sp.dma_start(pack_a[:, v0:], packs_a[0][:, v0:]).then_inc(v0_in, 16)

            def load_ctx(b):
                sp.dma_start(ctx_at[b][:, :, 0:S],
                             ctx_t[:, tok(b)].rearrange("(k p) t -> p k t", p=P)).then_inc(ctx_in[b], 16)
            load_ctx(0)
            load_ctx(1)
            sp.dma_start(x[:, :, :], x_d.rearrange("(c p) d -> p c d", p=P)).then_inc(x_in, 16)
            load_ctx(2)
            load_ctx(3)
            sp.dma_start(pack_a[:, 0:v0], packs_a[0][:, 0:v0]).then_inc(kq0_in, 16)
            sp.dma_start(ident[:, :], ident_d).then_inc(ident_in, 16)
            sp.dma_start(attp[:, :], params[0]).then_inc(attp_in, 16)
            sp.dma_start(pack_b[:, :], packs_b[0]).then_inc(pack_b_in, 16)
            sp.dma_start(mlpp[:, :], mlpp_d).then_inc(mlpp_in, 16)
            sp.wait_ge(w0_lo, 3)
            sp.wait_ge(bias0_step, 3)
            sp.dma_start(pack_a[:, :], packs_a[1]).then_inc(pack_a_in, 16)
            with sp.Fori(0, ATT) as a:
                with sp.Fori(0, NG) as g:
                    sp.wait_ge(wo_ready, a * NG + g + 1)
                    sp.dma_start(pack_b[:, :], packs_b[bass.ds(a * NG + g + 1, 1), :, :]
                                 .rearrange("g p c -> (g p) c")).then_inc(pack_b_in, 16)
                    sp.wait_ge(qkv_ready, a * NG + g + 1)
                    sp.dma_start(pack_a[:, :], packs_a[bass.ds(a * NG + g + 2, 1), :, :]
                                 .rearrange("g p c -> (g p) c")).then_inc(pack_a_in, 16)
                sp.wait_ge(bo_added, a + 1)
                sp.wait_ge(h_lo, HLO0 + a * B + B)
                sp.dma_start(attp[:, :], params[bass.ds(a + 1, 1), :, :]
                             .rearrange("a p c -> (a p) c")).then_inc(attp_in, 16)
            sp.wait_ge(mlpp_in, 16)
            sp.wait_ge(pack_a_in, 16 * (ATT * NG + 1))
            sp.wait_ge(pack_b_in, 16 * (ATT * NG + 1))
            sp.wait_ge(attp_in, 16 * (ATT + 1))

        @block.gpsimd
        def _(pool):
            pool.sem_inc(v_lo, VLO0)
            pool.memset(minus_half[:, :], -0.5).then_inc(rstd_step, 1)

            def split_qkv(G, i):
                done = (G - 1) * 5
                stand(pool, pack_a_in, G * 16)
                q, bq = pack_a[:, 0:KC * GC], pack_a[:, C_BQ:C_BQ + HG]
                pool.tensor_scalar(q, q, K ** -0.5, None, ALU.mult).then_inc(pool_step, 1)
                pool.tensor_scalar(bq, bq, K ** -0.5, None, ALU.mult).then_inc(pool_step, 1)
                stand(pool, pool_step, done + 2)
                pool.tensor_copy(wh[i][:, :], pack_a[:, 0:NQKV]).then_inc(pool_step, 1)
                pool.tensor_copy(bcol[i][:, :], pack_a[:, C_BQ:C_BQ + 3 * HG]).then_inc(pool_step, 1)
                pool.tensor_tensor(vrow[i][:, :], pack_a[:, C_BV:C_BV + GC], pack_a[:, C_VB:C_VB + GC],
                                   ALU.subtract).then_inc(pool_step, 1)
                pool.wait_ge(pool_step, done + 5)
                pool.tensor_tensor(wl[i][:, :], pack_a[:, 0:NQKV], wh[i][:, :].bitcast(F32),
                                   ALU.subtract).then_inc(qkv_ready, 1)

            def split_wo(G, i):
                stand(pool, pack_b_in, G * 16 + 16)
                pool.tensor_copy(woh[i][:, :], pack_b[:, 0:NWO]).then_inc(wo_step, 1)
                pool.tensor_copy(ocol[i][:, :], pack_b[:, NWO:NWO + HG]).then_inc(wo_step, 1)
                pool.wait_ge(wo_step, G * 2 + 2)
                pool.tensor_tensor(wol[i][:, :], pack_b[:, 0:NWO], woh[i][:, :].bitcast(F32),
                                   ALU.subtract).then_inc(wo_ready, 1)

            def learned_key(G, i):
                col = bcol[i][:, 2 * HG:3 * HG].rearrange("p (h o t) -> p h o t", o=1, t=1)
                col = col.to_broadcast([P, HG, B, 2])
                hi, lo = Kh[i][:, :, :, S:TP], Kl[i][:, :, :, S:TP]
                pool.tensor_copy(hi, col).then_inc(kb_step, 1)
                pool.wait_ge(kb_step, G + 1)
                pool.tensor_tensor(lo, col, hi.bitcast(F32), ALU.subtract).then_inc(kb_ready, 1)

            def value_lo(G, i, b):
                pool.wait_ge(v_hi, G * B + b + 1)
                pool.tensor_tensor(Vl[i][:, 2 * b:2 * b + 2, :], work[b % 2][:, :, :],
                                   Vh[i][:, 2 * b:2 * b + 2, :].bitcast(F32),
                                   ALU.subtract).then_inc(v_lo, 1)

            pool.wait_ge(v0_in, 16)
            pool.tensor_tensor(vrow[0][:, :], pack_a[:, C_BV:C_BV + GC], pack_a[:, C_VB:C_VB + GC],
                               ALU.subtract).then_inc(bias0_step, 1)
            bq = pack_a[:, C_BQ:C_BQ + HG]
            pool.tensor_scalar(bq, bq, K ** -0.5, None, ALU.mult).then_inc(bias0_step, 1)
            pool.wait_ge(bias0_step, 2)
            pool.tensor_copy(bcol[0][:, :], pack_a[:, C_BQ:C_BQ + 3 * HG]).then_inc(bias0_step, 1)
            pool.wait_ge(bias0_step, 3)
            learned_key(0, 0)
            for b in range(B):
                value_lo(0, 0, b)

            def deviations(k):
                stand(pool, ln_step, k * 2 * CH + 2 * CH)
                pool.tensor_scalar(rstd[:, :], mv[:, :, 1], LN_EPS, None,
                                   ALU.add).then_inc(rstd_step, 1)
                pool.wait_ge(rstd_step, k + 2)
                pool.tensor_tensor(rstd[:, :], rstd[:, :], minus_half[:, :],
                                   ALU.pow).then_inc(rstd_ready, 1)
            deviations(0)
            split_qkv(1, 1)
            split_wo(0, 0)

            def prologue(a, G):
                pool.wait_ge(xn_ready, a * B + B)
                pool.wait_ge(attp_in, a * 16 + 16)
                bo = attp[:, 2 * KC:NPAR].rearrange("p (o d) -> p o d", o=1).to_broadcast([P, CH, D])
                pool.tensor_tensor(x[:, :, :], x[:, :, :], bo, ALU.add).then_inc(bo_added, 1)

            def unit(a, G, p, u, first=False, last=False):
                if u == 0:
                    stand(pool, scored, G * UN + SCORE0)
                    learned_key(G + 1, 1 - p)
                if u == (3 if last else 0):
                    pool.wait_ge(drained, use(G, 0, 0, first=first))
                    split_qkv(G + 2, p)
                if u == 2:
                    pool.wait_ge(slot_done, use(G, 1, 0) + 1)
                    split_wo(G + 1, 1 - p)
                for item in slots(u, first, last):
                    if item and item[0] == "proj" and item[1] in VT:
                        value_lo(G + 1, 1 - p, item[1] - VT[0])

            att_loop(pool, prologue, unit, lambda a, G: deviations(a + 1))

        @block.scalar
        def _(act):
            act.sem_inc(exp_done, EXP0)
            act.sem_inc(h_full, FULL0)

            def ctx_part(b):
                act.wait_ge(ctx_in[b], 16)
                act.activation(cTh[:, :, tok(b)], ctx_at[b][:, :, 0:S], ACT.Copy).then_inc(ctx_hi, 1)

            def project_hi(G, i, t, where, n):
                hh, half, which, out = kq_tile(t, i, Kh, Qh)
                act.wait_ge(slot_done, n + 1)
                c = hh + which * HG
                act.activation(out, slot_bank[where][:, :, :], ACT.Identity,
                               bias=bcol[i][:, c:c + 1]).then_inc(proj_hi, 1)

            def value_hi(G, i, b, n):
                act.wait_ge(drained, n + 1)
                act.activation(Vh[i][:, 2 * b:2 * b + 2, :], work[b % 2][:, :, :],
                               ACT.Copy).then_inc(v_hi, 1)

            def exps(U, r):
                for c in range(2):
                    act.wait_ge(max_done, U + 1)
                    act.wait_ge(transposed, U - 1 + TR0)
                    act.activation(prob[r][:, c, 0:S + 1], Sb[r][:, c, 0:S + 1], ACT.Exp,
                                   bias=nmax[:, r, c:c + 1],
                                   accum_out=sums[:, r, c:c + 1]).then_inc(exp_done, 1)

            def output_hi(G, p, u, last):
                b, hh = u // HG, u % HG
                if hh == 0:
                    act.wait_ge(slot_done, output_use(G, b, last) + 1)
                if u == 0:
                    act.wait_ge(wo_ready, G + 1)
                act.wait_ge(pv_done, G * UN + u + 1)
                act.activation(Oh[b % 2][:, hh, :], Ob[:, 0:S], ACT.Identity,
                               bias=ocol[p][:, hh:hh + 1]).then_inc(o_hi, 1)

            v0, k0 = 2 * KC * GC, KC * GC
            act.wait_ge(v0_in, 16)
            act.activation(wh[0][:, v0:NQKV], pack_a[:, v0:NQKV], ACT.Copy).then_inc(w0_hi, 1)
            ctx_part(0)
            ctx_part(1)
            value_hi(0, 0, 0, 0)
            ctx_part(2)
            value_hi(0, 0, 1, 1)
            ctx_part(3)
            act.wait_ge(kq0_in, 16)
            act.activation(wh[0][:, k0:v0], pack_a[:, k0:v0], ACT.Copy).then_inc(w0_hi, 1)
            value_hi(0, 0, 2, 2)
            value_hi(0, 0, 3, 3)
            act.activation(wh[0][:, 0:k0], pack_a[:, 0:k0], ACT.Copy, scale=K ** -0.5).then_inc(w0_hi, 1)
            act.wait_ge(bias0_step, 3)

            def prologue(a, G):
                for t in KT:
                    project_hi(G, 0, t, (t + 1) % 2, prologue_use(G, t))
                act.wait_ge(attp_in, a * 16 + 16)
                for b in range(B):
                    act.wait_ge(xn_turned, a * B + b + 1 + TURN0)
                    act.wait_ge(h_lo, a * B + b - 1 + HLO0)
                    for kc in range(KC):
                        act.activation(prob[b % 2][:, kc, 0:S], slot_bank[(b + 1) % 2][:, kc, :],
                                       ACT.Identity, scale=attp[:, kc:kc + 1],
                                       bias=attp[:, KC + kc:KC + kc + 1]).then_inc(h_full, 1)
                    act.wait_ge(h_full, (a * B + b + 1) * 2 + FULL0)
                    act.activation(hTh[:, :, tok(b)], prob[b % 2][:, :, 0:S], ACT.Copy).then_inc(h_hi, 1)
                for t in QT:
                    if t == QT[-1]:
                        exps(G * UN, 0)
                    project_hi(G, 0, t, (t + 1) % 2, prologue_use(G, t))

            def unit(a, G, p, u, first=False, last=False):
                U = G * UN + u
                before = b_before(G, p, u, first, last)
                if before and before[0] not in VT:
                    project_hi(before[1], before[2], before[0], 1, before[3])
                if u == 0 and not first:
                    output_hi(G - 1, 1 - p, UN - 1, False)
                elif u > 0:
                    output_hi(G, p, u - 1, last)
                if u > 0:
                    item = slots(u - 1, first, last)[0]
                    if item and item[0] == "proj" and item[1] in VT:
                        value_hi(G + 1, 1 - p, item[1] - VT[0], use(G, u - 1, 0, first, last))
                if before and before[0] in VT:
                    value_hi(before[1], before[2], before[0] - VT[0], before[3])
                act.wait_ge(transposed, U + 1 + TR0)
                act.activation(PTh[u % 2][:, :, :], PTb[:, :, :], ACT.Copy).then_inc(pt_hi, 1)
                if not (last and u == UN - 1):
                    exps(U + 1, (u + 1) % 2)
                item = slots(u, first, last)[0]
                if item and item[0] == "proj" and item[1] not in VT:
                    project_hi(G + 1, 1 - p, item[1], 0, use(G, u, 0, first, last))

            att_loop(act, prologue, unit, lambda a, G: output_hi(G, 1, UN - 1, True))

        @block.vector
        def _(dve):
            dve.sem_inc(h_lo, HLO0)
            dve.sem_inc(pt_lo, PTLO0)
            dve.sem_inc(o_lo, OLO0)

            def ctx_part(b):
                dve.wait_ge(ctx_hi, b + 1)
                dve.tensor_tensor(cTl[:, :, tok(b)], ctx_at[b][:, :, 0:S],
                                  cTh[:, :, tok(b)].bitcast(F32), ALU.subtract).then_inc(ctx_split, 1)

            def project_lo(G, i, t, where):
                hh, half, which, lo = kq_tile(t, i, Kl, Ql)
                hi = kq_tile(t, i, Kh, Qh)[3]
                dve.wait_ge(proj_hi, G * 8 + t + 1)
                c = hh + which * HG
                dve.scalar_tensor_tensor(out=lo, in0=slot_bank[where][:, :, :], scalar=bcol[i][:, c:c + 1],
                                         in1=hi.bitcast(F32), op0=ALU.add,
                                         op1=ALU.subtract).then_inc(drained, 1)

            def value_sum(G, i, b, where, n):
                dve.wait_ge(slot_done, n + 1)
                dve.wait_ge(v_lo, G * B + b - 1 + VLO0)
                row = vrow[i][:, :].rearrange("p (o d) -> p o d", o=1).to_broadcast([P, 2, D])
                dve.tensor_tensor(work[b % 2][:, :, :], slot_bank[where][:, :, :], row,
                                  ALU.add).then_inc(drained, 1)

            def row_max(U, r):
                dve.wait_ge(scored, U + 1 + SCORE0)
                dve.tensor_reduce(nmax[:, r, :], Sb[r][:, :, 0:S + 1], AX.X, ALU.max,
                                  negate=True).then_inc(max_done, 1)

            def normalize(U, r):
                dve.wait_ge(exp_done, U * 2 + 2 + EXP0)
                dve.reciprocal(rsum[:, r, :], sums[:, r, :]).then_inc(rsum_done, 1)
                dve.wait_ge(rsum_done, U + 1)
                for c in range(2):
                    dve.tensor_scalar(prob[r][:, c, 0:S], prob[r][:, c, 0:S], rsum[:, r, c:c + 1],
                                      None, ALU.mult).then_inc(normed, 1)

            def moments(k, b, n=None):
                if n is not None:
                    dve.wait_ge(drained, n + 1)
                for c in range(2 * b, 2 * b + 2):
                    dve.bn_stats(stats[:, c, :], x[:, c, :]).then_inc(ln_step, 1)
                stand(dve, ln_step, k * 2 * CH + 4 * b + 2)
                for c in range(2 * b, 2 * b + 2):
                    dve.bn_aggr(mv[:, c, :], stats[:, c, :]).then_inc(ln_step, 1)

            def add_wo(a, b, n):
                dve.wait_ge(slot_done, n + 1)
                dve.wait_ge(bo_added, a + 1)
                dve.wait_ge(drained, n)
                dve.tensor_tensor(x[:, 2 * b:2 * b + 2, :], slot_bank[0][:, :, :],
                                  x[:, 2 * b:2 * b + 2, :], ALU.add).then_inc(drained, 1)

            def output_lo(G, p, u):
                b, hh = u // HG, u % HG
                dve.wait_ge(o_hi, G * UN + u + 1)
                dve.scalar_tensor_tensor(out=Ol[b % 2][:, hh, :], in0=Ob[:, 0:S],
                                         scalar=ocol[p][:, hh:hh + 1],
                                         in1=Oh[b % 2][:, hh, :].bitcast(F32), op0=ALU.add,
                                         op1=ALU.subtract).then_inc(o_lo, 1)

            v0, k0 = 2 * KC * GC, KC * GC
            dve.wait_ge(w0_hi, 1)
            dve.tensor_tensor(wl[0][:, v0:NQKV], pack_a[:, v0:NQKV], wh[0][:, v0:NQKV].bitcast(F32),
                              ALU.subtract).then_inc(w0_lo, 1)
            ctx_part(0)
            ctx_part(1)
            dve.wait_ge(bias0_step, 1)
            value_sum(0, 0, 0, 1, 0)
            ctx_part(2)
            value_sum(0, 0, 1, 0, 1)
            ctx_part(3)
            value_sum(0, 0, 2, 1, 2)
            dve.wait_ge(w0_hi, 2)
            dve.tensor_tensor(wl[0][:, k0:v0], pack_a[:, k0:v0], wh[0][:, k0:v0].bitcast(F32),
                              ALU.subtract).then_inc(w0_lo, 1)
            value_sum(0, 0, 3, 0, 3)
            dve.wait_ge(x_in, 16)
            for b in range(B):
                moments(0, b)
            dve.wait_ge(w0_hi, 3)
            dve.scalar_tensor_tensor(out=wl[0][:, 0:k0], in0=pack_a[:, 0:k0], scalar=K ** -0.5,
                                     in1=wh[0][:, 0:k0].bitcast(F32), op0=ALU.mult,
                                     op1=ALU.subtract).then_inc(w0_lo, 1)

            def prologue(a, G):
                for t in KT:
                    project_lo(G, 0, t, (t + 1) % 2)
                dve.wait_ge(rstd_ready, a + 1)

                def turned_lo(b):
                    dve.wait_ge(h_hi, a * B + b + 1)
                    dve.tensor_tensor(hTl[:, :, tok(b)], prob[b % 2][:, :, 0:S],
                                      hTh[:, :, tok(b)].bitcast(F32), ALU.subtract).then_inc(h_lo, 1)
                for b in range(B):
                    if b < 2:
                        dve.wait_ge(v_lo, G * B + 3 + b + VLO0)
                    dve.wait_ge(xn_turned, a * B + b - 1 + TURN0)
                    for c in range(2):
                        ins = dve.tensor_scalar(work[b % 2][:, c, :], x[:, 2 * b + c, :],
                                                mv[:, 2 * b + c, 0:1], rstd[:, 2 * b + c:2 * b + c + 1],
                                                ALU.subtract, ALU.mult)
                    ins.then_inc(xn_ready, 1)
                    if b >= 2:
                        turned_lo(b - 2)
                turned_lo(B - 2)
                turned_lo(B - 1)
                for t in QT:
                    if t == QT[-1]:
                        row_max(G * UN, 0)
                        normalize(G * UN, 0)
                    project_lo(G, 0, t, (t + 1) % 2)

            def unit(a, G, p, u, first=False, last=False):
                U = G * UN + u
                before = b_before(G, p, u, first, last)
                if before:
                    t, Gt, i, n = before
                    if t in VT:
                        value_sum(Gt, i, t - VT[0], 1, n)
                    else:
                        project_lo(Gt, i, t, 1)
                if not (last and u == UN - 1):
                    row_max(U + 1, (u + 1) % 2)
                if u == 0 and not first:
                    output_lo(G - 1, 1 - p, UN - 1)
                elif u > 0:
                    output_lo(G, p, u - 1)
                dve.wait_ge(pt_hi, U + 1)
                dve.tensor_tensor(PTl[u % 2][:, :, :], PTb[:, :, :],
                                  PTh[u % 2][:, :, :].bitcast(F32), ALU.subtract).then_inc(pt_lo, 1)
                if not (last and u == UN - 1):
                    normalize(U + 1, (u + 1) % 2)
                item = slots(u, first, last)[0]
                if item:
                    kind, t = item
                    n = use(G, u, 0, first, last)
                    if kind == "wo":
                        add_wo(a, t, n)
                    elif t in VT:
                        value_sum(G + 1, 1 - p, t - VT[0], 0, n)
                    else:
                        project_lo(G + 1, 1 - p, t, 0)
                if last and u in (4, 6):
                    moments(a + 1, u // 2 - 2, use(G, u - 1, 0, last=True))

            def epilogue(a, G):
                output_lo(G, 1, UN - 1)
                moments(a + 1, B - 2, use(G, UN - 1, 0, last=True))
                add_wo(a, B - 1, last_use(G))
                moments(a + 1, B - 1, last_use(G))

            att_loop(dve, prologue, unit, epilogue)

        @block.tensor
        def _(pe):
            pe.sem_inc(scored, SCORE0)
            pe.sem_inc(transposed, TR0)
            pe.sem_inc(xn_turned, TURN0)

            def three(out, w, m, first, final):
                (w_hi, w_lo), (m_hi, m_lo) = w, m
                pe.matmul(out, w_lo, m_hi, start=first, stop=False)
                pe.matmul(out, w_hi, m_lo, start=False, stop=False)
                return pe.matmul(out, w_hi, m_hi, start=False, stop=final)

            def project(i, t, where):
                tile = slot_bank[where]
                if t in VT:
                    for c in range(2):
                        for kc in range(KC):
                            ins = three(tile[:, c, :],
                                        [s[:, kc, tok(t - VT[0], c * P, P)] for s in (cTh, cTl)],
                                        [wcol(w[i], 2, kc) for w in (wh, wl)],
                                        kc == 0, kc == KC - 1)
                else:
                    hh, half, which, _ = kq_tile(t, i, Kh, Qh)
                    src = (hTh, hTl) if which == 0 else (cTh, cTl)
                    for kc in range(KC):
                        ins = three(tile[:, :, :].rearrange("p a b -> p (a b)"),
                                    [wcol(w[i], which, kc, hh) for w in (wh, wl)],
                                    [s[:, kc, half * 512:(half + 1) * 512] for s in src],
                                    kc == 0, kc == KC - 1)
                ins.then_inc(slot_done, 1)

            def scores(U, G, i, u, last_q=None):
                b, hh, r = u // HG, u % HG, u % 2
                if u == 0:
                    pe.wait_ge(drained, last_q + 1)
                    pe.wait_ge(kb_ready, G + 1)
                pe.wait_ge(exp_done, U * 2 - 2 + EXP0)
                for c in range(2):
                    ins = three(Sb[r][:, c, 0:TP],
                                [w[i][:, hh, tok(b, c * P, P)] for w in (Qh, Ql)],
                                [m[i][:, hh, b, :] for m in (Kh, Kl)], True, True)
                ins.then_inc(scored, 1)

            def wo_tile(Gw, i, b):
                pe.wait_ge(wo_ready, Gw + 1)
                pe.wait_ge(o_lo, Gw * UN + HG * b + HG + OLO0)
                for c in range(2):
                    for hh in range(HG):
                        ins = three(slot_bank[0][:, c, :],
                                    [o[b % 2][:, hh, c * P:(c + 1) * P] for o in (Oh, Ol)],
                                    [w[i][:, hh * D:(hh + 1) * D] for w in (woh, wol)],
                                    hh == 0, hh == HG - 1)
                ins.then_inc(slot_done, 1)

            pe.wait_ge(w0_lo, 1)
            for b in range(B):
                pe.wait_ge(ctx_split, b + 1)
                if b >= 2:
                    pe.wait_ge(drained, b - 1)
                project(0, VT[b], (b + 1) % 2)
            pe.wait_ge(w0_lo, 2)
            pe.wait_ge(ident_in, 16)

            def prologue(a, G):
                for t in KT:
                    pe.wait_ge(drained, prologue_use(G, t) - 1)
                    project(0, t, (t + 1) % 2)
                for b in range(B):
                    pe.wait_ge(xn_ready, a * B + b + 1)
                    if b < 2:
                        pe.wait_ge(drained, prologue_use(G, KT[2 + b]) + 1)
                    else:
                        pe.wait_ge(h_full, (a * B + b - 1) * 2 + FULL0)
                    for c in range(2):
                        for kc in range(KC):
                            ins = pe.transpose(slot_bank[(b + 1) % 2][:, kc, c * P:(c + 1) * P],
                                               work[b % 2][:, c, kc * P:(kc + 1) * P], ident[:, :])
                    ins.then_inc(xn_turned, 1)
                pe.wait_ge(w0_lo, 3)
                for t in QT:
                    half = kq_tile(t, 0, Kh, Qh)[1]
                    pe.wait_ge(h_lo, a * B + 2 * half + 2 + HLO0)
                    if half == 0:
                        pe.wait_ge(h_full, (a * B + 3 + t % 2) * 2 + FULL0)
                    else:
                        pe.wait_ge(drained, prologue_use(G, t) - 1)
                    if t == QT[-1]:
                        scores(G * UN, G, 0, 0, prologue_use(G, QT[0]))
                    project(0, t, (t + 1) % 2)

            def unit(a, G, p, u, first=False, last=False):
                U, b, hh = G * UN + u, u // HG, u % HG
                if first:
                    pe.wait_ge(drained, prologue_use(G, QT[1] if u == 0 else QT[-1]) + 1)
                if u < UN - 1:
                    scores(U + 1, G, p, u + 1)
                elif not last:
                    scores(U + 1, G + 1, 1 - p, 0, use(G, 4, 1))
                pe.wait_ge(normed, U * 2 + 2)
                pe.wait_ge(pt_lo, U + PTLO0)
                for c in range(2):
                    for tc in range(2):
                        ins = pe.transpose(PTb[:, tc, c * P:(c + 1) * P],
                                           prob[u % 2][:, c, tc * P:(tc + 1) * P], ident[:, :])
                ins.then_inc(transposed, 1)
                for where, item in enumerate(slots(u, first, last)):
                    if item is None:
                        continue
                    kind, t = item
                    n = use(G, u, where, first, last)
                    alone = first and u == where or last and u >= 3
                    pe.wait_ge(drained, n if alone else n - 1)
                    if kind == "proj":
                        if t == (VT if last else KT)[0]:
                            pe.wait_ge(qkv_ready, G + 1)
                        project(1 - p, t, where)
                    elif u == 1:
                        wo_tile(G - 1, 1 - p, t)
                    else:
                        wo_tile(G, p, t)
                if hh == 0:
                    pe.wait_ge(v_lo, G * B + b + 1 + VLO0)
                pe.wait_ge(pt_lo, U + 1 + PTLO0)
                pe.wait_ge(o_lo, U + OLO0)
                for tc in range(2):
                    ins = three(Ob[:, 0:S],
                                [v[p][:, 2 * b + tc, hh * K:(hh + 1) * K] for v in (Vh, Vl)],
                                [m[u % 2][:, tc, :] for m in (PTh, PTl)], tc == 0, tc == 1)
                ins.then_inc(pv_done, 1)

            def epilogue(a, G):
                pe.wait_ge(drained, last_use(G))
                wo_tile(G, 1, B - 1)

            att_loop(pe, prologue, unit, epilogue)


def feed_forward(nc, x, ident, mv, rstd, mlpp, w1_d, w2_d, l1w, wq_d, wk_d, wv_d, l1p_d):
    with ExitStack() as ctx:
        def sb(name, shape, dt=F32):
            return ctx.enter_context(nc.sbuf_tensor("m_" + name, shape, dt))

        def bank(name, shape):
            return ctx.enter_context(nc.psum_tensor("m_" + name, shape, F32))

        def sem(name):
            return ctx.enter_context(nc.semaphore("m_" + name))

        w1, w2 = sb("w1", [P, KC, F]), sb("w2", [P, FC, D])
        w1h, w1l = sb("w1h", [P, KC, F], F32R), sb("w1l", [P, KC, F], F32R)
        w2h, w2l = sb("w2h", [P, FC, D], F32R), sb("w2l", [P, FC, D], F32R)
        wqh, wql, wkh, wkl, wvh, wvl, l1p = l1w
        wk, wq = sb("wk", [P, KC, F]), sb("wq", [P, KC, D])
        wv = sb("wv", [P, KC, KVH * HD])
        hTh, hTl = sb("hTh", [P, KC, TOK], F32R), sb("hTl", [P, KC, TOK], F32R)
        Gh, Gl = sb("Gh", [P, FC, TOK], F32R), sb("Gl", [P, FC, TOK], F32R)
        xn = [sb(f"xn{i}", [P, 2, D]) for i in range(2)]
        full = [sb(f"full{i}", [P, KC, S]) for i in range(2)]
        act_out = [sb(f"act_out{i}", [P, 512]) for i in range(2)]
        turn = [bank(f"turn{i}", [P, KC, S]) for i in range(2)]
        hid = [bank(f"hid{i}", [P, 512]) for i in range(2)]
        res = [bank(f"res{i}", [P, 512]) for i in range(2)]

        w1_in, w2_in = sem("w1_in"), sem("w2_in")
        w1_hi, w1_lo, w2_hi, w2_lo = sem("w1_hi"), sem("w1_lo"), sem("w2_hi"), sem("w2_lo")
        wq_in, wk_in, wv_in, l1p_in = sem("wq_in"), sem("wk_in"), sem("wv_in"), sem("l1p_in")
        bq_scaled, wq_scaled, wq_hi, wq_lo = (
            sem(n) for n in ("bq_scaled", "wq_scaled", "wq_hi", "wq_lo"))
        wk_hi, wk_lo, wv_hi, wv_lo = (sem(n) for n in ("wk_hi", "wk_lo", "wv_hi", "wv_lo"))
        xn_ready, xn_turned, h_full = sem("xn_ready"), sem("xn_turned"), sem("h_full")
        h_hi, h_lo, b2_added = sem("h_hi"), sem("h_lo"), sem("b2_added")
        hid_done, gelu_done, g_hi, g_lo = sem("hid_done"), sem("gelu_done"), sem("g_hi"), sem("g_lo")
        res_done, res_added = sem("res_done"), sem("res_added")
        block = ctx.enter_context(nc.Block())
        NTILE = FC * 2

        @block.sync
        def _(sp):
            sp.dma_start(w1[:, :, :], w1_d).then_inc(w1_in, 16)
            sp.dma_start(w2[:, :, :], w2_d).then_inc(w2_in, 16)
            sp.dma_start(wk[:, :, :], wk_d).then_inc(wk_in, 16)
            sp.dma_start(wv[:, :, :], wv_d).then_inc(wv_in, 16)
            sp.dma_start(l1p[:, :], l1p_d).then_inc(l1p_in, 16)
            sp.dma_start(wq[:, :, :], wq_d).then_inc(wq_in, 16)

        @block.gpsimd
        def _(pool):
            def split(hi, lo, full, hi_done, lo_done):
                pool.tensor_copy(hi[:, :, :], full[:, :, :]).then_inc(hi_done, 1)
                pool.wait_ge(hi_done, 1)
                pool.tensor_tensor(lo[:, :, :], full[:, :, :], hi[:, :, :].bitcast(F32),
                                   ALU.subtract).then_inc(lo_done, 1)
            pool.wait_ge(w2_in, 16)
            split(w2h, w2l, w2, w2_hi, w2_lo)
            pool.wait_ge(xn_ready, B)
            b2 = mlpp[:, 2 * KC + FC:].rearrange("p (o d) -> p o d", o=1).to_broadcast([P, CH, D])
            pool.tensor_tensor(x[:, :, :], x[:, :, :], b2, ALU.add).then_inc(b2_added, 1)
            pool.wait_ge(wk_in, 16)
            split(wkh, wkl, wk, wk_hi, wk_lo)
            pool.wait_ge(wv_in, 16)
            split(wvh, wvl, wv, wv_hi, wv_lo)
            pool.wait_ge(l1p_in, 16)
            pool.tensor_scalar(l1p[:, 0:KB], l1p[:, 0:KB], HD ** -0.5, None, ALU.mult).then_inc(bq_scaled, 1)
            pool.wait_ge(wq_in, 16)
            pool.tensor_scalar(wq[:, :, :], wq[:, :, :], HD ** -0.5, None, ALU.mult).then_inc(wq_scaled, 1)
            pool.wait_ge(wq_scaled, 1)
            split(wqh, wql, wq, wq_hi, wq_lo)

        @block.scalar
        def _(act):
            for b in range(B):
                if b == 2:
                    act.wait_ge(w1_in, 16)
                    act.activation(w1h[:, :, :], w1[:, :, :], ACT.Copy).then_inc(w1_hi, 1)
                act.wait_ge(xn_turned, b + 1)
                if b >= 2:
                    act.wait_ge(h_lo, b - 1)
                for kc in range(KC):
                    act.activation(full[b % 2][:, kc, :], turn[b % 2][:, kc, :], ACT.Identity,
                                   scale=mlpp[:, kc:kc + 1],
                                   bias=mlpp[:, KC + kc:KC + kc + 1]).then_inc(h_full, 1)
                act.wait_ge(h_full, 2 * b + 2)
                act.activation(hTh[:, :, b * S:(b + 1) * S], full[b % 2][:, :, :],
                               ACT.Copy).then_inc(h_hi, 1)
            for n in range(2):
                for f in range(FC):
                    t = n * FC + f
                    act.wait_ge(hid_done, t + 1)
                    if t >= 2:
                        act.wait_ge(g_lo, t - 1)
                    act.activation(act_out[t % 2][:, :], hid[t % 2][:, :], ACT.Gelu,
                                   bias=mlpp[:, 2 * KC + f:2 * KC + f + 1]).then_inc(gelu_done, 1)
                    act.wait_ge(gelu_done, t + 1)
                    act.activation(Gh[:, f, n * 512:(n + 1) * 512], act_out[t % 2][:, :],
                                   ACT.Copy).then_inc(g_hi, 1)

        @block.vector
        def _(dve):
            def turned_lo(b):
                dve.wait_ge(h_hi, b + 1)
                dve.tensor_tensor(hTl[:, :, b * S:(b + 1) * S], full[b % 2][:, :, :],
                                  hTh[:, :, b * S:(b + 1) * S].bitcast(F32),
                                  ALU.subtract).then_inc(h_lo, 1)
            for b in range(B):
                if b >= 2:
                    dve.wait_ge(xn_turned, b - 1)
                for c in range(2 * b, 2 * b + 2):
                    ins = dve.tensor_scalar(xn[b % 2][:, c % 2, :], x[:, c, :], mv[:, c, 0:1],
                                            rstd[:, c:c + 1], ALU.subtract, ALU.mult)
                ins.then_inc(xn_ready, 1)
                if b == 3:
                    dve.wait_ge(w1_hi, 1)
                    dve.tensor_tensor(w1l[:, :, :], w1[:, :, :], w1h[:, :, :].bitcast(F32),
                                      ALU.subtract).then_inc(w1_lo, 1)
                if b >= 2:
                    turned_lo(b - 2)
            turned_lo(B - 2)
            turned_lo(B - 1)
            for n in range(2):
                for f in range(FC):
                    t = n * FC + f
                    dve.wait_ge(g_hi, t + 1)
                    dve.tensor_tensor(Gl[:, f, n * 512:(n + 1) * 512], act_out[t % 2][:, :],
                                      Gh[:, f, n * 512:(n + 1) * 512].bitcast(F32),
                                      ALU.subtract).then_inc(g_lo, 1)
                if n == 1:
                    dve.wait_ge(b2_added, 1)
            for c in range(CH):
                dve.wait_ge(res_done, c + 1)
                dve.tensor_tensor(x[:, c, :], res[c % 2][:, 0:D], x[:, c, :], ALU.add).then_inc(res_added, 1)

        @block.tensor
        def _(pe):
            def three(out, w, m, first, final):
                (w_hi, w_lo), (m_hi, m_lo) = w, m
                pe.matmul(out, w_lo, m_hi, start=first, stop=False)
                pe.matmul(out, w_hi, m_lo, start=False, stop=False)
                return pe.matmul(out, w_hi, m_hi, start=False, stop=final)

            for b in range(B):
                pe.wait_ge(xn_ready, b + 1)
                if b >= 2:
                    pe.wait_ge(h_full, 2 * (b - 1))
                for c in range(2):
                    for kc in range(KC):
                        ins = pe.transpose(turn[b % 2][:, kc, c * P:(c + 1) * P],
                                           xn[b % 2][:, c, kc * P:(kc + 1) * P], ident[:, :])
                ins.then_inc(xn_turned, 1)
            pe.wait_ge(w1_lo, 1)
            for n in range(2):
                pe.wait_ge(h_lo, 2 * n + 2)
                for f in range(FC):
                    t = n * FC + f
                    if t >= 2:
                        pe.wait_ge(gelu_done, t - 1)
                    for kc in range(KC):
                        ins = three(hid[t % 2][:, :], [w[:, kc, f * P:(f + 1) * P] for w in (w1h, w1l)],
                                    [m[:, kc, n * 512:(n + 1) * 512] for m in (hTh, hTl)],
                                    kc == 0, kc == KC - 1)
                    ins.then_inc(hid_done, 1)
            pe.wait_ge(w2_lo, 1)
            for c in range(CH):
                pe.wait_ge(g_lo, FC if c < CH // 2 else NTILE)
                if c >= 2:
                    pe.wait_ge(res_added, c - 1)
                for f in range(FC):
                    ins = three(res[c % 2][:, 0:D], [g[:, f, c * P:(c + 1) * P] for g in (Gh, Gl)],
                                [w[:, f, :] for w in (w2h, w2l)], f == 0, f == FC - 1)
                ins.then_inc(res_done, 1)


def load_queries(sp, b, kb, Qr, Qb, mask_d, maskb, q_in, mask_in):
    for k in range(GB):
        for i in range(REP):
            rows = Qr[32 * k:32 * k + 32, kb, 2 * i // REP, bass.ds(b * S, S)]
            sp.dma_start(Qb[kb][32 * i:32 * i + 32, k, :].bitcast(F32), rows.bitcast(F32)).then_inc(q_in, 16)
    sp.dma_start(maskb[kb][:, :, :], mask_d[bass.ds(b * S, S), :]
                 .rearrange("(c p) t -> p c t", p=P)).then_inc(mask_in, 16)


def grouped_projections(nc, x, ident, cTh, cTl, l1w, Qr, Qb, Kr, V, gmask, lastw, maskb, gmask_d, wo_d,
                        lastp_d, mask_d):
    with ExitStack() as ctx:
        def sb(name, shape, dt=F32):
            return ctx.enter_context(nc.sbuf_tensor("p_" + name, shape, dt))

        def bank(name, shape):
            return ctx.enter_context(nc.psum_tensor("p_" + name, shape, F32))

        def sem(name):
            return ctx.enter_context(nc.semaphore("p_" + name))

        VW = KVH * HD
        NTB = 4
        wqh, wql, wkh, wkl, wvh, wvl, l1p = l1w
        xTh, xTl = sb("xTh", [P, KC, TOK], F32R), sb("xTl", [P, KC, TOK], F32R)
        turn = [bank(f"turn{i}", [P, KC, S]) for i in range(2)]
        tile = [bank(f"tile{i}", [P, 512]) for i in range(NTB)]
        vbank = bank("vbank", [P, CH, VW])

        turned, x_hi, x_lo = sem("turned"), sem("x_hi"), sem("x_lo")
        tile_done, tile_hi, tile_lo = sem("tile_done"), sem("tile_hi"), sem("tile_lo")
        v_done, v_out = sem("v_done"), sem("v_out")
        gmask_in, wo_in, lastp_in, wo_hi, wo_lo, bo_added = (
            sem(n) for n in ("gmask_in", "wo_in", "lastp_in", "wo_hi", "wo_lo", "bo_added"))
        wo, woh, wol, lastp = lastw
        block = ctx.enter_context(nc.Block())
        TILES = [("k", g, n) for g in range(KVH) for n in range(2)]
        TILES[4:4] = [("q", kb, n) for kb in range(KB) for n in range(2)]
        TURNS = {0: (0, 1), 2: (2, 3)}

        @block.sync
        def _(sp):
            sp.dma_start(gmask[:, :], gmask_d).then_inc(gmask_in, 16)
            sp.dma_start(wo[:, :, :], wo_d).then_inc(wo_in, 16)
            sp.dma_start(lastp[:, :, :], lastp_d).then_inc(lastp_in, 16)
            q_in, mask_in = sem("q_in"), sem("mask_in")
            for kb in range(KB):
                sp.wait_ge(tile_lo, 6 + 2 * kb)
                load_queries(sp, 0, kb, Qr, Qb, mask_d, maskb, q_in, mask_in)
            sp.wait_ge(gmask_in, 16)
            sp.wait_ge(q_in, KB * GB * REP * 16)
            sp.wait_ge(mask_in, KB * 16)

        @block.gpsimd
        def _(pool):
            pool.wait_ge(wo_in, 16)
            pool.tensor_copy(woh[:, :, :], wo[:, :, :]).then_inc(wo_hi, 1)
            pool.wait_ge(wo_hi, 1)
            pool.tensor_tensor(wol[:, :, :], wo[:, :, :], woh[:, :, :].bitcast(F32),
                               ALU.subtract).then_inc(wo_lo, 1)
            pool.wait_ge(lastp_in, 16)
            pool.wait_ge(turned, B)
            bo = lastp[:, 0:1, :].to_broadcast([P, CH, D])
            pool.tensor_tensor(x[:, :, :], x[:, :, :], bo, ALU.add).then_inc(bo_added, 1)

        @block.scalar
        def _(act):
            for t, (kind, g, n) in enumerate(TILES):
                for b in TURNS.get(t, ()):
                    act.wait_ge(turned, b + 1)
                    act.activation(xTh[:, :, b * S:(b + 1) * S], turn[b % 2][:, :, :],
                                   ACT.Copy).then_inc(x_hi, 1)
                out, c = (Qr[:, g, 0], g) if kind == "q" else (Kr[:, g], KB + g)
                act.wait_ge(tile_done, t + 1)
                act.activation(out[:, n * 512:(n + 1) * 512], tile[t % NTB][:, :], ACT.Identity,
                               bias=l1p[:, c:c + 1]).then_inc(tile_hi, 1)

        @block.vector
        def _(dve):
            for t, (kind, g, n) in enumerate(TILES):
                for b in TURNS.get(t, ()):
                    dve.wait_ge(x_hi, b + 1)
                    dve.tensor_tensor(xTl[:, :, b * S:(b + 1) * S], turn[b % 2][:, :, :],
                                      xTh[:, :, b * S:(b + 1) * S].bitcast(F32),
                                      ALU.subtract).then_inc(x_lo, 1)
                dve.wait_ge(tile_hi, t + 1)
                cols = slice(n * 512, (n + 1) * 512)
                if kind == "q":
                    parts = [(0, P, g, Qr[:, g, 1, cols], Qr[:, g, 0, cols])]
                else:
                    parts = [(p0, p0 + 32, KB + g, Kr[p0:p0 + 32, g, cols], Kr[p0:p0 + 32, g, cols])
                             for p0 in (32, 96)]
                for p0, p1, c, lo, hi in parts:
                    ins = dve.scalar_tensor_tensor(out=lo, in0=tile[t % NTB][p0:p1, :],
                                                   scalar=l1p[p0:p1, c:c + 1], in1=hi.bitcast(F32),
                                                   op0=ALU.add, op1=ALU.subtract)
                ins.then_inc(tile_lo, 1)
            dve.wait_ge(v_done, 1)
            bv = l1p[:, KB + KVH:].rearrange("p (o d) -> p o d", o=1).to_broadcast([P, CH, VW])
            dve.tensor_tensor(V[:, :, :], vbank[:, :, :], bv, ALU.add).then_inc(v_out, 1)

        @block.tensor
        def _(pe):
            def three(out, w, m, first, final):
                (w_hi, w_lo), (m_hi, m_lo) = w, m
                pe.matmul(out, w_lo, m_hi, start=first, stop=False)
                pe.matmul(out, w_hi, m_lo, start=False, stop=False)
                return pe.matmul(out, w_hi, m_hi, start=False, stop=final)

            for t, (kind, g, n) in enumerate(TILES):
                for b in TURNS.get(t, ()):
                    if b >= 2:
                        pe.wait_ge(x_lo, b - 1)
                    for c in range(2):
                        for kc in range(KC):
                            ins = pe.transpose(turn[b % 2][:, kc, c * P:(c + 1) * P],
                                               x[:, 2 * b + c, kc * P:(kc + 1) * P], ident[:, :])
                    ins.then_inc(turned, 1)
                if kind == "q" and g == n == 0:
                    pe.wait_ge(x_lo, B)
                if t >= NTB:
                    pe.wait_ge(tile_lo, t - NTB + 1)
                w, m = ((wqh, wql), (xTh, xTl)) if kind == "q" else ((wkh, wkl), (cTh, cTl))
                for kc in range(KC):
                    ins = three(tile[t % NTB][:, :], [a[:, kc, g * P:(g + 1) * P] for a in w],
                                [a[:, kc, n * 512:(n + 1) * 512] for a in m], kc == 0, kc == KC - 1)
                ins.then_inc(tile_done, 1)
            for c in range(CH):
                for kc in range(KC):
                    ins = three(vbank[:, c, :], [a[:, kc, c * P:(c + 1) * P] for a in (cTh, cTl)],
                                [a[:, kc, :] for a in (wvh, wvl)], kc == 0, kc == KC - 1)
            ins.then_inc(v_done, 1)


SC0, MK0, PV0, PT0, OT0 = 3, 2, 2, 1, 1
IN0 = 1
ACT_BLOCKS = 2
NPR = 4
NV = KB * GB * 2


def grouped_attention(nc, ident, Qr, Qb, Kr, V, OT, sums, gmask, mask_d, maskb):
    with ExitStack() as ctx:
        def sb(name, shape, dt=F32):
            return ctx.enter_context(nc.sbuf_tensor("g_" + name, shape, dt))

        def bank(name, shape):
            return ctx.enter_context(nc.psum_tensor("g_" + name, shape, F32))

        def sem(name):
            return ctx.enter_context(nc.semaphore("g_" + name))

        KP = [sb(f"KP{i}", [P, GR, S], F32R) for i in range(2)]
        VP = [sb(f"VP{i}", [P, 2, GB, GR, GR * HD]) for i in range(KB)]
        PT = [sb(f"PT{i}", [P, GB, 2 * GR, S]) for i in range(KB)]
        prob = [sb(f"prob{i}", [P, GR, S]) for i in range(NPR)]
        nmax = sb("nmax", [P, NPR, GR])
        Sb = [bank(f"Sb{i}", [P, 2, 512]) for i in range(2)]
        PTb = [bank("PTb0", [P, GR, P]), bank("PTb1", [P, 2 * GR, P])]
        parts = [slice(0, ACT_BLOCKS), slice(ACT_BLOCKS, 2 * GR)]
        Ob = bank("Ob", [P, 512])

        q_in = [sem(f"q_in{i}") for i in range(KB)]
        mask_in = [sem(f"mask_in{i}") for i in range(KB)]
        kp_ready, vp_zero, vp_ready = sem("kp_ready"), sem("vp_zero"), sem("vp_ready")
        scored, masked, exp_done = sem("scored"), sem("masked"), sem("exp_done")
        turned = [sem(f"turned{i}") for i in range(2)]
        pt0_out, pt1_out, pv_done, ot_out = sem("pt0_out"), sem("pt1_out"), sem("pv_done"), sem("ot_out")
        stood = sem("stood")

        def stand(eng, semaphore, value):
            eng.wait_ge(semaphore, value)
            eng.sem_inc(stood, 1)

        def batches(eng, unit, last):
            for v in range(NV // 2):
                unit(0, v, first=True)
            with eng.Fori(0, B - 1) as b:
                for v in range(NV // 2, NV):
                    unit(b, v)
                for v in range(NV // 2):
                    unit(b + 1, v)
            for v in range(NV // 2, NV):
                unit(B - 1, v)
            last()

        def ahead(part, b, v, by):
            if v + by < NV:
                part(b, v + by, b * NV + v + by)
            elif not (isinstance(b, int) and b == B - 1):
                part(b + 1, v + by - NV, b * NV + v + by)

        block = ctx.enter_context(nc.Block())

        @block.sync
        def _(sp):
            for kb in range(KB):
                sp.sem_inc(q_in[kb], IN0)
                sp.sem_inc(mask_in[kb], IN0)
            with sp.Fori(0, B - 1) as b:
                for kb in range(KB):
                    stand(sp, masked, b * NV + (kb + 1) * 8 + MK0)
                    load_queries(sp, b + 1, kb, Qr, Qb, mask_d, maskb, q_in[kb], mask_in[kb])

        @block.gpsimd
        def _(pool):
            def keys(b, kb, k):
                J = b * KVH + kb * GB + k
                pool.wait_ge(scored, J * 2 - 2 + SC0)
                out = KP[k % 2][:, :, :]
                rows = Kr[:, kb * GB + k, bass.ds(b * S, S)].bitcast(F32)
                rows = rows.rearrange("p (o t) -> p o t", o=1).to_broadcast([P, GR, S])
                head = gmask[:, :].rearrange("p (g o) -> p g o", o=1).to_broadcast([P, GR, S])
                pool.tensor_tensor(out, rows, head, ALU.mult).then_inc(kp_ready, 1)

            def values(b, kb):
                su = b * KB + kb
                stand(pool, pv_done, su - 1 + PV0)
                for g in range(GR):
                    src = V[:, bass.ds(b * 2, 2), kb * GB * HD:(kb + 1) * GB * HD]
                    pool.tensor_copy(VP[kb][:, :, :, g, g * HD:(g + 1) * HD],
                                     src.rearrange("p c (k d) -> p c k d", d=HD)).then_inc(vp_ready, 1)

            def batch(b, done=0):
                for kb in range(KB):
                    for k in range(GB):
                        if kb * GB + k >= done:
                            keys(b, kb, k)
                    values(b, kb)
            keys(0, 0, 0)
            keys(0, 0, 1)
            for kb in range(KB):
                pool.memset(VP[kb][:, :, :, :, :], 0.0).then_inc(vp_zero, 1)
            pool.wait_ge(vp_zero, KB)
            batch(0, done=2)
            with pool.Fori(1, B) as b:
                batch(b)

        @block.scalar
        def _(act):
            act.sem_inc(pt0_out, PT0)

            def exps(b, v, N):
                kb, k, c = v // 8, v % 8 // 2, v % 2
                act.wait_ge(masked, N + 1 + MK0)
                for g in range(GR):
                    h = (kb * GB + k) * GR + g
                    ins = act.activation(prob[v % NPR][:, g, :], prob[v % NPR][:, g, :], ACT.Exp,
                                         scale=-1.0, bias=nmax[:, v % NPR, g:g + 1],
                                         accum_out=sums[:, bass.ds(b * 2 + c, 1), h])
                ins.then_inc(exp_done, 1)

            def unit(b, v, first=False):
                N, kb, k, c = b * NV + v, v // 8, v % 8 // 2, v % 2
                if first and v == 0:
                    exps(b, v, N)
                ahead(exps, b, v, 1)
                act.wait_ge(turned[0], N + 1)
                act.wait_ge(pv_done, b * KB + kb - 1 + PV0)
                act.activation(PT[kb][:, k, parts[0], c * P:(c + 1) * P], PTb[0][:, 0:ACT_BLOCKS, :],
                               ACT.Copy).then_inc(pt0_out, 1)
            batches(act, unit, lambda: None)

        @block.vector
        def _(dve):
            dve.sem_inc(masked, MK0)
            dve.sem_inc(pt1_out, PT0)
            dve.sem_inc(ot_out, OT0)

            def mask_and_max(b, v, N):
                kb, c = v // 8, v % 2
                if v % 8 == 0:
                    dve.wait_ge(mask_in[kb], b * 16 + IN0)
                stand(dve, scored, N + 1 + SC0)
                for g in range(GR):
                    ins = dve.tensor_tensor_reduce(
                        out=prob[v % NPR][:, g, :], in0=Sb[v % 2][:, g // 2, (g % 2) * S:(g % 2 + 1) * S],
                        in1=maskb[kb][:, c, :], scale=-1.0, scalar=BIG, op0=ALU.add, op1=ALU.min,
                        accum_out=nmax[:, v % NPR, g:g + 1])
                ins.then_inc(masked, 1)

            def out_block(su, kb, b):
                dve.wait_ge(pv_done, su + 1 + PV0)
                dve.tensor_copy(OT[:, kb, bass.ds(b * S, S)], Ob[:, 0:S]).then_inc(ot_out, 1)

            def unit(b, v, first=False):
                N, kb, k, c = b * NV + v, v // 8, v % 8 // 2, v % 2
                if first and v == 0:
                    mask_and_max(b, 0, N)
                    mask_and_max(b, 1, N + 1)
                ahead(mask_and_max, b, v, 2)
                dve.wait_ge(turned[1], N + 1)
                dve.wait_ge(pv_done, b * KB + kb - 1 + PV0)
                dve.tensor_copy(PT[kb][:, k, parts[1], c * P:(c + 1) * P],
                                PTb[1][:, 0:2 * GR - ACT_BLOCKS, :]).then_inc(pt1_out, 1)
                if v % 8 == 7 and not first:
                    out_block(b * KB + kb - 1, 1 - kb, b - 1 if kb == 0 else b)
            batches(dve, unit, lambda: out_block(B * KB - 1, 1, B - 1))

        @block.tensor
        def _(pe):
            pe.sem_inc(scored, SC0)
            pe.sem_inc(pv_done, PV0)

            def scores(b, v, N):
                kb, k, c = v // 8, v % 8 // 2, v % 2
                if v % 8 == 0:
                    pe.wait_ge(q_in[kb], b * GB * REP * 16 + IN0)
                if c == 0:
                    pe.wait_ge(kp_ready, b * KVH + kb * GB + k + 1)
                pe.wait_ge(masked, N - 1 + MK0)
                for half in range(2):
                    ins = pe.matmul(Sb[v % 2][:, half, :], Qb[kb][:, k, c * P:(c + 1) * P],
                                    KP[k % 2][:, 2 * half:2 * half + 2, :].rearrange("p g t -> p (g t)"),
                                    start=True, stop=True)
                ins.then_inc(scored, 1)

            def turn(v, N, part):
                pe.wait_ge((pt0_out, pt1_out)[part], N + PT0)
                for i in range(2 * GR)[parts[part]]:
                    tc, g = i // GR, i % GR
                    ins = pe.transpose(PTb[part][:, i - parts[part].start, :], prob[v % NPR][:, g, tc * P:(tc + 1) * P],
                                       ident[:, :])
                ins.then_inc(turned[part], 1)

            def sum_values(su, kb, steps):
                if steps[0] == 0:
                    pe.wait_ge(pt0_out, su * 8 + 8 + PT0)
                    pe.wait_ge(pt1_out, su * 8 + 8 + PT0)
                    pe.wait_ge(vp_ready, su * GR + GR)
                    pe.wait_ge(ot_out, su + OT0)
                for i in steps:
                    tc, g = i // GR, i % GR
                    for k in range(GB):
                        ins = pe.matmul(Ob[32 * k:32 * k + 32, 0:S], VP[kb][:, tc, k, g, :],
                                        PT[kb][:, k, i, :], start=(i == 0), stop=(i == 2 * GR - 1))
                if steps[-1] == 2 * GR - 1:
                    ins.then_inc(pv_done, 1)

            def unit(b, v, first=False):
                N, kb = b * NV + v, v // 8
                if first and v == 0:
                    scores(b, 0, N)
                    scores(b, 1, N + 1)
                ahead(scores, b, v, 2)
                pe.wait_ge(exp_done, N + 1)
                turn(v, N, 0)
                turn(v, N, 1)
                if v % 8 >= 1 and not first:
                    sum_values(b * KB + kb - 1, 1 - kb, [v % 8 - 1] if v % 8 < 7 else [6, 7])
            batches(pe, unit, lambda: sum_values(B * KB - 1, 1, list(range(2 * GR))))


def closing(nc, x, ident, OT, sums, lastw, out):
    with ExitStack() as ctx:
        def sb(name, shape, dt=F32):
            return ctx.enter_context(nc.sbuf_tensor("c_" + name, shape, dt))

        def bank(name, shape):
            return ctx.enter_context(nc.psum_tensor("c_" + name, shape, F32))

        def sem(name):
            return ctx.enter_context(nc.semaphore("c_" + name))

        _, woh, wol, lastp = lastw
        rsum = sb("rsum", [P, CH, KVH * GR])
        On = [sb(f"On{i}", [P, D]) for i in range(2)]
        Oh, Ol = sb("Oh", [P, KB, TOK], F32R), sb("Ol", [P, KB, TOK], F32R)
        stats, mv, rstd = sb("stats", [P, CH, 6]), sb("mv", [P, CH, 2]), sb("rstd", [P, CH])
        minus_half = sb("minus_half", [P, CH])
        y = sb("y", [P, CH, D])
        nat = [bank(f"nat{i}", [P, D]) for i in range(2)]
        back = [bank(f"back{i}", [P, KB, P]) for i in range(2)]
        res = [bank(f"res{i}", [P, 512]) for i in range(2)]

        rsum_done, natural, normed, turned = sem("rsum_done"), sem("natural"), sem("normed"), sem("turned")
        o_hi, o_lo, res_done, res_added = sem("o_hi"), sem("o_lo"), sem("res_done"), sem("res_added")
        stat_done, aggr_done = sem("stat_done"), sem("aggr_done")
        rstd_step, rstd_ready = sem("rstd_step"), sem("rstd_ready")
        centered, stored = sem("centered"), sem("stored")
        shifted = sem("shifted")
        block = ctx.enter_context(nc.Block())

        @block.sync
        def _(sp):
            for i in range(4):
                sp.wait_ge(shifted, 2 * i + 2)
                sp.dma_start(out.rearrange("(c p) d -> p c d", p=P)[:, 2 * i:2 * i + 2, :],
                             y[:, 2 * i:2 * i + 2, :]).then_inc(stored, 16)
            sp.wait_ge(stored, 64)

        @block.gpsimd
        def _(pool):
            pool.memset(minus_half[:, :], -0.5).then_inc(rstd_step, 1)
            for half in range(2):
                cs = slice(half * 4, half * 4 + 4)
                pool.wait_ge(aggr_done, half * 4 + 4)
                pool.tensor_scalar(rstd[:, cs], mv[:, cs, 1], L1_EPS, None, ALU.add).then_inc(rstd_step, 1)
                pool.wait_ge(rstd_step, half + 2)
                pool.tensor_tensor(rstd[:, cs], rstd[:, cs], minus_half[:, cs],
                                   ALU.pow).then_inc(rstd_ready, 1)

        @block.scalar
        def _(act):
            for c in range(CH):
                act.wait_ge(turned, c + 1)
                act.activation(Oh[:, :, c * P:(c + 1) * P], back[c % 2][:, :, :],
                               ACT.Copy).then_inc(o_hi, 1)

        @block.vector
        def _(dve):
            def normalize(c):
                dve.reciprocal(rsum[:, c, :], sums[:, c, :]).then_inc(rsum_done, 1)
                dve.wait_ge(rsum_done, c + 1)
                dve.wait_ge(natural, c + 1)
                if c >= 2:
                    dve.wait_ge(turned, c - 1)
                r = rsum[:, c, :].rearrange("p (h o) -> p h o", o=1).to_broadcast([P, KVH * GR, HD])
                dve.tensor_tensor(On[c % 2][:, :].rearrange("p (h d) -> p h d", d=HD),
                                  nat[c % 2][:, :].rearrange("p (h d) -> p h d", d=HD), r,
                                  ALU.mult).then_inc(normed, 1)

            def add(c):
                dve.wait_ge(res_done, c + 1)
                dve.tensor_tensor(x[:, c, :], res[c % 2][:, 0:D], x[:, c, :], ALU.add).then_inc(res_added, 1)
                dve.wait_ge(res_added, c + 1)
                dve.bn_stats(stats[:, c, :], x[:, c, :]).then_inc(stat_done, 1)
                dve.wait_ge(stat_done, c + 1)
                dve.bn_aggr(mv[:, c, :], stats[:, c, :]).then_inc(aggr_done, 1)
                dve.wait_ge(aggr_done, c + 1)
                dve.scalar_tensor_tensor(out=y[:, c, :], in0=x[:, c, :], scalar=mv[:, c, 0:1],
                                         in1=lastp[:, 1, :], op0=ALU.subtract,
                                         op1=ALU.mult).then_inc(centered, 1)

            def finish(c):
                dve.wait_ge(centered, c + 1)
                dve.wait_ge(rstd_ready, c // 4 + 1)
                dve.scalar_tensor_tensor(out=y[:, c, :], in0=y[:, c, :], scalar=rstd[:, c:c + 1],
                                         in1=lastp[:, 2, :], op0=ALU.mult, op1=ALU.add).then_inc(shifted, 1)

            normalize(0)
            for c in range(CH):
                if c + 1 < CH:
                    normalize(c + 1)
                dve.wait_ge(o_hi, c + 1)
                dve.tensor_tensor(Ol[:, :, c * P:(c + 1) * P], back[c % 2][:, :, :],
                                  Oh[:, :, c * P:(c + 1) * P].bitcast(F32), ALU.subtract).then_inc(o_lo, 1)
                if c >= 1:
                    add(c - 1)
            add(CH - 1)
            for c in range(CH // 2):
                finish(c)
            for c in range(CH // 2, CH):
                finish(c)

        @block.tensor
        def _(pe):
            def natural_chunk(c):
                if c >= 2:
                    pe.wait_ge(normed, c - 1)
                for kb in range(KB):
                    ins = pe.transpose(nat[c % 2][:, kb * P:(kb + 1) * P], OT[:, kb, c * P:(c + 1) * P],
                                       ident[:, :])
                ins.then_inc(natural, 1)

            def out_chunk(c):
                pe.wait_ge(o_lo, c + 1)
                if c >= 2:
                    pe.wait_ge(res_added, c - 1)
                n = 0
                for kb in range(KB):
                    for a, w in ((Ol, woh), (Oh, wol), (Oh, woh)):
                        n += 1
                        ins = pe.matmul(res[c % 2][:, 0:D], a[:, kb, c * P:(c + 1) * P], w[:, kb, :],
                                        start=(n == 1), stop=(n == 6))
                ins.then_inc(res_done, 1)

            natural_chunk(0)
            for c in range(CH):
                if c + 1 < CH:
                    natural_chunk(c + 1)
                pe.wait_ge(normed, c + 1)
                if c >= 2:
                    pe.wait_ge(o_lo, c - 1)
                for kb in range(KB):
                    ins = pe.transpose(back[c % 2][:, kb, :], On[c % 2][:, kb * P:(kb + 1) * P], ident[:, :])
                ins.then_inc(turned, 1)
                if c >= 1:
                    out_chunk(c - 1)
            out_chunk(CH - 1)


def build(nc, x_d, ident_d, ctx_t, packs_a, packs_b, params, w1_d, w2_d, mlpp_d, wq_d, wk_d, wv_d,
          l1p_d, mask_d, gmask_d, wo_d, lastp_d, out):
    with ExitStack() as ctx:
        def sb(name, shape, dt=F32):
            return ctx.enter_context(nc.sbuf_tensor(name, shape, dt))

        x = sb("x", [P, CH, D])
        ident = sb("ident", [P, P])
        mv, rstd = sb("mv", [P, CH, 2]), sb("rstd", [P, CH])
        mlpp = sb("mlpp", [P, 2 * KC + FC + D])
        with ExitStack() as inner:
            with ExitStack() as far:
                def far_sb(name, shape, dt=F32R):
                    return far.enter_context(nc.sbuf_tensor(name, shape, dt, side="right"))

                cTh, cTl = far_sb("cTh", [P, KC, TOK]), far_sb("cTl", [P, KC, TOK])
                cross_attentions(nc, x, ident, cTh, cTl, mv, rstd, mlpp, x_d, ident_d, ctx_t, packs_a,
                                 packs_b, params, mlpp_d)
                l1w = [far_sb(f"{name}{part}", [P, KC, n])
                       for name, n in (("wq", D), ("wk", F), ("wv", KVH * HD)) for part in "hl"]
                l1w.append(far_sb("l1p", [P, KB + KVH + KVH * HD], F32))
                feed_forward(nc, x, ident, mv, rstd, mlpp, w1_d, w2_d, l1w, wq_d, wk_d, wv_d, l1p_d)
                gmask = sb("gmask", [P, GR])
                lastw = [sb("wo", [P, KB, D]), sb("woh", [P, KB, D], F32R), sb("wol", [P, KB, D], F32R),
                         sb("lastp", [P, 3, D])]
                OT, sums = sb("OT", [P, KB, TOK]), sb("row_sums", [P, CH, KVH * GR])
                Qr = inner.enter_context(nc.sbuf_tensor("Qr", [P, KB, 2, TOK], F32R))
                Kr = inner.enter_context(nc.sbuf_tensor("Kr", [P, KVH, TOK], F32R))
                V = inner.enter_context(nc.sbuf_tensor("V", [P, CH, KVH * HD], F32))
                Qb = [inner.enter_context(nc.sbuf_tensor(f"Qb{i}", [P, GB, S], F32R)) for i in range(KB)]
                maskb = [inner.enter_context(nc.sbuf_tensor(f"maskb{i}", [P, 2, S], F32)) for i in range(KB)]
                grouped_projections(nc, x, ident, cTh, cTl, l1w, Qr, Qb, Kr, V, gmask, lastw, maskb,
                                    gmask_d, wo_d, lastp_d, mask_d)
            grouped_attention(nc, ident, Qr, Qb, Kr, V, OT, sums, gmask, mask_d, maskb)
        closing(nc, x, ident, OT, sums, lastw, out)


def kernel(**inputs):
    import numpy as np
    import concourse.bacc as bacc
    from concourse.bass_utils import run_bass_kernel_spmd as run

    def f(name):
        return np.ascontiguousarray(inputs[name])

    def feature_major(w):
        return w.reshape(KC, P, -1).transpose(1, 0, 2)

    def rows(v):
        return np.broadcast_to(v.reshape(1, -1), (P, v.size))

    def keys(w):
        w = w.reshape(-1, KVH, 1, HD)
        return np.broadcast_to(w, (w.shape[0], KVH, REP * GR, HD)).reshape(w.shape[0], -1)

    packs_a, packs_b, params = [], [], []
    for i in (1, 2):
        L = "L0_xattn_"
        for g in range(NG):
            cols, heads = slice(g * GC, (g + 1) * GC), slice(g * HG, (g + 1) * HG)
            parts = [feature_major(f(f"{L}w{n}{i}")[:, cols]).reshape(P, -1) for n in "qkv"]
            parts += [f(f"{L}b{n}{i}").reshape(H, K)[heads].T for n in "qk"]
            parts += [f(f"{L}bias_k{i}").reshape(H, K)[heads].T]
            parts += [rows(f(f"{L}bv{i}")[cols]), rows(f(f"{L}bias_v{i}").reshape(-1)[cols])]
            packs_a.append(np.concatenate(parts, 1))
            wo = f(f"{L}wo{i}").reshape(H, K, D)[heads].transpose(1, 0, 2).reshape(P, -1)
            packs_b.append(np.concatenate([wo, f(f"{L}bias_v{i}").reshape(H, K)[heads].T], 1))
        params.append(np.concatenate([f(f"{L}ln{i}_scale").reshape(KC, P).T,
                                      f(f"{L}ln{i}_offset").reshape(KC, P).T,
                                      rows(f(f"{L}bo{i}"))], 1))
    arrays = {
        "x": f("x").reshape(TOK, D),
        "ident": np.eye(P, dtype=np.float32),
        "ctx_t": np.ascontiguousarray(f("ctx_2048").reshape(TOK, D).T),
        "packs_a": np.stack(packs_a + packs_a[:2]),
        "packs_b": np.stack(packs_b + packs_b[:1]),
        "params": np.stack(params + params[:1]),
        "w1": feature_major(f("L0_xattn_w_fc1")),
        "w2": f("L0_xattn_w_fc2").reshape(FC, P, D).transpose(1, 0, 2),
        "mlpp": np.concatenate([f("L0_xattn_ln_mlp_scale").reshape(KC, P).T,
                                f("L0_xattn_ln_mlp_offset").reshape(KC, P).T,
                                f("L0_xattn_b_fc1").reshape(FC, P).T, rows(f("L0_xattn_b_fc2"))], 1),
        "wq": feature_major(f("L1_xattn_Wq")),
        "wk": feature_major(keys(f("L1_xattn_Wk"))),
        "wv": feature_major(f("L1_xattn_Wv")),
        "l1p": np.concatenate([f("L1_xattn_bq").reshape(KB, P).T,
                               keys(f("L1_xattn_bk")).reshape(KVH, P).T, rows(f("L1_xattn_bv"))], 1),
        "mask": f("mask_Bx1xSxS2_ff0").reshape(TOK, S),
        "gmask": (np.arange(P)[:, None] // HD % GR == np.arange(GR)).astype(np.float32),
        "wo": f("L1_xattn_Wo").reshape(KB, P, D).transpose(1, 0, 2),
        "lastp": np.stack([rows(f(f"L1_xattn_{n}")) for n in ("bo", "gamma", "beta")], 1),
    }
    arrays = {n: np.ascontiguousarray(a) for n, a in arrays.items()}
    nc = bacc.Bacc("TRN2", target_bir_lowering=False, num_devices=1)
    args = [nc.dram_tensor(n + "_dram", a.shape, F32, kind="ExternalInput").ap() for n, a in arrays.items()]
    out = nc.dram_tensor("out_dram", (TOK, D), F32, kind="ExternalOutput").ap()
    build(nc, *args, out)
    r = run(nc, [{n + "_dram": a for n, a in arrays.items()}], core_ids=[0])
    return r.results[0]["out_dram"].reshape(B, S, D)
```
